# Optimizing a Trainium2 kernel written in Bass

```python
import numpy as np
import jax
import jax.numpy as jnp

def _softmax(x, axis=-1):
    return jax.nn.softmax(x, axis=axis)

def _gelu(x):
    return jax.nn.gelu(x, approximate=True)

def _silu(x):
    return jax.nn.silu(x)

def _sigmoid(x):
    return jax.nn.sigmoid(x)

def _layernorm(x, axis=-1, eps=1e-05):
    m = jnp.mean(x, axis=axis, keepdims=True)
    v = jnp.var(x, axis=axis, keepdims=True)
    return (x - m) / jnp.sqrt(v + eps)

def _scatter_add(tgt, idx, src, axis=0):
    return tgt.at[idx].add(src)

def _segment_sum(src, seg, n):
    return jax.ops.segment_sum(src, seg, n)
kernel_name = 'mk_adaln_ffn_d2_seqx_r8_a518df'

def setup_inputs(seed: int=0):
    np.random.seed(seed)
    _w = jnp.asarray

    def _rec_inputs():
        import jax
        import jax.numpy as jnp
        _rk = jax.random.key(seed)
        x = -0.0002071 + 1 * jax.random.normal(jax.random.fold_in(_rk, 1), (8, 256, 128), jnp.float32)
        _lenS = 256 - jax.random.randint(jax.random.fold_in(_rk, 7), (8,), 0, max(1, 256 // 4) + 1, jnp.int32)
        _lenS2 = 256 - jax.random.randint(jax.random.fold_in(_rk, 8), (8,), 0, max(1, 256 // 4) + 1, jnp.int32)
        cond_8 = jax.random.uniform(jax.random.fold_in(_rk, 11), (8, 8), jnp.float32, 0.0, 0.983423)
        return (x, cond_8)
    x, cond_8 = _rec_inputs()

    def _L0_cond_setup():
        import jax, jax.numpy as jnp
        import numpy as np
        R = 16
        ALPHA = 32.0
        SCALING = ALPHA / R
        key = jax.random.key(seed)
        ks = jax.random.split(key, 6)
        B, T, C, O, E = (16, 1500, 128, 128, 8)
        x = jax.random.normal(ks[0], (B, T, C), dtype=jnp.float32)
        w = jax.random.uniform(ks[1], (B, E), dtype=jnp.float32)
        W_base = jax.random.normal(ks[2], (O, C), dtype=jnp.float32) * 0.02
        b_base = jax.random.normal(ks[3], (O,), dtype=jnp.float32) * 0.02
        As = jax.random.normal(ks[4], (E, R, C), dtype=jnp.float32) * 0.02
        Bs = jax.random.normal(ks[5], (E, O, R), dtype=jnp.float32) * 0.02
        return {'x': x, 'w': w, 'W_base': W_base, 'b_base': b_base, 'As': As, 'Bs': Bs}
    _L0_cond_all = _L0_cond_setup()
    _L0_cond_in = {k: v for k, v in _L0_cond_all.items() if k in ('W_base', 'b_base', 'As', 'Bs')}
    del _L0_cond_all

    def _L0_ffn_setup():
        import jax, jax.numpy as jnp
        import numpy as np
        E = 8
        K = 2
        key = jax.random.key(seed)
        ks = jax.random.split(key, 6)
        B, S, D, F = (4, 256, 128, 512)
        s_d = 1.0 / np.sqrt(D).astype(np.float32)
        s_f = 1.0 / np.sqrt(F).astype(np.float32)
        return {'x': jax.random.normal(ks[0], (B, S, D), jnp.float32), 'ln_w': jnp.ones((D,), jnp.float32), 'Wg': jax.random.normal(ks[1], (D, E), jnp.float32) * s_d, 'bg': jnp.zeros((E,), jnp.float32), 'W1a': jax.random.normal(ks[2], (E, D, F), jnp.float32) * s_d, 'b1a': jnp.zeros((E, F), jnp.float32), 'W1b': jax.random.normal(ks[3], (E, D, F), jnp.float32) * s_d, 'b1b': jnp.zeros((E, F), jnp.float32), 'W2': jax.random.normal(ks[4], (E, F, D), jnp.float32) * s_f, 'b2': jnp.zeros((E, D), jnp.float32)}
    _L0_ffn_all = _L0_ffn_setup()
    _L0_ffn_in = {k: v for k, v in _L0_ffn_all.items() if k in ('ln_w', 'Wg', 'bg', 'W1a', 'b1a', 'W1b', 'b1b', 'W2', 'b2')}
    del _L0_ffn_all

    def _L1_cond_setup():
        import jax, jax.numpy as jnp
        import numpy as np
        key = jax.random.key(seed)
        k1, k2, k3, k4, k5 = jax.random.split(key, 5)
        B, N, T, O, G = (32, 32, 128, 128, 8)
        x = jax.random.normal(k1, (B, N, T), dtype=jnp.float32)
        y = jax.random.uniform(k2, (B, G), dtype=jnp.float32)
        weight = jax.random.normal(k3, (G, O, T), dtype=jnp.float32) * (1.0 / np.sqrt(T))
        mask = jax.random.uniform(k4, (O, T), dtype=jnp.float32)
        bias = jax.random.normal(k5, (O,), dtype=jnp.float32)
        return {'x': x, 'y': y, 'weight': weight, 'mask': mask, 'bias': bias}
    _L1_cond_all = _L1_cond_setup()
    _L1_cond_in = {k: v for k, v in _L1_cond_all.items() if k in ('weight', 'mask', 'bias')}
    del _L1_cond_all

    def _L1_ffn_setup():
        import jax, jax.numpy as jnp
        import numpy as np
        B, S, D, H, L, E, K = (4, 128, 128, 16, 2, 8, 2)
        DFF = 4 * D

        def _ln(x, w, b):
            m = x.mean(-1, keepdims=True)
            v = x.var(-1, keepdims=True)
            return (x - m) / jnp.sqrt(v + 1e-05) * w + b

        def _attn(x, wq, wk, wv, wo, bq, bk, bv, bo):
            Bb, T, C = x.shape
            hd = C // H
            q = (x @ wq + bq).reshape(Bb, T, H, hd).transpose(0, 2, 1, 3)
            k = (x @ wk + bk).reshape(Bb, T, H, hd).transpose(0, 2, 1, 3)
            v = (x @ wv + bv).reshape(Bb, T, H, hd).transpose(0, 2, 1, 3)
            att = jnp.einsum('bhqd,bhkd->bhqk', q, k) * hd ** (-0.5)
            causal = jnp.tril(jnp.ones((T, T), bool))
            att = jnp.where(causal, att, -jnp.inf)
            att = jax.nn.softmax(att, axis=-1)
            y = jnp.einsum('bhqk,bhkd->bhqd', att, v).transpose(0, 2, 1, 3).reshape(Bb, T, C)
            return y @ wo + bo

        def _ffn(h, w1, b1, w2, b2):
            return jax.nn.gelu(h @ w1 + b1, approximate=False) @ w2 + b2

        def _combine_weights(logits):
            vals, idx = jax.lax.top_k(logits, K)
            w = jax.nn.softmax(vals, axis=-1)
            onehot = (idx[..., None] == jnp.arange(E)).astype(w.dtype)
            return jnp.sum(w[..., None] * onehot, axis=-2)

        def _token_moe(h, gw, gb, w1, b1, w2, b2):
            cw = _combine_weights(h @ gw + gb)
            out = jnp.zeros_like(h)
            for e in range(E):
                out = out + _ffn(h, w1[e], b1[e], w2[e], b2[e]) * cw[..., e:e + 1]
            return out

        def _seq_moe(h, gw, gb, w1, b1, w2, b2):
            cw = _combine_weights(h.mean(axis=1) @ gw + gb)
            out = jnp.zeros_like(h)
            for e in range(E):
                out = out + _ffn(h, w1[e], b1[e], w2[e], b2[e]) * cw[:, e, None, None]
            return out
        key = jax.random.key(seed)
        ks = jax.random.split(key, 9)
        n = lambda k, shp: jax.random.normal(k, shp, dtype=jnp.float32) * 0.02
        return {'x': jax.random.normal(ks[0], (B, S, D), dtype=jnp.float32), 'ln1_w': jnp.ones((L, D), jnp.float32), 'ln1_b': jnp.zeros((L, D), jnp.float32), 'ln2_w': jnp.ones((L, D), jnp.float32), 'ln2_b': jnp.zeros((L, D), jnp.float32), 'wq': n(ks[1], (L, D, D)), 'wk': n(ks[2], (L, D, D)), 'wv': n(ks[3], (L, D, D)), 'wo': n(ks[4], (L, D, D)), 'bq': jnp.zeros((L, D), jnp.float32), 'bk': jnp.zeros((L, D), jnp.float32), 'bv': jnp.zeros((L, D), jnp.float32), 'bo': jnp.zeros((L, D), jnp.float32), 'gate_w': n(ks[5], (L, D, E)), 'gate_b': jnp.zeros((L, E), jnp.float32), 'e_w1': n(ks[6], (L, E, D, DFF)), 'e_b1': jnp.zeros((L, E, DFF), jnp.float32), 'e_w2': n(ks[7], (L, E, DFF, D)), 'e_b2': jnp.zeros((L, E, D), jnp.float32)}
    _L1_ffn_all = _L1_ffn_setup()
    _L1_ffn_in = {k: v for k, v in _L1_ffn_all.items() if k in ('ln1_w', 'ln1_b', 'ln2_w', 'ln2_b', 'wq', 'wk', 'wv', 'wo', 'bq', 'bk', 'bv', 'bo', 'gate_w', 'gate_b', 'e_w1', 'e_b1', 'e_w2', 'e_b2')}
    del _L1_ffn_all
    return {'x': x, 'cond_8': cond_8, 'L0_cond_W_base': _L0_cond_in['W_base'], 'L0_cond_b_base': _L0_cond_in['b_base'], 'L0_cond_As': _L0_cond_in['As'], 'L0_cond_Bs': _L0_cond_in['Bs'], 'L0_ffn_ln_w': _L0_ffn_in['ln_w'], 'L0_ffn_Wg': _L0_ffn_in['Wg'], 'L0_ffn_bg': _L0_ffn_in['bg'], 'L0_ffn_W1a': _L0_ffn_in['W1a'], 'L0_ffn_b1a': _L0_ffn_in['b1a'], 'L0_ffn_W1b': _L0_ffn_in['W1b'], 'L0_ffn_b1b': _L0_ffn_in['b1b'], 'L0_ffn_W2': _L0_ffn_in['W2'], 'L0_ffn_b2': _L0_ffn_in['b2'], 'L1_cond_weight': _L1_cond_in['weight'], 'L1_cond_mask': _L1_cond_in['mask'], 'L1_cond_bias': _L1_cond_in['bias'], 'L1_ffn_ln1_w': _L1_ffn_in['ln1_w'], 'L1_ffn_ln1_b': _L1_ffn_in['ln1_b'], 'L1_ffn_ln2_w': _L1_ffn_in['ln2_w'], 'L1_ffn_ln2_b': _L1_ffn_in['ln2_b'], 'L1_ffn_wq': _L1_ffn_in['wq'], 'L1_ffn_wk': _L1_ffn_in['wk'], 'L1_ffn_wv': _L1_ffn_in['wv'], 'L1_ffn_wo': _L1_ffn_in['wo'], 'L1_ffn_bq': _L1_ffn_in['bq'], 'L1_ffn_bk': _L1_ffn_in['bk'], 'L1_ffn_bv': _L1_ffn_in['bv'], 'L1_ffn_bo': _L1_ffn_in['bo'], 'L1_ffn_gate_w': _L1_ffn_in['gate_w'], 'L1_ffn_gate_b': _L1_ffn_in['gate_b'], 'L1_ffn_e_w1': _L1_ffn_in['e_w1'], 'L1_ffn_e_b1': _L1_ffn_in['e_b1'], 'L1_ffn_e_w2': _L1_ffn_in['e_w2'], 'L1_ffn_e_b2': _L1_ffn_in['e_b2']}

def reference(x, cond_8, L0_cond_W_base, L0_cond_b_base, L0_cond_As, L0_cond_Bs, L0_ffn_ln_w, L0_ffn_Wg, L0_ffn_bg, L0_ffn_W1a, L0_ffn_b1a, L0_ffn_W1b, L0_ffn_b1b, L0_ffn_W2, L0_ffn_b2, L1_cond_weight, L1_cond_mask, L1_cond_bias, L1_ffn_ln1_w, L1_ffn_ln1_b, L1_ffn_ln2_w, L1_ffn_ln2_b, L1_ffn_wq, L1_ffn_wk, L1_ffn_wv, L1_ffn_wo, L1_ffn_bq, L1_ffn_bk, L1_ffn_bv, L1_ffn_bo, L1_ffn_gate_w, L1_ffn_gate_b, L1_ffn_e_w1, L1_ffn_e_b1, L1_ffn_e_w2, L1_ffn_e_b2):
    import jax
    import jax.numpy as jnp

    def _L0_cond_ref(x, w, W_base, b_base, As, Bs):
        import jax, jax.numpy as jnp
        import numpy as np
        R = 16
        ALPHA = 32.0
        SCALING = ALPHA / R
        out = jnp.einsum('btc,oc->bto', x, W_base) + b_base
        h = jnp.einsum('btc,erc->bter', x, As)
        lora = jnp.einsum('bter,eor,be->bto', h, Bs, w)
        return out + lora * SCALING

    def _L0_ffn_ref(x, ln_w, Wg, bg, W1a, b1a, W1b, b1b, W2, b2):
        import jax, jax.numpy as jnp
        import numpy as np
        E = 8
        K = 2
        B, S, D = x.shape
        eps = jnp.finfo(x.dtype).eps
        xn = x * jax.lax.rsqrt(jnp.mean(x * x, axis=-1, keepdims=True) + eps) * ln_w
        logits = xn @ Wg + bg
        vals, idx = jax.lax.top_k(logits, K)
        topk_w = jax.nn.softmax(vals, axis=-1)
        we = jnp.sum(jax.nn.one_hot(idx, E, dtype=x.dtype) * topk_w[..., None], axis=-2)
        T = B * S
        xf = xn.reshape(T, D)
        wef = we.reshape(T, E).T

        def step(acc, params):
            W1a_e, b1a_e, W1b_e, b1b_e, W2_e, b2_e, w_e = params
            a = xf @ W1a_e + b1a_e
            b = xf @ W1b_e + b1b_e
            y = jax.nn.silu(a) * b @ W2_e + b2_e
            return (acc + w_e[:, None] * y, None)
        out0 = jnp.zeros_like(xf)
        out, _ = jax.lax.scan(step, out0, (W1a, b1a, W1b, b1b, W2, b2, wef))
        return out.reshape(B, S, D)

    def _L1_cond_ref(x, y, weight, mask, bias):
        import jax, jax.numpy as jnp
        import numpy as np
        masked_w = weight * mask[None, :, :]
        w_bot = jnp.einsum('bg,got->bot', y, masked_w)
        return jnp.einsum('bnt,bot->bno', x, w_bot) + bias

    def _L1_ffn_ref(x, ln1_w, ln1_b, ln2_w, ln2_b, wq, wk, wv, wo, bq, bk, bv, bo, gate_w, gate_b, e_w1, e_b1, e_w2, e_b2):
        import jax, jax.numpy as jnp
        import numpy as np
        B, S, D, H, L, E, K = (4, 128, 128, 16, 2, 8, 2)
        DFF = 4 * D

        def _ln(x, w, b):
            m = x.mean(-1, keepdims=True)
            v = x.var(-1, keepdims=True)
            return (x - m) / jnp.sqrt(v + 1e-05) * w + b

        def _attn(x, wq, wk, wv, wo, bq, bk, bv, bo):
            Bb, T, C = x.shape
            hd = C // H
            q = (x @ wq + bq).reshape(Bb, T, H, hd).transpose(0, 2, 1, 3)
            k = (x @ wk + bk).reshape(Bb, T, H, hd).transpose(0, 2, 1, 3)
            v = (x @ wv + bv).reshape(Bb, T, H, hd).transpose(0, 2, 1, 3)
            att = jnp.einsum('bhqd,bhkd->bhqk', q, k) * hd ** (-0.5)
            causal = jnp.tril(jnp.ones((T, T), bool))
            att = jnp.where(causal, att, -jnp.inf)
            att = jax.nn.softmax(att, axis=-1)
            y = jnp.einsum('bhqk,bhkd->bhqd', att, v).transpose(0, 2, 1, 3).reshape(Bb, T, C)
            return y @ wo + bo

        def _ffn(h, w1, b1, w2, b2):
            return jax.nn.gelu(h @ w1 + b1, approximate=False) @ w2 + b2

        def _combine_weights(logits):
            vals, idx = jax.lax.top_k(logits, K)
            w = jax.nn.softmax(vals, axis=-1)
            onehot = (idx[..., None] == jnp.arange(E)).astype(w.dtype)
            return jnp.sum(w[..., None] * onehot, axis=-2)

        def _token_moe(h, gw, gb, w1, b1, w2, b2):
            cw = _combine_weights(h @ gw + gb)
            out = jnp.zeros_like(h)
            for e in range(E):
                out = out + _ffn(h, w1[e], b1[e], w2[e], b2[e]) * cw[..., e:e + 1]
            return out

        def _seq_moe(h, gw, gb, w1, b1, w2, b2):
            cw = _combine_weights(h.mean(axis=1) @ gw + gb)
            out = jnp.zeros_like(h)
            for e in range(E):
                out = out + _ffn(h, w1[e], b1[e], w2[e], b2[e]) * cw[:, e, None, None]
            return out
        for l in range(L):
            x = x + _attn(_ln(x, ln1_w[l], ln1_b[l]), wq[l], wk[l], wv[l], wo[l], bq[l], bk[l], bv[l], bo[l])
            h = _ln(x, ln2_w[l], ln2_b[l])
            moe = _token_moe if l % 2 == 0 else _seq_moe
            x = x + moe(h, gate_w[l], gate_b[l], e_w1[l], e_b1[l], e_w2[l], e_b2[l])
        return x
    x = x + _L0_ffn_ref(_L0_cond_ref(x, cond_8, L0_cond_W_base, L0_cond_b_base, L0_cond_As, L0_cond_Bs), L0_ffn_ln_w, L0_ffn_Wg, L0_ffn_bg, L0_ffn_W1a, L0_ffn_b1a, L0_ffn_W1b, L0_ffn_b1b, L0_ffn_W2, L0_ffn_b2)
    x = x + _L1_ffn_ref(_L1_cond_ref(x, cond_8, L1_cond_weight, L1_cond_mask, L1_cond_bias), L1_ffn_ln1_w, L1_ffn_ln1_b, L1_ffn_ln2_w, L1_ffn_ln2_b, L1_ffn_wq, L1_ffn_wk, L1_ffn_wv, L1_ffn_wo, L1_ffn_bq, L1_ffn_bk, L1_ffn_bv, L1_ffn_bo, L1_ffn_gate_w, L1_ffn_gate_b, L1_ffn_e_w1, L1_ffn_e_b1, L1_ffn_e_w2, L1_ffn_e_b2)
    return x

_drawn_inputs = setup_inputs


def setup_inputs(seed=0):
    import zlib

    import numpy as np

    out = dict(_drawn_inputs(seed))
    spreads = {'L0_ffn_ln_w': (1.0, 0.2),
     'L0_ffn_bg': (0.0, 0.1),
     'L0_ffn_b1a': (0.0, 0.1),
     'L0_ffn_b1b': (0.0, 0.1),
     'L0_ffn_b2': (0.0, 0.1),
     'L1_ffn_ln1_w': (1.0, 0.6),
     'L1_ffn_ln1_b': (0.0, 0.8),
     'L1_ffn_ln2_w': (1.0, 0.6),
     'L1_ffn_ln2_b': (0.0, 0.58),
     'L1_ffn_bq': (0.0, 2.0),
     'L1_ffn_bk': (0.0, 2.0),
     'L1_ffn_bv': (0.0, 0.435),
     'L1_ffn_bo': (0.0, 0.1),
     'L1_ffn_gate_b': (0.0, 0.1),
     'L1_ffn_e_b1': (0.0, 0.531),
     'L1_ffn_e_b2': (0.0, 0.1)}
    factors = {'L1_ffn_wq': 8.0, 'L1_ffn_wk': 8.0}
    for name, (base, spread) in spreads.items():
        noise = np.random.default_rng([zlib.crc32(name.encode()), seed]).standard_normal(out[name].shape)
        drawn = base * np.exp(spread * noise) if base else spread * noise
        out[name] = jnp.asarray(drawn.astype(out[name].dtype))
    for name, factor in factors.items():
        out[name] = (out[name] * factor).astype(out[name].dtype)
    return out
```

```python
from contextlib import ExitStack

import numpy as np

import concourse.bass as bass
from concourse import mybir

F32 = mybir.dt.float32
F32R = mybir.dt.float32r
BF16 = mybir.dt.bfloat16
U32 = mybir.dt.uint32
ALU = mybir.AluOpType
ACT = mybir.ActivationFunctionType
AX = mybir.AxisListType

B, S, D = 8, 256, 128
P = 128
N = B * S
NT = N // P
TPB = S // P
BLK = 512
NBLK = N // BLK
TB = BLK // P
E = 8
F = 512
FC = F // P
EC = NBLK * FC
CH = E * EC
H, HD = 16, 8
L = 2
HG = 4
NG = H // HG
SLOT = 32
LORA_SCALE = 2.0
RMS_EPS = float(np.finfo(np.float32).eps)
LN_EPS = 1e-5
ATT_SCALE = HD ** -0.5
NEG = -1e30
PARTS = 3
ROW_OF = [0, 3 * HD, 5 * HD]
MROW = 6 * HD
MROWS = 2
RING = 3
QK_LOADS = 2 * 6 + 1
SUNITS = 12
T_FREE = 3
S_FREE = 2
PROB_FREE = 2
OT_FREE = 2
BANK_FREE = 1
GEL_FREE = 4
U_FREE = 4
ACT_FREE = 4
U32_FREE = 4


def lay(items):
    table, at = {}, 0
    for name, n in items:
        table[name] = (at, at + n)
        at += n
    return table, at


COL, NCOL = lay([("ln_w", 1), ("ln1_w", L), ("ln1_b", L), ("ln2_w", L), ("ln2_b", L), ("bq", L), ("bk", L),
                 ("b1a", E * FC), ("b1b", E * FC), ("e_b1", E * FC)])
ROW, NROW = lay([("b_base", D), ("bias", D), ("bg", E), ("gate_b0", E), ("gate_b1", E), ("bv0", D), ("bv1", D),
                 ("bo0", D), ("bo1", D), ("cond", B * E), ("iota", E)])


class Signals:

    def __init__(self, sem, tag, names):
        self.all = {n: sem(f"{tag}_{n}") for n in names.split()}

    def __getattr__(self, name):
        return self.all[name]


def build(nc, xT, As, BsT, WbT, w_er, cols_in, rows_in, Wg, W1a, W1b, W2, b2, WT, maskT,
          att_in, e_w1, e_w2, e_b1s, out):
    we_dram = [nc.dram_tensor(f"we_dram{m}", [E, N], F32, kind="Internal").ap() for m in range(2)]
    qk_dram = nc.dram_tensor("qk_dram", [PARTS, 2, HD, H * S], BF16, kind="Internal").ap()
    ids_dram = nc.dram_tensor("ids_dram", [B, 2], U32, kind="Internal").ap()

    with ExitStack() as ctx:
        def sb(name, shape, dt=F32):
            return ctx.enter_context(nc.sbuf_tensor(name, shape, dt))

        def sem(name):
            return ctx.enter_context(nc.semaphore(name))

        bank = [ctx.enter_context(nc.psum_tensor(f"bank{i}", [P, BLK], F32)) for i in range(8)]

        xTs = sb("xTs", [P, N])
        z = sb("z", [P, TPB + NT, D])
        hn = sb("hn", [P, NT, D])
        hT = sb("hT", [P, N])
        hT_hi = sb("hT_hi", [P, N], F32R)
        hT_lo = sb("hT_lo", [P, N], F32R)
        cols = sb("cols", [P, NCOL])
        rows = sb("rows", [P, NROW])
        ident = sb("ident", [P, P])
        ident_bf = sb("ident_bf", [P, P], BF16)
        mask_q = sb("mask_q", [P, 2 * P], BF16)
        mask_k = sb("mask_k", [P, 2 * P], BF16)
        weff = sb("weff", [P, B, D])
        stat = sb("stat", [P, NT, 6])
        mv = sb("mv", [P, NT, 2])
        var = sb("var", [P, NT])
        rstd = sb("rstd", [P, NT])
        half = sb("half", [P, NT])
        logit = sb("logit", [P, NT, E])
        top_v = sb("top_v", [P, NT, 8])
        top_i = sb("top_i", [P, NT, 8], U32)
        top_f = sb("top_f", [P, NT, 2])
        pair = sb("pair", [P, 4, NT])
        we = sb("we", [P, E, NT])
        onehot = sb("onehot", [P, E, NT])
        weT = sb("weT", [P, P])
        gate_sb = sb("gate_sb", [P, 3, E])
        b2_sb = sb("b2_sb", [E, 3, D])
        att_w = sb("att_w", [P, L, 4, D])
        whi = sb("whi", [P, 2, 3, F], F32R)
        wlo = sb("wlo", [P, 2, 3, F], F32R)
        bias1 = sb("bias1", [P, 2, 2, FC])
        u_hi = sb("u_hi", [P, U_FREE, BLK], F32R)
        u_lo = sb("u_lo", [P, U_FREE, BLK], F32R)
        qp = sb("qp", [P, RING, H * S], BF16)
        kp = sb("kp", [P, RING, H * S], BF16)
        mT = sb("mT", [MROWS * H, S], BF16)
        ids = sb("ids", [1, B * 2], U32)
        weT8 = hn[0:E, :, :].rearrange("p t d -> p (t d)")

        arena = sb("arena", [P, 12288])

        def views(items):
            got, at = [], 0
            for shape, dt in items:
                n = int(np.prod(shape)) * (2 if dt == BF16 else 4) // 4
                v = arena[:, at:at + n]
                at += n
                v = v.bitcast(BF16) if dt == BF16 else v
                if len(shape) == 2:
                    v = v.rearrange("p (a b) -> p a b", a=shape[0])
                elif len(shape) == 3:
                    v = v.rearrange("p (a b c) -> p a b c", a=shape[0], b=shape[1])
                elif len(shape) == 4:
                    v = v.rearrange("p (a b c d) -> p a b c d", a=shape[0], b=shape[1], c=shape[2])
                got.append(v)
            assert at <= arena.shape[1], at
            return got

        wraw, wbc, act_s, gated, u32 = views([([2, 3, F], F32), ([2, N], F32), ([4, BLK], F32), ([2, BLK], F32),
                                              ([U32_FREE, BLK], F32)])
        (prob, vaug, oT, qk32, qkr, qks, zn, zT, onorm, onT, orec, mmax, msp) = views([
            ([2, 3 * BLK], F32), ([RING, TPB, H, SLOT], F32), ([NG, S], F32), ([2, S], F32), ([2, S], F32),
            ([PARTS, 2, S], BF16), ([TPB, D], F32), ([S], F32), ([TPB, D], F32), ([S], F32), ([TPB, H], F32),
            ([TPB, H], F32), ([TPB, MROWS, H], BF16)])
        w1s, w2s, b1s, gel, ug, yx, oseq, cw, diag, ones8, b2s, hmean = views([
            ([4, F], F32), ([4, FC, D], F32), ([4, FC], F32), ([2, FC, S], F32), ([2, FC, S], F32), ([2, S], F32),
            ([B, TPB, D], F32), ([B, 2], F32), ([B, 2], F32), ([P], F32), ([B], F32), ([B], F32)])
        start = z[:, TPB:, :].rearrange("p t d -> p (t d)")
        wt = start[:, 0:B * D].rearrange("p (g o) -> p g o", g=E)
        As_sb, BsT_sb, WbT_sb, maskT_sb = (start[:, (8 + n) * D:(9 + n) * D] for n in range(4))
        bsw = arena[:, 0:B * D].rearrange("p (b o) -> p b o", b=B)
        wer = arena[:, B * D:B * D + B]
        square = arena[:, 2 * B * D:2 * B * D + D]
        x_all = hn[:].rearrange("p t d -> p (t d)")

        def oseq_at(b):
            return oseq[:, bass.ds(b, 1)].rearrange("p a t d -> p (a t) d")

        def col(name, i=0):
            a = COL[name][0] + i
            return cols[:, a:a + 1]

        def row(name, n=P):
            a, b = ROW[name]
            return rows[0:n, a:b]

        def mid(v, n):
            return v.rearrange("p (a d) -> p a d", a=1).to_broadcast([v.shape[0], n, v.shape[1]])

        def last(v, n):
            return v.unsqueeze(2).to_broadcast([v.shape[0], v.shape[1], n])

        g = Signals(sem, "g", "ld_lora ld_vec ld_rest ident masks ones bsw weff_mm weff_ok h0_mm h0_ok sq ms rms "
                    "line mixmask mix x1 z_mm z_ok back_mm back pad carry_sp carry_dve")
        prep = [Signals(sem, f"p{m}", "hn tr hT logits diff exp we var rstd" +
                        (" hi lo weT_mm weT store load" if m < 2 else "")) for m in range(3)]
        moe = [Signals(sem, f"x{m}", "split a b act gate scaled hi lo y yT") for m in range(2)]
        PER = {}
        PER.update({n: B for n in "st ag var rstd zn zb zT_mm zT qk_mm qk v_mm v p1 r p2 p3 mhi msp mT_mm mT".split()})
        PER.update({n: SUNITS * B for n in "s_mm red t_mm exp".split()})
        PER.update({n: TPB * (B + 1) for n in "oTT rec on".split()})
        PER.update({n: B + 1 for n in "on_mm onT wo_mm z".split()})
        PER.update(vinit=3, av=NG * B, oT=2 * B, qk_st=16 * PARTS * B, qk_ld=16 * QK_LOADS * B, m_ld=16 * MROWS * B)
        att = Signals(sem, "a", " ".join(PER))
        q = Signals(sem, "q", "mean cw_in cw_mm cw b2_mm b2 a gel ug y yx t o store ids ids_ld weT weT_mm ones")
        w_ld = [sem(f"w_ld{n}") for n in range(2)]
        r_ld = [sem(f"r_ld{n}") for n in range(2)]
        q_w = [sem(f"q_w{n}") for n in range(4)]

        block = ctx.enter_context(nc.Block())

        def expert_dram(m):
            return ([W1a, W1b], W2) if m == 0 else ([e_w1[0]], e_w2[0])

        @block.sync
        def _(sp):
            for dst, src in ((xTs[:], xT), (As_sb, As), (BsT_sb, BsT), (WbT_sb, WbT), (wer, w_er)):
                sp.dma_start(dst, src).then_inc(g.ld_lora, 16)
            sp.dma_start(cols[:], cols_in).then_inc(g.ld_vec, 16)
            sp.dma_start(rows[:], rows_in.to_broadcast([P, NROW])).then_inc(g.ld_vec, 16)
            for dst, src in ((gate_sb[:], Wg), (b2_sb[:], b2), (wt, WT), (maskT_sb, maskT), (att_w[:], att_in)):
                sp.dma_start(dst, src).then_inc(g.ld_rest, 16)

            def prepare(m):
                s = prep[m]
                sp.wait_ge(s.weT, 1)
                sp.dma_start(we_dram[m].rearrange("e (t p) -> (e t) p", t=NT), weT[:]).then_inc(s.store, 16)
                sp.wait_ge(s.store, 16)
                sp.dma_start(weT8, we_dram[m]).then_inc(s.load, 16)

            def moe_loads(m):
                s = moe[m]
                firsts, second = expert_dram(m)
                second = second.rearrange("e (c p) d -> e p c d", p=P)
                with sp.Fori(0, E // 2) as i:
                    for k in range(2):
                        e = 2 * i + k
                        sp.wait_ge(s.split, 6 * e + 6)
                        sp.sem_inc(g.carry_sp, 1)
                        for n, w in enumerate(firsts):
                            sp.dma_start(wraw[:, k, n, :], w[e]).then_inc(w_ld[k], 16)
                        sp.dma_start(wraw[:, k, 2, :].rearrange("p (c d) -> p c d", c=FC),
                                     second[e]).then_inc(w_ld[k], 16)
                        sp.wait_ge(s.scaled, EC * e + EC)
                        sp.sem_inc(g.carry_sp, 1)
                        sp.dma_start(wbc[:, k, :], we_dram[m][bass.ds(e, 1), :].to_broadcast([P, N])
                                     ).then_inc(r_ld[k], 16)

            def attention(l):
                s = att

                def queries_keys(a, r):
                    sp.wait_ge(s.p3, l * PER["p3"] + a + 1)
                    sp.sem_inc(g.carry_sp, 1)
                    sp.wait_ge(s.qk_ld, l * PER["qk_ld"] + 16 * QK_LOADS * a)
                    sp.sem_inc(g.carry_sp, 1)
                    for n in range(PARTS):
                        sp.dma_start(qk_dram[n].rearrange("w d (h t) -> (d h) w t", h=H),
                                     qks[:, n]).then_inc(s.qk_st, 16)
                    sp.wait_ge(s.qk_st, l * PER["qk_st"] + 16 * PARTS * (a + 1))
                    sp.sem_inc(g.carry_sp, 1)
                    for i in range(PARTS):
                        n = PARTS - i
                        a0 = ROW_OF[i]
                        for w, ring in ((0, qp), (1, kp)):
                            for j in range(n):
                                part = i if w == 0 else j
                                sp.dma_start(
                                    ring[a0 + HD * j:a0 + HD * (j + 1), r, :].rearrange("d (h t) -> d h t", h=H),
                                    qk_dram[part, w].rearrange("d (h t) -> d h t", h=H)).then_inc(s.qk_ld, 16)
                    sp.dma_start(qp[MROW:MROW + MROWS, r, :], qp[2 * 32:2 * 32 + MROWS, r, :]).then_inc(s.qk_ld, 16)

                def maxima(b, r):
                    sp.wait_ge(s.mT, l * PER["mT"] + b + 1)
                    sp.sem_inc(g.carry_sp, 1)
                    dst = qp[MROW:MROW + MROWS, r, :].rearrange("r (h t) -> r h t", h=H)
                    for n in range(MROWS):
                        sp.dma_start(dst[n:n + 1], mT[n * H:(n + 1) * H, :]).then_inc(s.m_ld, 16)

                queries_keys(0, 0)
                queries_keys(1, 1)
                maxima(0, 0)

                def step(b, k, more_a, more_b):
                    if more_a:
                        sp.wait_ge(s.exp, l * PER["exp"] + T_FREE + SUNITS * b)
                        sp.sem_inc(g.carry_sp, 1)
                        queries_keys(b + 2, (k + 2) % RING)
                    if more_b:
                        maxima(b + 1, (k + 1) % RING)

                with sp.Fori(0, (B - 2) // RING) as i:
                    for k in range(RING):
                        step(RING * i + k, k, True, True)
                step(B - 2, (B - 2) % RING, False, True)

            prepare(0)
            moe_loads(0)
            attention(0)
            prepare(1)
            moe_loads(1)
            attention(1)

            sp.wait_ge(prep[2].we, 1)
            sp.dma_start(ids_dram, top_i[0:B, 0, 0:2]).then_inc(q.ids, 16)
            sp.wait_ge(q.ids, 16)
            sp.dma_start(ids[:], ids_dram.rearrange("b k -> (b k)").rearrange("(a n) -> a n", a=1)
                         ).then_inc(q.ids_ld, 16)
            sp.wait_ge(q.ids_ld, 16)
            second = e_w2[1].rearrange("e (c p) d -> e p c d", p=P)
            def expert_loads(i, k):
                e = sp.value_load(ids[0:1, bass.ds(4 * i + k, 1)], min_val=0, max_val=E - 1)
                sp.wait_ge(q.y, 4 * i + k + 1)
                sp.sem_inc(g.carry_sp, 1)
                sp.dma_start(w1s[:, k, :], e_w1[1][bass.ds(e, 1), :, :].rearrange("a p f -> (a p) f")
                             ).then_inc(q_w[k], 16)
                sp.dma_start(w2s[:, k], second[bass.ds(e, 1)].rearrange("a p c d -> (a p) c d")
                             ).then_inc(q_w[k], 16)
                sp.dma_start(b1s[:, k, :], e_b1s[bass.ds(e, 1)].rearrange("a p c -> (a p) c")
                             ).then_inc(q_w[k], 16)

            def store(b):
                sp.wait_ge(q.o, b + 1)
                sp.sem_inc(g.carry_sp, 1)
                sp.dma_start(out[bass.ds(b, 1)].rearrange("a (t p) d -> p (a t) d", p=P), oseq_at(b)
                             ).then_inc(q.store, 16)

            for k in range(4):
                expert_loads(0, k)
            with sp.Fori(1, B // 2) as i:
                for k in range(4):
                    expert_loads(i, k)
                    if k % 2:
                        store(2 * i - 2 + k // 2)
            store(B - 2)
            store(B - 1)
            sp.wait_ge(q.store, 16 * B)

        @block.gpsimd
        def _(pool):
            pool.memset(ident[:], 0.0).then_inc(g.ident, 1)
            pool.wait_ge(g.ident, 1)
            pool.affine_select(out=ident[:], in_=ident[:], compare_op=ALU.not_equal, fill=1.0, base=0,
                               pattern=[[-1, P]], channel_multiplier=1).then_inc(g.ident, 1)
            pool.memset(half[:], -0.5).then_inc(g.masks, 1)
            pool.memset(mask_q[:], 0.0).then_inc(g.masks, 1)
            pool.memset(mask_k[:], 0.0).then_inc(g.masks, 1)
            pool.wait_ge(g.ident, 2)
            pool.tensor_copy(ident_bf[:], ident[:]).then_inc(g.ident, 1)
            pool.wait_ge(g.masks, 3)
            pool.affine_select(out=mask_q[:, P:2 * P], in_=mask_q[:, P:2 * P], compare_op=ALU.is_ge, fill=NEG,
                               base=0, pattern=[[-1, P]], channel_multiplier=1).then_inc(g.masks, 1)
            pool.affine_select(out=mask_k[:, 0:P], in_=mask_k[:, 0:P], compare_op=ALU.is_ge, fill=NEG,
                               base=0, pattern=[[1, P]], channel_multiplier=-1).then_inc(g.masks, 1)

            def power(before, after):
                pool.wait_ge(before, 1)
                pool.tensor_tensor(rstd[:], var[:], half[:], ALU.pow).then_inc(after, 1)

            power(g.ms, g.rms)
            pool.wait_ge(g.ld_rest, 16 * 5)
            pool.tensor_tensor(wt, wt, mid(maskT_sb, E), ALU.mult).then_inc(g.mixmask, 1)
            pool.memset(qp[:].bitcast(F32), 0.0).then_inc(g.pad, 1)
            pool.memset(kp[:].bitcast(F32), 0.0).then_inc(g.pad, 1)
            pool.wait_ge(g.pad, 2)
            pool.memset(kp[32:64, :, :], 1.0).then_inc(g.pad, 1)
            pool.wait_ge(g.pad, 3)
            pool.memset(z[:, 0:TPB, :], 0.0).then_inc(g.pad, 1)

            s = moe[0]
            pool.sem_inc(s.scaled, 2 * EC)
            with pool.Fori(0, E // 2) as i:
                for kk in range(2 * EC):
                    k = 2 * EC * i + kk
                    e, blk = kk // EC, kk % EC // FC
                    if kk % EC == 0:
                        pool.wait_ge(r_ld[e], 16 * (i + 1))
                    pool.wait_ge(s.gate, ACT_FREE + k + 1)
                    pool.wait_ge(s.lo, k + 1)
                    pool.tensor_tensor(u32[:, kk % U32_FREE, :], gated[:, kk % 2, :],
                                       wbc[:, e, blk * BLK:(blk + 1) * BLK], ALU.mult).then_inc(s.scaled, 1)

            def attention(l):
                s = att
                pool.wait_ge(moe[l].lo, U32_FREE + CH)
                v = vaug.rearrange("p r k h s -> p (r k h) s")
                pool.memset(v, 0.0).then_inc(s.vinit, 1)
                pool.memset(oT.rearrange("p a b -> p (a b)"), 1.0).then_inc(s.vinit, 1)
                pool.wait_ge(s.vinit, l * PER["vinit"] + 2)
                pool.memset(v[:, :, HD:HD + 1], 1.0).then_inc(s.vinit, 1)

                def norm(b):
                    pool.wait_ge(s.var, l * PER["var"] + b + 1)
                    pool.tensor_tensor(rstd[:, 0:TPB], var[:, 0:TPB], half[:, 0:TPB], ALU.pow).then_inc(s.rstd, 1)
                    pool.wait_ge(s.zn, l * PER["zn"] + b + 1)
                    zb = z[:, bass.ds(TPB * (b + 1), TPB), :]
                    pool.tensor_tensor(zb, zb, mid(row(f"bo{l}"), TPB), ALU.add).then_inc(s.zb, 1)

                norm(0)
                norm(1)
                with pool.Fori(2, B) as b:
                    norm(b)

            attention(0)
            power(prep[1].var, prep[1].rstd)
            attention(1)
            power(prep[2].var, prep[2].rstd)
            pool.memset(ones8, 1.0).then_inc(q.ones, 1)

        @block.scalar
        def _(act):
            for t in range(NT):
                if t % TB == 0:
                    act.wait_ge(g.h0_ok, t // TB + 1)
                if t:
                    act.wait_ge(g.sq, t)
                act.activation(square, hn[:, t, :], ACT.Square, accum_out=stat[:, t, 0:1]).then_inc(g.sq, 1)

            def prepare(m, l_bias):
                s = prep[m]
                for j in range(NBLK):
                    act.wait_ge(s.tr, j + 1)
                    if m == 0:
                        act.activation(hT[:, j * BLK:(j + 1) * BLK], bank[j % 2][:], ACT.Copy,
                                       scale=col("ln_w")).then_inc(s.hT, 1)
                    else:
                        act.activation(hT[:, j * BLK:(j + 1) * BLK], bank[j % 2][:], ACT.Identity,
                                       bias=col("ln2_b", l_bias), scale=col("ln2_w", l_bias)).then_inc(s.hT, 1)
                n, c = (P, NT) if m < 2 else (B, 1)
                act.wait_ge(s.diff, 1)
                act.activation(pair[0:n, 1, 0:c], pair[0:n, 0, 0:c], ACT.Exp).then_inc(s.exp, 1)
                if m < 2:
                    act.wait_ge(s.weT_mm, 1)
                    act.activation(weT[:], bank[3][:, 0:P], ACT.Copy).then_inc(s.weT, 1)

            def token_moe(m):
                s = moe[m]
                func = ACT.Silu if m == 0 else ACT.Gelu
                n_a = 2 if m == 0 else 4

                def nonlinear(i, kk):
                    k = 2 * EC * i + kk
                    e, c = kk // EC, kk % FC
                    act.wait_ge(s.a, k + 1)
                    if m == 0:
                        act.wait_ge(s.gate, k + 1)
                    else:
                        act.wait_ge(s.scaled, 2 * EC + k - 3)
                    act.activation(act_s[:, kk % 4, :], bank[kk % n_a][:], func,
                                   bias=bias1[:, e, 0, c:c + 1]).then_inc(s.act, 1)

                def high(i, kk):
                    k = 2 * EC * i + kk
                    act.wait_ge(s.scaled, 2 * EC + k + 1)
                    act.wait_ge(s.y, k + 1)
                    act.activation(u_hi[:, kk % U_FREE, :], u32[:, kk % U32_FREE, :], ACT.Copy).then_inc(s.hi, 1)

                def body(i, end):
                    for kk in range(2 * EC):
                        if kk + 2 < end:
                            if kk + 2 < 2 * EC:
                                nonlinear(i, kk + 2)
                            else:
                                nonlinear(i + 1, kk + 2 - 2 * EC)
                        high(i, kk)

                nonlinear(0, 0)
                nonlinear(0, 1)
                with act.Fori(0, E // 2 - 1) as i:
                    body(i, 2 * EC + 2)
                body(E // 2 - 1, 2 * EC)

            prepare(0, 0)
            token_moe(0)

            def attention(l):
                s = att

                def norm_T(a):
                    act.wait_ge(s.zT_mm, l * PER["zT_mm"] + a + 1)
                    act.activation(zT, bank[0][:, 0:S], ACT.Identity, bias=col("ln1_b", l),
                                   scale=col("ln1_w", l)).then_inc(s.zT, 1)

                def part(a, n):
                    if n == 0:
                        act.wait_ge(s.qk, l * PER["qk"] + a + 1)
                        act.wait_ge(s.qk_st, l * PER["qk_st"] + 16 * PARTS * a)
                        act.activation(qks[:, 0], qk32, ACT.Copy).then_inc(s.p1, 1)
                    else:
                        act.wait_ge(s.r, l * PER["r"] + a + 1)
                        act.activation(qks[:, 1], qkr, ACT.Copy).then_inc(s.p2, 1)

                def exps(b, gr):
                    for t in range(3):
                        act.wait_ge(s.t_mm, l * PER["t_mm"] + SUNITS * b + 3 * gr + t + 1)
                        if t == 0:
                            act.wait_ge(s.av, l * PER["av"] + NG * b + gr + 1)
                        act.activation(prob[:, gr % 2, t * BLK:(t + 1) * BLK], bank[4 + t][:], ACT.Exp,
                                       scale=ATT_SCALE).then_inc(s.exp, 1)

                def attended(b, r):
                    act.wait_ge(s.av, l * PER["av"] + PROB_FREE + NG * b + 2 * r + 2)
                    act.wait_ge(s.oTT, l * PER["oTT"] + TPB * (b + 1))
                    act.activation(oT[:, 2 * r:2 * r + 2, :], bank[7][:].rearrange("p (g t) -> p g t", g=2),
                                   ACT.Copy).then_inc(s.oT, 1)

                def normal_T(d1):
                    act.wait_ge(s.on_mm, l * PER["on_mm"] + d1)
                    act.activation(onT, bank[0][:, 0:S], ACT.Copy).then_inc(s.onT, 1)

                def maxima_T(b):
                    act.wait_ge(s.mT_mm, l * PER["mT_mm"] + b + 1)
                    act.wait_ge(s.m_ld, l * PER["m_ld"] + 16 * MROWS * b)
                    act.activation(mT[:], bank[2][0:MROWS * H, 0:P].bitcast(BF16), ACT.Copy).then_inc(s.mT, 1)

                def step(b, more_a, more_b):
                    if more_a:
                        norm_T(b + 2)
                        part(b + 2, 0)
                    exps(b, 0)
                    if more_a:
                        part(b + 2, 1)
                    normal_T(b + 1)
                    exps(b, 1)
                    if more_b:
                        maxima_T(b + 1)
                    exps(b, 2)
                    attended(b, 0)
                    exps(b, 3)
                    attended(b, 1)

                if l == 0:
                    act.sem_inc(s.exp, T_FREE)
                    act.sem_inc(s.oT, OT_FREE)
                    act.sem_inc(s.onT, BANK_FREE)
                for a in range(2):
                    norm_T(a)
                    part(a, 0)
                    part(a, 1)
                maxima_T(0)
                with act.Fori(0, B - 2) as b:
                    step(b, True, True)
                step(B - 2, False, True)
                step(B - 1, False, False)
                normal_T(B + 1)

            attention(0)
            prepare(1, 0)
            token_moe(1)
            act.wait_ge(moe[1].y, U_FREE + CH)
            for j in range(NBLK):
                act.activation(hT[:, j * BLK:(j + 1) * BLK], bank[4 + j][:], ACT.Copy).then_inc(moe[1].yT, 1)
            attention(1)
            prepare(2, 1)

            act.sem_inc(q.gel, GEL_FREE)
            act.wait_ge(q.cw_mm, 1)
            act.activation(cw.rearrange("p b k -> p (b k)"), bank[2][:, 0:2 * B], ACT.Copy).then_inc(q.cw, 1)
            act.wait_ge(q.weT_mm, 1)
            act.activation(weT[0:E, 0:B], bank[3][0:E, 0:B], ACT.Copy).then_inc(q.weT, 1)
            act.wait_ge(q.b2_mm, 1)
            act.activation(b2s, bank[3][:, 0:B], ACT.Copy).then_inc(q.b2, 1)
            with act.Fori(0, B // 2) as i:
                for k in range(4):
                    n = 4 * i + k
                    act.wait_ge(q.ug, n + 1)
                    for c in range(FC):
                        if c % 2 == 0:
                            act.wait_ge(q.a, 2 * n + c // 2 + 1)
                        last_ = act.activation(gel[:, k % 2, c, :],
                                               bank[2 * (k % 2) + c // 2][:, (c % 2) * S:(c % 2 + 1) * S], ACT.Gelu,
                                               bias=b1s[:, k, c:c + 1])
                        if c % 2:
                            last_.then_inc(q.gel, 1)

        @block.vector
        def _(dve):
            lines = [0]

            def line(ins):
                lines[0] += 1
                ins.then_inc(g.line, 1)
                dve.wait_ge(g.line, lines[0])

            dve.wait_ge(g.ld_lora, 16 * 5)
            for b in range(B):
                up = dve.tensor_scalar(bsw[:, b, :], BsT_sb, wer[:, b:b + 1], LORA_SCALE, ALU.mult, ALU.mult)
            up.then_inc(g.bsw, 1)
            for j in range(2):
                dve.wait_ge(g.weff_mm, j + 1)
                dve.tensor_tensor(weff[:, 4 * j:4 * j + 4, :], bank[j][:].rearrange("p (b o) -> p b o", b=4),
                                  mid(WbT_sb, 4), ALU.add).then_inc(g.weff_ok, 1)
            dve.wait_ge(g.ld_vec, 32)
            for j in range(NBLK):
                dve.wait_ge(g.h0_mm, j + 1)
                dve.tensor_tensor(hn[:, TB * j:TB * (j + 1), :], bank[2 + j][:].rearrange("p (t o) -> p t o", t=TB),
                                  mid(row("b_base"), TB), ALU.add).then_inc(g.h0_ok, 1)
            dve.wait_ge(g.sq, NT)
            dve.tensor_scalar(var[:], stat[:, :, 0], 1.0 / D, RMS_EPS, ALU.mult, ALU.add).then_inc(g.ms, 1)
            dve.wait_ge(g.rms, 1)
            for j in range(NBLK):
                v = hn[:, TB * j:TB * (j + 1), :]
                dve.tensor_tensor(v, v, last(rstd[:, TB * j:TB * (j + 1)], D), ALU.mult).then_inc(prep[0].hn, 1)

            def layer_norm(s):
                for t in range(NT):
                    ins = dve.bn_stats(stat[:, t, :], z[:, TPB + t, :])
                line(ins)
                for t in range(NT):
                    ins = dve.bn_aggr(mv[:, t, :], stat[:, t, :])
                line(ins)
                dve.tensor_scalar(var[:], mv[:, :, 1], LN_EPS, None, ALU.add).then_inc(s.var, 1)
                dve.wait_ge(s.rstd, 1)
                for t in range(NT):
                    ins = dve.tensor_scalar(hn[:, t, :], z[:, TPB + t, :], mv[:, t, 0:1], rstd[:, t:t + 1],
                                            ALU.subtract, ALU.mult)
                    if t % TB == TB - 1:
                        ins.then_inc(s.hn, 1)

            def route(s, n, c, raw, bias):
                lg, tv, ti, tf, pr = logit[0:n, 0:c, :], top_v[0:n, 0:c, :], top_i[0:n, 0:c, :], top_f[0:n, 0:c, :], \
                    pair[0:n, :, 0:c]
                w, o = we[0:n, :, 0:c], onehot[0:n, :, 0:c]
                line(dve.tensor_tensor(lg, raw, mid(bias, c), ALU.add))
                for t in range(c):
                    ins = dve.max(tv[:, t, :], lg[:, t, :])
                line(ins)
                dve.tensor_tensor(pr[:, 0, :], tv[:, :, 1], tv[:, :, 0], ALU.subtract).then_inc(s.diff, 1)
                for t in range(c):
                    ins = dve.max_index(ti[:, t, :], tv[:, t, :], lg[:, t, :])
                line(ins)
                line(dve.tensor_copy(tf, ti[:, :, 0:2]))
                dve.wait_ge(s.exp, 1)
                line(dve.tensor_scalar(pr[:, 3, :], pr[:, 1, :], 1.0, None, ALU.add))
                line(dve.reciprocal(pr[:, 2, :], pr[:, 3, :]))
                line(dve.tensor_tensor(pr[:, 3, :], pr[:, 1, :], pr[:, 2, :], ALU.mult))
                experts = last(row("iota", n), c)
                line(dve.tensor_tensor(w, experts, mid(tf[:, :, 0], E), ALU.is_equal))
                line(dve.tensor_tensor(w, w, mid(pr[:, 2, :], E), ALU.mult))
                line(dve.tensor_tensor(o, experts, mid(tf[:, :, 1], E), ALU.is_equal))
                line(dve.tensor_tensor(o, o, mid(pr[:, 3, :], E), ALU.mult))
                dve.tensor_tensor(w, w, o, ALU.add).then_inc(s.we, 1)

            def prepare(m):
                s = prep[m]
                for j in range(NBLK):
                    v = slice(j * BLK, (j + 1) * BLK)
                    dve.wait_ge(s.hT, j + 1)
                    dve.tensor_copy(hT_hi[:, v], hT[:, v]).then_inc(s.hi, 1)
                    dve.wait_ge(s.hi, j + 1)
                    dve.tensor_tensor(hT_lo[:, v], hT[:, v], hT_hi[:, v].bitcast(F32), ALU.subtract
                                      ).then_inc(s.lo, 1)
                dve.wait_ge(s.logits, 1)
                route(s, P, NT, bank[2][:, 0:NT * E].rearrange("p (t e) -> p t e", t=NT),
                      row(("bg", "gate_b0")[m]))

            def token_moe(m):
                s = moe[m]
                n_w = 3 if m == 0 else 2
                which = (0, 1, 2) if m == 0 else (0, 2)
                dve.sem_inc(s.split, 12)
                dve.sem_inc(s.lo, U32_FREE)
                if m == 1:
                    dve.sem_inc(s.scaled, 2 * EC)
                else:
                    dve.sem_inc(s.gate, ACT_FREE)

                def split(i, e, n):
                    w, low = which[min(n // 2, n_w - 1)], n % 2
                    exp = 2 * i + e
                    if n == 0:
                        dve.wait_ge(w_ld[e], 16 * (m * 3 * E // 2 + n_w * (i + 1)))
                        dve.wait_ge(s.y, EC * (exp - 1) + U_FREE) if not isinstance(exp, int) or exp > 0 else None
                        for j, name in enumerate(("b1a", "b1b") if m == 0 else ("e_b1",)):
                            dve.tensor_copy(bias1[:, e, j, :], cols[:, bass.ds(COL[name][0] + FC * exp, FC)])
                    if n // 2 >= n_w:
                        dve.sem_inc(s.split, 1)
                    elif not low:
                        dve.tensor_copy(whi[:, e, w, :], wraw[:, e, w, :]).then_inc(s.split, 1)
                    else:
                        dve.wait_ge(s.split, 12 + 6 * exp + n)
                        dve.tensor_tensor(wlo[:, e, w, :], wraw[:, e, w, :], whi[:, e, w, :].bitcast(F32),
                                          ALU.subtract).then_inc(s.split, 1)

                def gate(i, kk):
                    k = 2 * EC * i + kk
                    e, c = kk // EC, kk % FC
                    dve.wait_ge(s.b, k + 1)
                    dve.wait_ge(s.act, k + 1)
                    dve.wait_ge(s.scaled, 2 * EC + k - 1)
                    dve.scalar_tensor_tensor(out=gated[:, kk % 2, :], in0=bank[2 + kk % 2][:],
                                             scalar=bias1[:, e, 1, c:c + 1], in1=act_s[:, kk % 4, :],
                                             op0=ALU.add, op1=ALU.mult).then_inc(s.gate, 1)

                def scale(i, kk):
                    k = 2 * EC * i + kk
                    e, blk = kk // EC, kk % EC // FC
                    if kk % EC == 0:
                        dve.wait_ge(r_ld[e], 16 * (E // 2 + i + 1))
                    dve.wait_ge(s.act, k + 1)
                    dve.wait_ge(s.lo, k + 1)
                    dve.tensor_tensor(u32[:, kk % U32_FREE, :], act_s[:, kk % 4, :],
                                      wbc[:, e, blk * BLK:(blk + 1) * BLK], ALU.mult).then_inc(s.scaled, 1)

                def low(i, kk):
                    k = 2 * EC * i + kk
                    dve.wait_ge(s.hi, k + 1)
                    dve.tensor_tensor(u_lo[:, kk % U_FREE, :], u32[:, kk % U32_FREE, :],
                                      u_hi[:, kk % U_FREE, :].bitcast(F32), ALU.subtract).then_inc(s.lo, 1)

                def mix(i, n):
                    b, gg = 2 * i + n // E, n % E
                    a0 = ROW["cond"][0]
                    acc = weff[:, bass.ds(b, 1), :].rearrange("p a o -> p (a o)")
                    c = rows[:, bass.ds(a0 + E * b + gg, 1)]
                    if gg == 0:
                        dve.tensor_scalar(acc, wt[:, gg, :], c, None, ALU.mult).then_inc(g.mix, 1)
                    else:
                        dve.wait_ge(g.mix, 2 * E * i + n)
                        dve.scalar_tensor_tensor(out=acc, in0=wt[:, gg, :], scalar=c, in1=acc, op0=ALU.mult,
                                                 op1=ALU.add).then_inc(g.mix, 1)

                lead = 2 if m == 0 else 1
                ahead = gate if m == 0 else scale

                def body(i, last_pair):
                    for kk in range(2 * EC):
                        nk = kk + lead
                        if nk < 2 * EC:
                            ahead(i, nk)
                        elif not last_pair:
                            ahead(i + 1, nk - 2 * EC)
                        low(i, kk)
                        if 4 <= kk % EC < 10:
                            if kk < EC:
                                split(i, 1, kk % EC - 4)
                            elif not last_pair:
                                split(i + 1, 0, kk % EC - 4)
                        if m == 0 and kk % 2:
                            mix(i, kk // 2)

                for n in range(6):
                    split(0, 0, n)
                if m == 0:
                    dve.wait_ge(g.mixmask, 1)
                for kk in range(lead):
                    ahead(0, kk)
                with dve.Fori(0, E // 2 - 1) as i:
                    body(i, False)
                body(E // 2 - 1, True)

            prepare(0)
            token_moe(0)
            dve.wait_ge(moe[0].y, U_FREE + CH)
            for j in range(NBLK):
                v = xTs[:, j * BLK:(j + 1) * BLK]
                dve.tensor_tensor(v, v, bank[4 + j][:], ALU.add).then_inc(g.x1, 1)
            for j in range(NBLK):
                dve.wait_ge(g.z_mm, j + 1)
                dve.tensor_tensor(z[:, TPB + TB * j:TPB + TB * (j + 1), :],
                                  bank[j][:].rearrange("p (t o) -> p t o", t=TB), mid(row("bias"), TB), ALU.add
                                  ).then_inc(g.z_ok, 1)
            dve.wait_ge(g.z_ok, NBLK)

            def attention(l):
                s = att
                if l == 0:
                    dve.sem_inc(s.red, S_FREE)
                    dve.sem_inc(s.z, BANK_FREE)

                def norm(b):
                    for t in range(TPB):
                        ins = dve.bn_stats(stat[:, t, :], z[:, bass.ds(TPB * (b + 1) + t, 1), :].rearrange(
                            "p a d -> p (a d)"))
                    ins.then_inc(s.st, 1)
                    dve.wait_ge(s.st, l * PER["st"] + b + 1)
                    dve.sem_inc(g.carry_dve, 1)
                    for t in range(TPB):
                        ins = dve.bn_aggr(mv[:, t, :], stat[:, t, :])
                    ins.then_inc(s.ag, 1)
                    dve.wait_ge(s.ag, l * PER["ag"] + b + 1)
                    dve.tensor_scalar(var[:, 0:TPB], mv[:, 0:TPB, 1], LN_EPS, None, ALU.add).then_inc(s.var, 1)
                    dve.wait_ge(s.rstd, l * PER["rstd"] + b + 1)
                    dve.wait_ge(s.zT_mm, l * PER["zT_mm"] + b)
                    for t in range(TPB):
                        ins = dve.tensor_scalar(zn[:, t, :], z[:, bass.ds(TPB * (b + 1) + t, 1), :].rearrange(
                            "p a d -> p (a d)"), mv[:, t, 0:1], rstd[:, t:t + 1], ALU.subtract, ALU.mult)
                    ins.then_inc(s.zn, 1)

                def project(a, r):
                    dve.wait_ge(s.qk_mm, l * PER["qk_mm"] + a + 1)
                    dve.tensor_scalar(qk32[:, 0, :], bank[0][:, 0:S], col("bq", l), None, ALU.add)
                    dve.tensor_scalar(qk32[:, 1, :], bank[0][:, S:2 * S], col("bk", l), None, ALU.add
                                      ).then_inc(s.qk, 1)
                    dve.wait_ge(s.v_mm, l * PER["v_mm"] + a + 1)
                    for t in range(TPB):
                        ins = dve.tensor_tensor(
                            vaug[:, r, t, :, 0:HD], bank[1][:, t * P:(t + 1) * P].rearrange("p (h d) -> p h d", h=H),
                            row(f"bv{l}").rearrange("p (h d) -> p h d", h=H), ALU.add)
                    ins.then_inc(s.v, 1)

                def rest(a):
                    dve.wait_ge(s.p1, l * PER["p1"] + a + 1)
                    dve.tensor_tensor(qkr, qk32, qks[:, 0], ALU.subtract).then_inc(s.r, 1)

                def rest2(a):
                    dve.wait_ge(s.p2, l * PER["p2"] + a + 1)
                    dve.tensor_tensor(qks[:, 2], qkr, qks[:, 1], ALU.subtract).then_inc(s.p3, 1)

                def reduce(b, u):
                    dve.wait_ge(s.s_mm, l * PER["s_mm"] + SUNITS * b + u + 1)
                    n = 4 if u < 4 else 2
                    h = 4 * u if u < 4 else 2 * (u - 4)
                    dve.tensor_reduce(mmax[:, int(u >= 4), h:h + n], bank[2 + u % 2][:].rearrange(
                        "p (h k) -> p h k", h=n), AX.X, ALU.max).then_inc(s.red, 1)

                def minus_max(b):
                    dve.wait_ge(s.red, l * PER["red"] + S_FREE + SUNITS * (b + 1))
                    dve.wait_ge(s.mT_mm, l * PER["mT_mm"] + b)
                    dve.tensor_scalar(msp[:, :, 0, :], mmax, -1.0, None, ALU.mult).then_inc(s.mhi, 1)
                    dve.wait_ge(s.mhi, l * PER["mhi"] + b + 1)
                    dve.scalar_tensor_tensor(out=msp[:, :, 1, :], in0=mmax, scalar=-1.0, in1=msp[:, :, 0, :],
                                             op0=ALU.mult, op1=ALU.subtract).then_inc(s.msp, 1)

                def normalize(d1):
                    for t in range(TPB):
                        dve.wait_ge(s.oTT, l * PER["oTT"] + TPB * (d1 - 1) + t + 1)
                        v = bank[t][:].rearrange("p (h s) -> p h s", h=H)
                        dve.reciprocal(orec[:, t, :], v[:, :, HD]).then_inc(s.rec, 1)
                    for t in range(TPB):
                        v = bank[t][:].rearrange("p (h s) -> p h s", h=H)
                        dve.wait_ge(s.rec, l * PER["rec"] + TPB * (d1 - 1) + t + 1)
                        dve.tensor_tensor(onorm[:, t, :].rearrange("p (h d) -> p h d", h=H), v[:, :, 0:HD],
                                          last(orec[:, t, :], HD), ALU.mult).then_inc(s.on, 1)

                def residual(d1):
                    dve.wait_ge(s.wo_mm, l * PER["wo_mm"] + d1)
                    dve.wait_ge(s.zb, l * PER["zb"] + (B if isinstance(d1, int) and d1 > B else d1))
                    zb = z[:, bass.ds(TPB * (d1 - 1 + 1) - TPB, TPB), :]
                    dve.tensor_tensor(zb, zb, bank[1][:, 0:S].rearrange("p (t d) -> p t d", t=TPB), ALU.add
                                      ).then_inc(s.z, 1)

                def step(b, k, more_a, more_b):
                    if more_a:
                        norm(b + 2)
                    if more_b:
                        for u in range(0, 4):
                            reduce(b + 1, u)
                    if more_a:
                        if k is not None:
                            dve.wait_ge(s.av, l * PER["av"] + NG * b + PROB_FREE)
                        project(b + 2, (k + 2) % RING)
                        rest(b + 2)
                    normalize(b + 1)
                    if more_b:
                        for u in range(4, 6):
                            reduce(b + 1, u)
                    if more_a:
                        rest2(b + 2)
                    if more_b:
                        for u in range(6, SUNITS):
                            reduce(b + 1, u)
                        minus_max(b + 1)
                    residual(b + 1)

                dve.wait_ge(s.vinit, l * PER["vinit"] + 3)
                norm(0)
                project(0, 0)
                rest(0)
                rest2(0)
                norm(1)
                project(1, 1)
                rest(1)
                rest2(1)
                for u in range(SUNITS):
                    reduce(0, u)
                minus_max(0)
                with dve.Fori(0, (B - 2) // RING) as i:
                    for k in range(RING):
                        step(RING * i + k, k, True, True)
                step(B - 2, (B - 2) % RING, False, True)
                step(B - 1, (B - 1) % RING, False, False)
                normalize(B + 1)
                residual(B + 1)
                dve.wait_ge(s.z, l * PER["z"] + BANK_FREE + B + 1)

            attention(0)
            layer_norm(prep[1])
            prepare(1)
            token_moe(1)
            for j in range(NBLK):
                dve.wait_ge(g.back_mm, j + 1)
                v = z[:, TPB + TB * j:TPB + TB * (j + 1), :]
                dve.tensor_tensor(v, v, bank[j][:].rearrange("p (t o) -> p t o", t=TB), ALU.add).then_inc(g.back, 1)
            dve.wait_ge(g.back, NBLK)
            attention(1)
            layer_norm(prep[2])

            s = prep[2]
            dve.wait_ge(s.hT, NBLK)
            line(dve.tensor_reduce(hmean, hT[:].rearrange("p (b t) -> p b t", b=B), AX.X, ALU.add))
            dve.tensor_scalar(hmean, hmean, 1.0 / S, None, ALU.mult).then_inc(q.mean, 1)
            dve.wait_ge(s.logits, 1)
            route(s, B, 1, bank[2][0:B, 0:E].rearrange("p (t e) -> p t e", t=1), row("gate_b1", B))
            dve.tensor_tensor(diag[0:B], last(ident[0:B, 0:B], 2),
                              pair[0:B, 2:4, 0].rearrange("p (a k) -> p a k", a=1).to_broadcast([B, B, 2]), ALU.mult
                              ).then_inc(q.cw_in, 1)
            dve.sem_inc(q.ug, 2)
            dve.wait_ge(q.cw, 1)

            def scale6(i, k):
                n = 4 * i + k
                b = 2 * i + k // 2
                dve.wait_ge(q.gel, GEL_FREE + 2 * n + 2)
                dve.wait_ge(q.y, n + 3)
                dve.tensor_scalar(ug[:, k % 2], gel[:, k % 2], cw[:, bass.ds(b, 1), k % 2], None, ALU.mult
                                  ).then_inc(q.ug, 1)

            dve.wait_ge(q.b2, 1)
            with dve.Fori(0, B // 2) as i:
                for k in range(4):
                    scale6(i, k)
                    if k % 2:
                        b = 2 * i + k // 2
                        dve.wait_ge(q.y, 4 + 2 * b + 2)
                        dve.scalar_tensor_tensor(out=yx[:, k // 2, :], in0=bank[4 + k // 2][:, 0:S],
                                                 scalar=b2s[:, bass.ds(b, 1)], in1=xTs[:, bass.ds(S * b, S)],
                                                 op0=ALU.add, op1=ALU.add).then_inc(q.yx, 1)
                        dve.wait_ge(q.t, b + 1)
                        dve.tensor_tensor(oseq_at(b), z[:, bass.ds(TPB * (b + 1), TPB), :],
                                          bank[6 + k // 2][:, 0:S].rearrange("p (t d) -> p t d", t=TPB), ALU.add
                                          ).then_inc(q.o, 1)

        @block.tensor
        def _(pe):
            pe.wait_ge(g.bsw, 1)
            pe.wait_ge(g.ld_lora, 16 * 5)
            for j in range(2):
                pe.matmul(bank[j][:], As_sb, bsw[:, 4 * j:4 * j + 4, :].rearrange("p b o -> p (b o)"), start=True,
                          stop=True).then_inc(g.weff_mm, 1)
            for t in range(NT):
                b = t // TPB
                if b % 4 == 0:
                    pe.wait_ge(g.weff_ok, b // 4 + 1)
                mm = pe.matmul(bank[2 + t // TB][:, (t % TB) * P:(t % TB + 1) * P], xTs[:, t * P:(t + 1) * P],
                               weff[:, b, :], start=True, stop=True)
                if t % TB == TB - 1:
                    mm.then_inc(g.h0_mm, 1)
            pe.wait_ge(g.ident, 3)
            pe.wait_ge(g.ld_rest, 16 * 5)

            def transposes(s):
                for j in range(NBLK):
                    pe.wait_ge(s.hn, j + 1)
                    if j >= 2:
                        pe.wait_ge(s.hT, j - 1)
                    for t in range(TB):
                        mm = pe.transpose(bank[j % 2][:, t * P:(t + 1) * P], hn[:, TB * j + t, :], ident[:])
                    mm.then_inc(s.tr, 1)

            def prepare(m):
                s = prep[m]
                transposes(s)
                for t in range(NT):
                    if t % TB == 0:
                        pe.wait_ge(s.hT, t // TB + 1)
                    mm = pe.matmul(bank[2][:, t * E:(t + 1) * E], hT[:, t * P:(t + 1) * P], gate_sb[:, m, :],
                                   start=True, stop=True)
                mm.then_inc(s.logits, 1)
                pe.wait_ge(s.we, 1)
                pe.transpose(bank[3][:, 0:P], we[:].rearrange("p e t -> p (e t)"), ident[:]).then_inc(s.weT_mm, 1)

            def token_moe(m):
                s = moe[m]
                n_a = 2 if m == 0 else 4
                pe.sem_inc(s.y, U_FREE)
                pe.wait_ge(prep[m].load, 16)
                pe.wait_ge(prep[m].lo, NBLK)
                for j in range(NBLK):
                    pe.matmul(bank[4 + j][:], b2_sb[:, m, :], weT8[:, j * BLK:(j + 1) * BLK], start=True, stop=False,
                              skip_group_check=True)

                def three(dst, w, x, sl, start, done=None):
                    pe.matmul(dst, w[0], x[0], start=start, stop=False, skip_group_check=True)
                    pe.matmul(dst, w[0], x[1], start=False, stop=False, skip_group_check=True)
                    pe.matmul(dst, w[1], x[0], start=False, stop=True, skip_group_check=True).then_inc(done, 1)

                def first(i, kk):
                    k = 2 * EC * i + kk
                    e, blk, c = kk // EC, kk % EC // FC, kk % FC
                    if kk % EC == 0:
                        pe.wait_ge(s.split, 12 + 6 * (2 * i + e + 1))
                    tok, f = slice(blk * BLK, (blk + 1) * BLK), slice(c * P, (c + 1) * P)
                    x = hT_hi[:, tok], hT_lo[:, tok]
                    if not isinstance(k, int) or k >= n_a:
                        pe.wait_ge(s.act, k - n_a + 1)
                    three(bank[kk % n_a][:], (whi[:, e, 0, f], wlo[:, e, 0, f]), x, None, True, s.a)
                    if m == 0:
                        pe.wait_ge(s.gate, ACT_FREE + k - 1)
                        three(bank[2 + kk % 2][:], (whi[:, e, 1, f], wlo[:, e, 1, f]), x, None, True, s.b)

                def second(i, kk):
                    k = 2 * EC * i + kk
                    e, blk, c = kk // EC, kk % EC // FC, kk % FC
                    d = slice(c * D, (c + 1) * D)
                    pe.wait_ge(s.lo, U32_FREE + k + 1)
                    three(bank[4 + blk][:], (whi[:, e, 2, d], wlo[:, e, 2, d]),
                          (u_hi[:, kk % U_FREE, :], u_lo[:, kk % U_FREE, :]), None, False, s.y)

                lead = 3

                def body(i, last_pair):
                    for kk in range(2 * EC):
                        nk = kk + lead
                        if nk < 2 * EC:
                            first(i, nk)
                        elif not last_pair:
                            first(i + 1, nk - 2 * EC)
                        second(i, kk)

                for kk in range(lead):
                    first(0, kk)
                with pe.Fori(0, E // 2 - 1) as i:
                    body(i, False)
                body(E // 2 - 1, True)

            prepare(0)
            token_moe(0)
            for t in range(NT):
                if t % TB == 0:
                    pe.wait_ge(g.x1, t // TB + 1)
                if t == 0:
                    pe.wait_ge(g.mix, B * E)
                mm = pe.matmul(bank[t // TB][:, (t % TB) * P:(t % TB + 1) * P], xTs[:, t * P:(t + 1) * P],
                               weff[:, t // TPB, :], start=True, stop=True)
                if t % TB == TB - 1:
                    mm.then_inc(g.z_mm, 1)

            def attention(l):
                s = att
                pe.wait_ge(g.masks, 5)
                pe.wait_ge(g.pad, 4)
                pe.wait_ge(s.vinit, l * PER["vinit"] + 3)
                if l == 0:
                    pe.sem_inc(s.av, PROB_FREE)

                def norm_T(a):
                    pe.wait_ge(s.zn, l * PER["zn"] + a + 1)
                    for t in range(TPB):
                        mm = pe.transpose(bank[0][:, t * P:(t + 1) * P], zn[:, t, :], ident[:])
                    mm.then_inc(s.zT_mm, 1)

                def project(a):
                    pe.wait_ge(s.zT, l * PER["zT"] + a + 1)
                    pe.matmul(bank[0][:, 0:S], att_w[:, l, 0, :], zT, start=True, stop=True)
                    pe.matmul(bank[0][:, S:2 * S], att_w[:, l, 1, :], zT, start=True, stop=True).then_inc(s.qk_mm, 1)
                    for t in range(TPB):
                        mm = pe.matmul(bank[1][:, t * P:(t + 1) * P], zT[:, t * P:(t + 1) * P], att_w[:, l, 2, :],
                                       start=True, stop=True)
                    mm.then_inc(s.v_mm, 1)

                def scores(b, r, u):
                    pe.wait_ge(s.red, l * PER["red"] + SUNITS * b + u + 1)
                    if u == 0:
                        pe.wait_ge(s.qk_ld, l * PER["qk_ld"] + 16 * QK_LOADS * (b + 1))
                        pe.wait_ge(s.mT, l * PER["mT"] + b)
                    t = int(u >= 4)
                    n = 4 if u < 4 else 2
                    h0 = 4 * u if u < 4 else 2 * (u - 4)
                    keys = BLK // n
                    dst = bank[2 + u % 2]
                    pe.matmul(dst[:].rearrange("p (h k) -> p h k", h=n), ident_bf[:],
                              mid(mask_q[:, 2 * P - keys:2 * P], n), start=True, stop=False, skip_group_check=True)
                    for j in range(n):
                        h = (h0 + j) * S
                        mm = pe.matmul(dst[:, j * keys:(j + 1) * keys], qp[:, r, h + t * P:h + (t + 1) * P],
                                       kp[:, r, h:h + keys], start=False, stop=True, skip_group_check=True)
                    mm.then_inc(s.s_mm, 1)

                def scores_T(b, r, gr):
                    if gr == 0:
                        pe.wait_ge(s.m_ld, l * PER["m_ld"] + 16 * MROWS * (b + 1))
                    for t in range(3):
                        pe.wait_ge(s.exp, l * PER["exp"] + SUNITS * b + 3 * gr + t + 1)
                        n = 2 if t < 2 else 4
                        kt = int(t == 2)
                        keys, width = slice(kt * P, (kt + 1) * P), BLK // n
                        dst = bank[4 + t]
                        pe.matmul(dst[:].rearrange("p (h k) -> p h k", h=n), ident_bf[:], mid(mask_k[:, 0:width], n),
                                  start=True, stop=False, skip_group_check=True)
                        for j in range(n):
                            h = (HG * gr + (2 * t + j if t < 2 else j)) * S
                            mm = pe.matmul(dst[:, j * width:(j + 1) * width], kp[:, r, h + kt * P:h + (kt + 1) * P],
                                           qp[:, r, h + kt * P:h + S], start=False, stop=True,
                                           skip_group_check=True)
                        mm.then_inc(s.t_mm, 1)

                def attend(b, r, gr):
                    pe.wait_ge(s.exp, l * PER["exp"] + T_FREE + SUNITS * b + 3 * gr + 3)
                    pe.wait_ge(s.v, l * PER["v"] + b + 1)
                    if gr % 2 == 0:
                        pe.wait_ge(s.oT, l * PER["oT"] + OT_FREE + 2 * b + gr // 2)
                    for j in range(HG):
                        pe.matmul(bank[7][SLOT * j:SLOT * (j + 1), (gr % 2) * S:(gr % 2 + 1) * S],
                                  vaug[:, r, 0, HG * gr + j, :], prob[:, gr % 2, j * S:(j + 1) * S], start=True,
                                  stop=False, skip_group_check=True)
                    for j in range(HG):
                        mm = pe.matmul(bank[7][SLOT * j:SLOT * (j + 1), (gr % 2) * S + P:(gr % 2 + 1) * S],
                                       vaug[:, r, 1, HG * gr + j, :],
                                       prob[:, gr % 2, 2 * BLK + j * P:2 * BLK + (j + 1) * P], start=False, stop=True,
                                       skip_group_check=True)
                    mm.then_inc(s.av, 1)

                def attended_T(d1, n_a):
                    pe.wait_ge(s.oT, l * PER["oT"] + OT_FREE + 2 * (d1 - 1))
                    pe.wait_ge(s.onT, l * PER["onT"] + BANK_FREE + d1 - 1)
                    pe.wait_ge(s.z, l * PER["z"] + BANK_FREE + d1 - 1)
                    pe.wait_ge(s.qk, l * PER["qk"] + n_a)
                    pe.wait_ge(s.v, l * PER["v"] + n_a)
                    for t in range(TPB):
                        for gr in range(NG):
                            mm = pe.transpose(bank[t][:, gr * P:(gr + 1) * P], oT[:, gr, t * P:(t + 1) * P], ident[:])
                        mm.then_inc(s.oTT, 1)

                def normal_T(d1):
                    pe.wait_ge(s.on, l * PER["on"] + TPB * d1)
                    for t in range(TPB):
                        mm = pe.transpose(bank[0][:, t * P:(t + 1) * P], onorm[:, t, :], ident[:])
                    mm.then_inc(s.on_mm, 1)

                def output(d1):
                    pe.wait_ge(s.onT, l * PER["onT"] + BANK_FREE + d1)
                    for t in range(TPB):
                        mm = pe.matmul(bank[1][:, t * P:(t + 1) * P], onT[:, t * P:(t + 1) * P], att_w[:, l, 3, :],
                                       start=True, stop=True)
                    mm.then_inc(s.wo_mm, 1)

                def maxima_T(b):
                    pe.wait_ge(s.msp, l * PER["msp"] + b + 1)
                    for t in range(TPB):
                        mm = pe.transpose(bank[2][0:MROWS * H, 0:P].bitcast(BF16)[:, t * P:(t + 1) * P],
                                          msp[:, t].rearrange("p r h -> p (r h)"), ident_bf[:])
                    mm.then_inc(s.mT_mm, 1)

                def step(b, k, more_a, more_b):
                    r, r1 = k % RING, (k + 1) % RING
                    if more_b:
                        scores(b + 1, r1, 0)
                        scores(b + 1, r1, 1)
                    if more_a:
                        pe.wait_ge(s.onT, l * PER["onT"] + BANK_FREE + b)
                        norm_T(b + 2)
                    if more_b:
                        scores(b + 1, r1, 2)
                        scores(b + 1, r1, 3)
                    if more_a:
                        pe.wait_ge(s.z, l * PER["z"] + BANK_FREE + b)
                        project(b + 2)
                    scores_T(b, r, 0)
                    attended_T(b + 1, b + 3 if more_a else B)
                    if more_b:
                        for u in range(4, 8):
                            scores(b + 1, r1, u)
                    scores_T(b, r, 1)
                    normal_T(b + 1)
                    attend(b, r, 0)
                    if more_b:
                        for u in range(8, SUNITS):
                            scores(b + 1, r1, u)
                        maxima_T(b + 1)
                    output(b + 1)
                    scores_T(b, r, 2)
                    attend(b, r, 1)
                    scores_T(b, r, 3)
                    attend(b, r, 2)
                    attend(b, r, 3)

                for a in range(2):
                    norm_T(a)
                    project(a)
                for u in range(SUNITS):
                    scores(0, 0, u)
                maxima_T(0)
                with pe.Fori(0, (B - 2) // RING) as i:
                    for k in range(RING):
                        step(RING * i + k, k, True, True)
                step(B - 2, (B - 2) % RING, False, True)
                step(B - 1, (B - 1) % RING, False, False)
                attended_T(B + 1, B)
                normal_T(B + 1)
                output(B + 1)

            attention(0)
            prepare(1)
            token_moe(1)
            for t in range(NT):
                if t % TB == 0:
                    pe.wait_ge(moe[1].yT, t // TB + 1)
                mm = pe.transpose(bank[t // TB][:, (t % TB) * P:(t % TB + 1) * P], hT[:, t * P:(t + 1) * P], ident[:])
                if t % TB == TB - 1:
                    mm.then_inc(g.back_mm, 1)
            pe.wait_ge(g.back, NBLK)
            attention(1)

            s = prep[2]
            transposes(s)
            pe.wait_ge(q.mean, 1)
            pe.matmul(bank[2][0:B, 0:E], hmean, gate_sb[:, 2, :], start=True, stop=True).then_inc(s.logits, 1)
            pe.wait_ge(q.ones, 1)
            pe.wait_ge(q.cw_in, 1)
            pe.matmul(bank[2][:, 0:2 * B], ones8[0:B, :], diag[0:B].rearrange("p b k -> p (b k)"), start=True,
                      stop=True).then_inc(q.cw_mm, 1)
            pe.transpose(bank[3][0:E, 0:B], we[0:B, :, 0], ident[0:B, 0:B]).then_inc(q.weT_mm, 1)
            pe.wait_ge(q.weT, 1)
            pe.matmul(bank[3][:, 0:B], b2_sb[:, 2, :], weT[0:E, 0:B], start=True, stop=True).then_inc(q.b2_mm, 1)
            pe.wait_ge(q.b2, 1)
            pe.sem_inc(q.y, 4)

            def first6(i, k):
                n = 4 * i + k
                pe.wait_ge(q_w[k], 48 * (i + 1))
                pe.wait_ge(q.gel, GEL_FREE + 2 * n - 2)
                tok = hT[:, bass.ds(S * (2 * i + k // 2), S)]
                for c in range(FC):
                    mm = pe.matmul(bank[2 * (k % 2) + c // 2][:, (c % 2) * S:(c % 2 + 1) * S],
                                   w1s[:, k, c * P:(c + 1) * P], tok, start=True, stop=True)
                    if c % 2:
                        mm.then_inc(q.a, 1)

            def second6(i, k):
                n = 4 * i + k
                pe.wait_ge(q.ug, n + 3)
                for c in range(FC):
                    mm = pe.matmul(bank[4 + k // 2][:, 0:S], w2s[:, k, c, :], ug[:, k % 2, c, :],
                                   start=(k % 2 == 0 and c == 0), stop=(k % 2 == 1 and c == FC - 1))
                mm.then_inc(q.y, 1)

            def body6(i, last_two):
                for k in range(4):
                    if k < 3:
                        first6(i, k + 1)
                    elif not last_two:
                        first6(i + 1, 0)
                    second6(i, k)
                    if k % 2:
                        pe.wait_ge(q.yx, 2 * i + k // 2 + 1)
                        for t in range(TPB):
                            mm = pe.transpose(bank[6 + k // 2][:, t * P:(t + 1) * P], yx[:, k // 2, t * P:(t + 1) * P],
                                              ident[:])
                        mm.then_inc(q.t, 1)

            first6(0, 0)
            with pe.Fori(0, B // 2 - 1) as i:
                body6(i, False)
            body6(B // 2 - 1, True)


def kernel(x, cond_8, L0_cond_W_base, L0_cond_b_base, L0_cond_As, L0_cond_Bs, L0_ffn_ln_w, L0_ffn_Wg, L0_ffn_bg,
           L0_ffn_W1a, L0_ffn_b1a, L0_ffn_W1b, L0_ffn_b1b, L0_ffn_W2, L0_ffn_b2, L1_cond_weight, L1_cond_mask,
           L1_cond_bias, L1_ffn_ln1_w, L1_ffn_ln1_b, L1_ffn_ln2_w, L1_ffn_ln2_b, L1_ffn_wq, L1_ffn_wk, L1_ffn_wv,
           L1_ffn_wo, L1_ffn_bq, L1_ffn_bk, L1_ffn_bv, L1_ffn_bo, L1_ffn_gate_w, L1_ffn_gate_b, L1_ffn_e_w1,
           L1_ffn_e_b1, L1_ffn_e_w2, L1_ffn_e_b2):
    import numpy as _np
    import concourse.bacc as _bacc
    from concourse import mybir as _mybir
    from concourse.bass_utils import run_bass_kernel_spmd as _run

    def npa(a):
        return _np.asarray(a)

    def dim_major(w):
        w = npa(w)
        return w.reshape(w.shape[:-1] + (H, HD)).swapaxes(-1, -2).reshape(w.shape)

    def chunks(b):
        return npa(b).reshape(-1, P).T

    cols = _np.concatenate([npa(L0_ffn_ln_w).reshape(D, 1), npa(L1_ffn_ln1_w).T, npa(L1_ffn_ln1_b).T,
                            npa(L1_ffn_ln2_w).T, npa(L1_ffn_ln2_b).T, dim_major(L1_ffn_bq).T, dim_major(L1_ffn_bk).T,
                            chunks(L0_ffn_b1a), chunks(L0_ffn_b1b), chunks(npa(L1_ffn_e_b1)[0])], axis=1)
    rows = _np.concatenate([npa(v).reshape(-1) for v in (
        L0_cond_b_base, L1_cond_bias, L0_ffn_bg, L1_ffn_gate_b, L1_ffn_bv, L1_ffn_bo, cond_8,
        _np.arange(E, dtype=_np.float32))]).reshape(1, -1)
    arrays = {
        "xT": npa(x).reshape(N, D).T,
        "As": npa(L0_cond_As).reshape(P, D),
        "BsT": npa(L0_cond_Bs).transpose(0, 2, 1).reshape(P, D),
        "WbT": npa(L0_cond_W_base).T,
        "w_er": _np.repeat(npa(cond_8).T, P // E, axis=0),
        "cols": cols,
        "rows": rows,
        "Wg": _np.stack([npa(L0_ffn_Wg), npa(L1_ffn_gate_w)[0], npa(L1_ffn_gate_w)[1]], axis=1),
        "W1a": npa(L0_ffn_W1a), "W1b": npa(L0_ffn_W1b), "W2": npa(L0_ffn_W2),
        "b2": _np.stack([npa(L0_ffn_b2), npa(L1_ffn_e_b2)[0], npa(L1_ffn_e_b2)[1]], axis=1),
        "WT": npa(L1_cond_weight).transpose(2, 0, 1),
        "maskT": npa(L1_cond_mask).T,
        "att_w": _np.stack([dim_major(L1_ffn_wq), dim_major(L1_ffn_wk), npa(L1_ffn_wv), npa(L1_ffn_wo)],
                           axis=1).transpose(2, 0, 1, 3),
        "e_w1": npa(L1_ffn_e_w1), "e_w2": npa(L1_ffn_e_w2),
        "e_b1s": npa(L1_ffn_e_b1)[1].reshape(E, FC, P).transpose(0, 2, 1),
    }
    nc = _bacc.Bacc("TRN2", target_bir_lowering=False, num_devices=1)
    feeds, args = {}, []
    for name, a in arrays.items():
        a = _np.ascontiguousarray(a)
        feeds[f"in_{name}"] = a
        args.append(nc.dram_tensor(f"in_{name}", a.shape, _mybir.dt.from_np(a.dtype), kind="ExternalInput").ap())
    args.append(nc.dram_tensor("out_0", (B, S, D), F32, kind="ExternalOutput").ap())
    build(nc, *args)
    r = _run(nc, [feeds], core_ids=[0])
    return r.results[0]["out_0"]
```

```python
from contextlib import ExitStack

import numpy as np

import concourse.bass as bass
from concourse import mybir

F32 = mybir.dt.float32
F32R = mybir.dt.float32r
BF16 = mybir.dt.bfloat16
U32 = mybir.dt.uint32
ALU = mybir.AluOpType
ACT = mybir.ActivationFunctionType
AX = mybir.AxisListType

B, S, D = 8, 256, 128
P = 128
N = B * S
NT = N // P
TPB = S // P
BLK = 512
NBLK = N // BLK
TB = BLK // P
E = 8
F = 512
FC = F // P
EC = NBLK * FC
CH = E * EC
H, HD = 16, 8
L = 2
HG = 4
NG = H // HG
SLOT = 32
LORA_SCALE = 2.0
RMS_EPS = float(np.finfo(np.float32).eps)
LN_EPS = 1e-5
ATT_SCALE = HD ** -0.5
NEG = -1e30
PARTS = 3
ROW_OF = [0, 3 * HD, 5 * HD]
MROW = 6 * HD
MROWS = 2
RING = 3
QK_LOADS = 2 * PARTS + 1
SUNITS = 12
T_FREE = 3
S_FREE = 2
PROB_FREE = 2
OT_FREE = 2
BANK_FREE = 1
GEL_FREE = 4
U_FREE = 4
ACT_FREE = 4
A_FREE = 4
PRODUCT_FREE = 2
U32_FREE = 4


def lay(items):
    table, at = {}, 0
    for name, n in items:
        table[name] = (at, at + n)
        at += n
    return table, at


COL, NCOL = lay([("ln_w", 1), ("ln1_w", L), ("ln1_b", L), ("ln2_w", L), ("ln2_b", L), ("bq", L), ("bk", L),
                 ("b1a", E * FC), ("b1b", E * FC), ("e_b1", E * FC)])
ROW, NROW = lay([("b_base", D), ("bias", D), ("bg", E), ("gate_b0", E), ("gate_b1", E), ("bv0", D), ("bv1", D),
                 ("bo0", D), ("bo1", D), ("cond", B * E), ("iota", E)])


class Signals:

    def __init__(self, sem, tag, names):
        self.all = {n: sem(f"{tag}_{n}") for n in names.split()}

    def __getattr__(self, name):
        return self.all[name]


def build(nc, xT, As, BsT, WbT, w_er, cols_in, rows_in, Wg, W1a, W1b, W2, b2, WT, maskT,
          att_in, e_w1, e_w2, e_b1s, out):
    we_dram = [nc.dram_tensor(f"we_dram{m}", [E, N], F32, kind="Internal").ap() for m in range(2)]
    qk_dram = nc.dram_tensor("qk_dram", [PARTS, 2, HD, H * S], BF16, kind="Internal").ap()
    ids_dram = nc.dram_tensor("ids_dram", [B, 2], U32, kind="Internal").ap()

    with ExitStack() as ctx:
        def sb(name, shape, dt=F32):
            return ctx.enter_context(nc.sbuf_tensor(name, shape, dt))

        def sem(name):
            return ctx.enter_context(nc.semaphore(name))

        bank = [ctx.enter_context(nc.psum_tensor(f"bank{i}", [P, BLK], F32)) for i in range(8)]

        xTs = sb("xTs", [P, N])
        z = sb("z", [P, TPB + NT, D])
        hn = sb("hn", [P, NT, D])
        hT = sb("hT", [P, N])
        hT_hi = sb("hT_hi", [P, N], F32R)
        hT_lo = sb("hT_lo", [P, N], F32R)
        cols = sb("cols", [P, NCOL])
        rows = sb("rows", [P, NROW])
        ident = sb("ident", [P, P])
        ident_bf = sb("ident_bf", [P, P], BF16)
        mask_q = sb("mask_q", [P, P], BF16)
        mask_k = sb("mask_k", [P, P], BF16)
        weff = sb("weff", [P, B, D])
        stat = sb("stat", [P, NT, 6])
        mv = sb("mv", [P, NT, 2])
        var = sb("var", [P, NT])
        rstd = sb("rstd", [P, NT])
        half = sb("half", [P, NT])
        logit = sb("logit", [P, NT, E])
        top_v = sb("top_v", [P, NT, 8])
        top_i = sb("top_i", [P, NT, 8], U32)
        top_f = sb("top_f", [P, NT, 2])
        pair = sb("pair", [P, 4, NT])
        we = sb("we", [P, E, NT])
        onehot = sb("onehot", [P, E, NT])
        weT = sb("weT", [P, P])
        gate_sb = sb("gate_sb", [P, 3, E])
        b2_sb = sb("b2_sb", [E, 3, D])
        att_w = sb("att_w", [P, L, 4, D])
        whi = sb("whi", [P, 2, 3, F], F32R)
        wlo = sb("wlo", [P, 2, 3, F], F32R)
        bias1 = sb("bias1", [P, 2, 2, FC])
        u_hi = sb("u_hi", [P, U_FREE, BLK], F32R)
        u_lo = sb("u_lo", [P, U_FREE, BLK], F32R)
        qp = sb("qp", [P, RING, H * S], BF16)
        kp = sb("kp", [P, RING, H * S], BF16)
        mT = sb("mT", [MROWS * H, S], BF16)
        ids = sb("ids", [1, B * 2], U32)
        weT8 = hn[0:E, :, :].rearrange("p t d -> p (t d)")

        arena = sb("arena", [P, 12288])

        def views(items):
            got, at = [], 0
            for shape, dt in items:
                n = int(np.prod(shape)) * (2 if dt == BF16 else 4) // 4
                v = arena[:, at:at + n]
                at += n
                v = v.bitcast(BF16) if dt == BF16 else v
                if len(shape) == 2:
                    v = v.rearrange("p (a b) -> p a b", a=shape[0])
                elif len(shape) == 3:
                    v = v.rearrange("p (a b c) -> p a b c", a=shape[0], b=shape[1])
                elif len(shape) == 4:
                    v = v.rearrange("p (a b c d) -> p a b c d", a=shape[0], b=shape[1], c=shape[2])
                got.append(v)
            assert at <= arena.shape[1], at
            return got

        wraw, wbc, act_s, gated, u32 = views([([2, 3, F], F32), ([2, N], F32), ([4, BLK], F32), ([2, BLK], F32),
                                              ([U32_FREE, BLK], F32)])
        product = gated
        y_sum = u32
        (prob, vaug, oT, qk32, qkr, qks, onorm, onT, orec, mmax, msp) = views([
            ([2, 3 * BLK], F32), ([RING, TPB, H, SLOT], F32), ([NG, S], F32), ([2, S], F32), ([2, S], F32),
            ([PARTS, 2, S], BF16), ([TPB, D], F32), ([S], F32), ([TPB, H], F32),
            ([TPB, H], F32), ([TPB, MROWS, H], BF16)])
        w1s, w2s, b1s, gel, ug, yx, oseq, cw, diag, ones8, b2s, hmean = views([
            ([4, F], F32), ([4, FC, D], F32), ([4, FC], F32), ([2, FC, S], F32), ([2, FC, S], F32), ([2, S], F32),
            ([B, TPB, D], F32), ([B, 2], F32), ([B, 2], F32), ([P], F32), ([B], F32), ([B], F32)])
        start = z[:, TPB:, :].rearrange("p t d -> p (t d)")
        wt = start[:, 0:B * D].rearrange("p (g o) -> p g o", g=E)
        As_sb, BsT_sb, WbT_sb, maskT_sb = (start[:, (8 + n) * D:(9 + n) * D] for n in range(4))
        bsw = arena[:, 0:B * D].rearrange("p (b o) -> p b o", b=B)
        wer = arena[:, B * D:B * D + B]
        square = arena[:, 2 * B * D:2 * B * D + D]
        x_all = hn[:].rearrange("p t d -> p (t d)")

        def oseq_at(b):
            return oseq[:, bass.ds(b, 1)].rearrange("p a t d -> p (a t) d")

        def col(name, i=0):
            a = COL[name][0] + i
            return cols[:, a:a + 1]

        def row(name, n=P):
            a, b = ROW[name]
            return rows[0:n, a:b]

        def mid(v, n):
            return v.rearrange("p (a d) -> p a d", a=1).to_broadcast([v.shape[0], n, v.shape[1]])

        def last(v, n):
            return v.unsqueeze(2).to_broadcast([v.shape[0], v.shape[1], n])

        g = Signals(sem, "g", "ld_lora ld_vec ld_rest ident masks ones bsw weff_mm weff_ok h0_mm h0_ok sq ms rms "
                    "line mixmask mix x1 z_mm z_ok back_mm back pad carry_sp carry_dve")
        prep = [Signals(sem, f"p{m}", "hn tr hT logits diff exp we var rstd" +
                        (" hi lo weT_mm weT store load" if m < 2 else "")) for m in range(3)]
        norm1 = [Signals(sem, f"n{l}", "hn tr hT var rstd") for l in range(L)]
        moe = [Signals(sem, f"x{m}", "split a b act gate scaled hi lo y init sum") for m in range(2)]
        PER = {}
        PER.update({n: B for n in "qk_mm qk vr p1 r p2 p3 mhi msp mT_mm mT".split()})
        PER.update({n: NBLK for n in "zb v_mm v".split()})
        PER.update({n: SUNITS * B for n in "s_mm red t_mm exp".split()})
        PER.update({n: TPB * (B + 1) for n in "oTT rec on".split()})
        PER.update({n: B + 1 for n in "on_mm onT wo_mm z".split()})
        PER.update(vinit=3, av=NG * B, oT=2 * B, qk_st=16 * B, qk_ld=16 * QK_LOADS * B, m_ld=16 * MROWS * B)
        att = Signals(sem, "a", " ".join(PER))
        q = Signals(sem, "q", "mean cw_in cw_mm cw b2_mm b2 a gel ug y yx t o store ids ids_ld weT weT_mm ones")
        w_ld = [sem(f"w_ld{n}") for n in range(2)]
        r_ld = [sem(f"r_ld{n}") for n in range(2)]
        q_w = [sem(f"q_w{n}") for n in range(4)]

        block = ctx.enter_context(nc.Block())

        def expert_dram(m):
            return ([W1a, W1b], W2) if m == 0 else ([e_w1[0]], e_w2[0])

        @block.sync
        def _(sp):
            for dst, src in ((xTs[:], xT), (As_sb, As), (BsT_sb, BsT), (WbT_sb, WbT), (wer, w_er)):
                sp.dma_start(dst, src).then_inc(g.ld_lora, 16)
            sp.dma_start(cols[:], cols_in).then_inc(g.ld_vec, 16)
            sp.dma_start(rows[:], rows_in.to_broadcast([P, NROW])).then_inc(g.ld_vec, 16)
            for dst, src in ((gate_sb[:], Wg), (b2_sb[:], b2), (wt, WT), (maskT_sb, maskT), (att_w[:], att_in)):
                sp.dma_start(dst, src).then_inc(g.ld_rest, 16)

            def prepare(m):
                s = prep[m]
                sp.wait_ge(s.weT, 1)
                sp.dma_start(we_dram[m].rearrange("e (t p) -> (e t) p", t=NT), weT[:]).then_inc(s.store, 16)
                sp.wait_ge(s.store, 16)
                sp.dma_start(weT8, we_dram[m]).then_inc(s.load, 16)

            def moe_loads(m):
                s = moe[m]
                firsts, second = expert_dram(m)
                second = second.rearrange("e (c p) d -> e p c d", p=P)
                with sp.Fori(0, E // 2) as i:
                    for k in range(2):
                        e = 2 * i + k
                        sp.wait_ge(s.split, 6 * e + 6)
                        sp.sem_inc(g.carry_sp, 1)
                        for n, w in enumerate(firsts):
                            sp.dma_start(wraw[:, k, n, :], w[e]).then_inc(w_ld[k], 16)
                        sp.dma_start(wraw[:, k, 2, :].rearrange("p (c d) -> p c d", c=FC),
                                     second[e]).then_inc(w_ld[k], 16)
                        used = EC if m == 0 else NBLK
                        sp.wait_ge(s.scaled, used * e + used)
                        sp.sem_inc(g.carry_sp, 1)
                        sp.dma_start(wbc[:, k, :], we_dram[m][bass.ds(e, 1), :].to_broadcast([P, N])
                                     ).then_inc(r_ld[k], 16)

            def attention(l):
                s = att

                def queries_keys(a, r):
                    sp.wait_ge(s.p3, l * PER["p3"] + a + 1)
                    sp.sem_inc(g.carry_sp, 1)
                    sp.wait_ge(s.qk_ld, l * PER["qk_ld"] + 16 * QK_LOADS * a)
                    sp.sem_inc(g.carry_sp, 1)
                    sp.dma_start(qk_dram.rearrange("n w d (h t) -> (d h) n w t", h=H), qks).then_inc(s.qk_st, 16)
                    sp.wait_ge(s.qk_st, l * PER["qk_st"] + 16 * (a + 1))
                    sp.sem_inc(g.carry_sp, 1)
                    for i in range(PARTS):
                        n = PARTS - i
                        to = slice(ROW_OF[i], ROW_OF[i] + HD * n)
                        part = qk_dram[i, 0].rearrange("(a d) x -> a d x", a=1).to_broadcast([n, HD, H * S])
                        sp.dma_start(qp[to, r, :], part).then_inc(s.qk_ld, 16)
                        sp.dma_start(kp[to, r, :], qk_dram[0:n, 1]).then_inc(s.qk_ld, 16)
                    sp.dma_start(qp[MROW:MROW + MROWS, r, :], qp[2 * 32:2 * 32 + MROWS, r, :]).then_inc(s.qk_ld, 16)

                def maxima(b, r):
                    sp.wait_ge(s.mT, l * PER["mT"] + b + 1)
                    sp.sem_inc(g.carry_sp, 1)
                    dst = qp[MROW:MROW + MROWS, r, :].rearrange("r (h t) -> r h t", h=H)
                    for n in range(MROWS):
                        sp.dma_start(dst[n:n + 1], mT[n * H:(n + 1) * H, :]).then_inc(s.m_ld, 16)

                queries_keys(0, 0)
                queries_keys(1, 1)
                maxima(0, 0)

                def step(b, k, more_a, more_b):
                    if more_a:
                        sp.wait_ge(s.exp, l * PER["exp"] + T_FREE + SUNITS * b)
                        sp.sem_inc(g.carry_sp, 1)
                        queries_keys(b + 2, (k + 2) % RING)
                    if more_b:
                        maxima(b + 1, (k + 1) % RING)

                with sp.Fori(0, (B - 2) // RING) as i:
                    for k in range(RING):
                        step(RING * i + k, k, True, True)
                step(B - 2, (B - 2) % RING, False, True)

            prepare(0)
            moe_loads(0)
            attention(0)
            prepare(1)
            moe_loads(1)
            attention(1)

            sp.wait_ge(prep[2].we, 1)
            sp.dma_start(ids_dram, top_i[0:B, 0, 0:2]).then_inc(q.ids, 16)
            sp.wait_ge(q.ids, 16)
            sp.dma_start(ids[:], ids_dram.rearrange("b k -> (b k)").rearrange("(a n) -> a n", a=1)
                         ).then_inc(q.ids_ld, 16)
            sp.wait_ge(q.ids_ld, 16)
            second = e_w2[1].rearrange("e (c p) d -> e p c d", p=P)
            def expert_loads(i, k):
                e = sp.value_load(ids[0:1, bass.ds(4 * i + k, 1)], min_val=0, max_val=E - 1)
                sp.wait_ge(q.y, 4 * i + k + 1)
                sp.sem_inc(g.carry_sp, 1)
                sp.dma_start(w1s[:, k, :], e_w1[1][bass.ds(e, 1), :, :].rearrange("a p f -> (a p) f")
                             ).then_inc(q_w[k], 16)
                sp.dma_start(w2s[:, k], second[bass.ds(e, 1)].rearrange("a p c d -> (a p) c d")
                             ).then_inc(q_w[k], 16)
                sp.dma_start(b1s[:, k, :], e_b1s[bass.ds(e, 1)].rearrange("a p c -> (a p) c")
                             ).then_inc(q_w[k], 16)

            def store(b):
                sp.wait_ge(q.o, b + 1)
                sp.sem_inc(g.carry_sp, 1)
                sp.dma_start(out[bass.ds(b, 1)].rearrange("a (t p) d -> p (a t) d", p=P), oseq_at(b)
                             ).then_inc(q.store, 16)

            for k in range(4):
                expert_loads(0, k)
            with sp.Fori(1, B // 2) as i:
                for k in range(4):
                    expert_loads(i, k)
                    if k % 2:
                        store(2 * i - 2 + k // 2)
            store(B - 2)
            store(B - 1)
            sp.wait_ge(q.store, 16 * B)

        @block.gpsimd
        def _(pool):
            pool.memset(ident[:], 0.0).then_inc(g.ident, 1)
            pool.wait_ge(g.ident, 1)
            pool.affine_select(out=ident[:], in_=ident[:], compare_op=ALU.not_equal, fill=1.0, base=0,
                               pattern=[[-1, P]], channel_multiplier=1).then_inc(g.ident, 1)
            pool.memset(half[:], -0.5).then_inc(g.masks, 1)
            pool.memset(mask_q[:], 0.0).then_inc(g.masks, 1)
            pool.memset(mask_k[:], 0.0).then_inc(g.masks, 1)
            pool.wait_ge(g.ident, 2)
            pool.tensor_copy(ident_bf[:], ident[:]).then_inc(g.ident, 1)
            pool.wait_ge(g.masks, 3)
            pool.affine_select(out=mask_q[:], in_=mask_q[:], compare_op=ALU.is_ge, fill=NEG,
                               base=0, pattern=[[-1, P]], channel_multiplier=1).then_inc(g.masks, 1)
            pool.affine_select(out=mask_k[:], in_=mask_k[:], compare_op=ALU.is_ge, fill=NEG,
                               base=0, pattern=[[1, P]], channel_multiplier=-1).then_inc(g.masks, 1)

            def power(before, after):
                pool.wait_ge(before, 1)
                pool.tensor_tensor(rstd[:], var[:], half[:], ALU.pow).then_inc(after, 1)

            power(g.ms, g.rms)
            pool.wait_ge(g.ld_rest, 16 * 5)
            pool.tensor_tensor(wt, wt, mid(maskT_sb, E), ALU.mult).then_inc(g.mixmask, 1)
            pool.memset(qp[:].bitcast(F32), 0.0).then_inc(g.pad, 1)
            pool.memset(kp[:].bitcast(F32), 0.0).then_inc(g.pad, 1)
            pool.wait_ge(g.pad, 2)
            pool.memset(kp[32:64, :, :], 1.0).then_inc(g.pad, 1)
            pool.wait_ge(g.pad, 3)
            pool.memset(z[:, 0:TPB, :], 0.0).then_inc(g.pad, 1)

            s = moe[0]
            pool.sem_inc(s.scaled, 2 * EC)
            with pool.Fori(0, E // 2) as i:
                for kk in range(2 * EC):
                    k = 2 * EC * i + kk
                    e, blk = kk // EC, kk % EC // FC
                    if kk % EC == 0:
                        pool.wait_ge(r_ld[e], 16 * (i + 1))
                    pool.wait_ge(s.gate, ACT_FREE + k + 1)
                    pool.wait_ge(s.lo, k + 1)
                    pool.tensor_tensor(u32[:, kk % U32_FREE, :], gated[:, kk % 2, :],
                                       wbc[:, e, blk * BLK:(blk + 1) * BLK], ALU.mult).then_inc(s.scaled, 1)

            def attention(l):
                s = att
                power(norm1[l].var, norm1[l].rstd)
                pool.wait_ge(moe[l].lo, U32_FREE + CH)
                if l:
                    pool.wait_ge(g.back_mm, NBLK)
                v = vaug.rearrange("p r k h s -> p (r k h) s")
                pool.memset(v, 0.0).then_inc(s.vinit, 1)
                pool.memset(oT.rearrange("p a b -> p (a b)"), 1.0).then_inc(s.vinit, 1)
                pool.wait_ge(s.vinit, l * PER["vinit"] + 2)
                pool.memset(v[:, :, HD:HD + 1], 1.0).then_inc(s.vinit, 1)

                for j in range(NBLK):
                    pool.wait_ge(norm1[l].hn, j + 1)
                    zb = z[:, TPB + TB * j:TPB + TB * (j + 1), :]
                    pool.tensor_tensor(zb, zb, mid(row(f"bo{l}"), TB), ALU.add).then_inc(s.zb, 1)

                def values(a, r):
                    for t in range(TPB):
                        cp = pool.tensor_copy(vaug[:, r, t, :, 0:HD], hn[:, bass.ds(TPB * a + t, 1), :].rearrange(
                            "p a (h d) -> p (a h) d", h=H))
                    cp.then_inc(s.vr, 1)

                pool.wait_ge(s.vinit, l * PER["vinit"] + 3)
                pool.wait_ge(s.v, (l + 1) * NBLK)
                values(0, 0)
                values(1, 1)
                with pool.Fori(0, (B - 2) // RING) as i:
                    for k in range(RING):
                        a = RING * i + 2 + k
                        pool.wait_ge(s.av, l * PER["av"] + PROB_FREE + NG * (RING * i + k))
                        values(a, (2 + k) % RING)

            attention(0)
            power(prep[1].var, prep[1].rstd)
            s = moe[1]
            pool.sem_inc(s.sum, PRODUCT_FREE)
            pool.wait_ge(s.init, NBLK)
            with pool.Fori(0, E // 2) as i:
                for kk in range(2 * NBLK):
                    k = 2 * NBLK * i + kk
                    pool.wait_ge(s.scaled, 2 * NBLK + k + 1)
                    pool.wait_ge(s.sum, PRODUCT_FREE + k)
                    acc = y_sum[:, kk % NBLK, :]
                    pool.tensor_tensor(acc, acc, product[:, kk % 2, :], ALU.add).then_inc(s.sum, 1)
            attention(1)
            power(prep[2].var, prep[2].rstd)
            pool.memset(ones8, 1.0).then_inc(q.ones, 1)

        @block.scalar
        def _(act):
            for t in range(NT):
                if t % TB == 0:
                    act.wait_ge(g.h0_ok, t // TB + 1)
                if t:
                    act.wait_ge(g.sq, t)
                act.activation(square, hn[:, t, :], ACT.Square, accum_out=stat[:, t, 0:1]).then_inc(g.sq, 1)

            def prepare(m, l_bias):
                s = prep[m]
                for j in range(NBLK):
                    act.wait_ge(s.tr, j + 1)
                    if m == 0:
                        act.activation(hT[:, j * BLK:(j + 1) * BLK], bank[j % 2][:], ACT.Copy,
                                       scale=col("ln_w")).then_inc(s.hT, 1)
                    else:
                        act.activation(hT[:, j * BLK:(j + 1) * BLK], bank[j % 2][:], ACT.Identity,
                                       bias=col("ln2_b", l_bias), scale=col("ln2_w", l_bias)).then_inc(s.hT, 1)
                n, c = (P, NT) if m < 2 else (B, 1)
                act.wait_ge(s.diff, 1)
                act.activation(pair[0:n, 1, 0:c], pair[0:n, 0, 0:c], ACT.Exp).then_inc(s.exp, 1)
                if m < 2:
                    act.wait_ge(s.weT_mm, 1)
                    act.activation(weT[:], bank[3][:, 0:P], ACT.Copy).then_inc(s.weT, 1)

            def token_moe_1():
                s = moe[1]
                act.sem_inc(s.act, A_FREE)
                for j in range(NBLK):
                    act.wait_ge(s.y, U_FREE + j + 1)
                    act.activation(y_sum[:, j, :], bank[4 + j][:], ACT.Copy).then_inc(s.init, 1)
                with act.Fori(0, E // 2) as i:
                    for kk in range(2 * EC):
                        k = 2 * EC * i + kk
                        e, c = kk // EC, kk % FC
                        act.wait_ge(s.a, k + 1)
                        act.wait_ge(s.lo, k + 1)
                        act.activation(act_s[:, kk % 4, :], bank[kk % 4][:], ACT.Gelu, bias=bias1[:, e, 0, c:c + 1])
                        act.wait_ge(s.y, NBLK + k + 1)
                        act.activation(u_hi[:, kk % U_FREE, :], bank[kk % 4][:], ACT.Gelu,
                                       bias=bias1[:, e, 0, c:c + 1]).then_inc(s.act, 1)

            def token_moe_0():
                s = moe[0]

                def nonlinear(i, kk):
                    k = 2 * EC * i + kk
                    e, c = kk // EC, kk % FC
                    act.wait_ge(s.a, k + 1)
                    act.wait_ge(s.gate, k + 1)
                    act.activation(act_s[:, kk % 4, :], bank[kk % 2][:], ACT.Silu,
                                   bias=bias1[:, e, 0, c:c + 1]).then_inc(s.act, 1)

                def high(i, kk):
                    k = 2 * EC * i + kk
                    act.wait_ge(s.scaled, 2 * EC + k + 1)
                    act.wait_ge(s.y, k + 1)
                    act.activation(u_hi[:, kk % U_FREE, :], u32[:, kk % U32_FREE, :], ACT.Copy).then_inc(s.hi, 1)

                def body(i, end):
                    for kk in range(2 * EC):
                        if kk + 2 < end:
                            if kk + 2 < 2 * EC:
                                nonlinear(i, kk + 2)
                            else:
                                nonlinear(i + 1, kk + 2 - 2 * EC)
                        high(i, kk)

                nonlinear(0, 0)
                nonlinear(0, 1)
                with act.Fori(0, E // 2 - 1) as i:
                    body(i, 2 * EC + 2)
                body(E // 2 - 1, 2 * EC)

            prepare(0, 0)
            token_moe_0()

            def attention(l):
                s = att

                for j in range(NBLK):
                    act.wait_ge(norm1[l].tr, j + 1)
                    act.activation(hT[:, j * BLK:(j + 1) * BLK], bank[j % 2][:], ACT.Identity, bias=col("ln1_b", l),
                                   scale=col("ln1_w", l)).then_inc(norm1[l].hT, 1)

                def part(a, n):
                    if n == 0:
                        act.wait_ge(s.qk, l * PER["qk"] + a + 1)
                        act.wait_ge(s.qk_st, l * PER["qk_st"] + 16 * a)
                        act.activation(qks[:, 0], qk32, ACT.Copy).then_inc(s.p1, 1)
                    else:
                        act.wait_ge(s.r, l * PER["r"] + a + 1)
                        act.activation(qks[:, 1], qkr, ACT.Copy).then_inc(s.p2, 1)

                def exps(b, gr):
                    for t in range(3):
                        act.wait_ge(s.t_mm, l * PER["t_mm"] + SUNITS * b + 3 * gr + t + 1)
                        if t == 0:
                            act.wait_ge(s.av, l * PER["av"] + NG * b + gr + 1)
                        act.activation(prob[:, gr % 2, t * BLK:(t + 1) * BLK], bank[4 + t][:], ACT.Exp,
                                       scale=ATT_SCALE).then_inc(s.exp, 1)

                def attended(b, r):
                    act.wait_ge(s.av, l * PER["av"] + PROB_FREE + NG * b + 2 * r + 2)
                    act.wait_ge(s.oTT, l * PER["oTT"] + TPB * (b + 1))
                    act.activation(oT[:, 2 * r:2 * r + 2, :], bank[7][:].rearrange("p (g t) -> p g t", g=2),
                                   ACT.Copy).then_inc(s.oT, 1)

                def normal_T(d1):
                    act.wait_ge(s.on_mm, l * PER["on_mm"] + d1)
                    act.activation(onT, bank[0][:, 0:S], ACT.Copy).then_inc(s.onT, 1)

                def maxima_T(b):
                    act.wait_ge(s.mT_mm, l * PER["mT_mm"] + b + 1)
                    act.wait_ge(s.m_ld, l * PER["m_ld"] + 16 * MROWS * b)
                    act.activation(mT[:], bank[2][0:MROWS * H, 0:P].bitcast(BF16), ACT.Copy).then_inc(s.mT, 1)

                def step(b, more_a, more_b):
                    exps(b, 0)
                    if more_a:
                        part(b + 2, 0)
                        part(b + 2, 1)
                    exps(b, 1)
                    exps(b, 2)
                    normal_T(b + 1)
                    attended(b, 0)
                    exps(b, 3)
                    if more_b:
                        maxima_T(b + 1)
                    attended(b, 1)

                if l == 0:
                    act.sem_inc(s.exp, T_FREE)
                    act.sem_inc(s.oT, OT_FREE)
                    act.sem_inc(s.onT, BANK_FREE)
                for a in range(2):
                    part(a, 0)
                    part(a, 1)
                maxima_T(0)
                with act.Fori(0, (B - 2) // RING) as i:
                    for k in range(RING):
                        step(RING * i + k, True, True)
                step(B - 2, False, True)
                step(B - 1, False, False)
                normal_T(B + 1)

            attention(0)
            prepare(1, 0)
            token_moe_1()
            attention(1)
            prepare(2, 1)

            act.sem_inc(q.gel, GEL_FREE)
            act.wait_ge(q.cw_mm, 1)
            act.activation(cw.rearrange("p b k -> p (b k)"), bank[2][:, 0:2 * B], ACT.Copy).then_inc(q.cw, 1)
            act.wait_ge(q.weT_mm, 1)
            act.activation(weT[0:E, 0:B], bank[3][0:E, 0:B], ACT.Copy).then_inc(q.weT, 1)
            act.wait_ge(q.b2_mm, 1)
            act.activation(b2s, bank[3][:, 0:B], ACT.Copy).then_inc(q.b2, 1)
            with act.Fori(0, B // 2) as i:
                for k in range(4):
                    n = 4 * i + k
                    act.wait_ge(q.ug, n + 1)
                    for c in range(FC):
                        if c % 2 == 0:
                            act.wait_ge(q.a, 2 * n + c // 2 + 1)
                        last_ = act.activation(gel[:, k % 2, c, :],
                                               bank[2 * (k % 2) + c // 2][:, (c % 2) * S:(c % 2 + 1) * S], ACT.Gelu,
                                               bias=b1s[:, k, c:c + 1])
                        if c % 2:
                            last_.then_inc(q.gel, 1)

        @block.vector
        def _(dve):
            lines = [0]

            def line(ins):
                lines[0] += 1
                ins.then_inc(g.line, 1)
                dve.wait_ge(g.line, lines[0])

            dve.wait_ge(g.ld_lora, 16 * 5)
            for b in range(B):
                up = dve.tensor_scalar(bsw[:, b, :], BsT_sb, wer[:, b:b + 1], LORA_SCALE, ALU.mult, ALU.mult)
            up.then_inc(g.bsw, 1)
            for j in range(2):
                dve.wait_ge(g.weff_mm, j + 1)
                dve.tensor_tensor(weff[:, 4 * j:4 * j + 4, :], bank[j][:].rearrange("p (b o) -> p b o", b=4),
                                  mid(WbT_sb, 4), ALU.add).then_inc(g.weff_ok, 1)
            dve.wait_ge(g.ld_vec, 32)
            for j in range(NBLK):
                dve.wait_ge(g.h0_mm, j + 1)
                dve.tensor_tensor(hn[:, TB * j:TB * (j + 1), :], bank[2 + j][:].rearrange("p (t o) -> p t o", t=TB),
                                  mid(row("b_base"), TB), ALU.add).then_inc(g.h0_ok, 1)
            dve.wait_ge(g.sq, NT)
            dve.tensor_scalar(var[:], stat[:, :, 0], 1.0 / D, RMS_EPS, ALU.mult, ALU.add).then_inc(g.ms, 1)
            dve.wait_ge(g.rms, 1)
            for j in range(NBLK):
                v = hn[:, TB * j:TB * (j + 1), :]
                dve.tensor_tensor(v, v, last(rstd[:, TB * j:TB * (j + 1)], D), ALU.mult).then_inc(prep[0].hn, 1)

            def layer_norm(s):
                for t in range(NT):
                    ins = dve.bn_stats(stat[:, t, :], z[:, TPB + t, :])
                line(ins)
                for t in range(NT):
                    ins = dve.bn_aggr(mv[:, t, :], stat[:, t, :])
                line(ins)
                dve.tensor_scalar(var[:], mv[:, :, 1], LN_EPS, None, ALU.add).then_inc(s.var, 1)
                dve.wait_ge(s.rstd, 1)
                for t in range(NT):
                    ins = dve.tensor_scalar(hn[:, t, :], z[:, TPB + t, :], mv[:, t, 0:1], rstd[:, t:t + 1],
                                            ALU.subtract, ALU.mult)
                    if t % TB == TB - 1:
                        ins.then_inc(s.hn, 1)

            def route(s, n, c, raw, bias):
                lg, tv, ti, tf, pr = logit[0:n, 0:c, :], top_v[0:n, 0:c, :], top_i[0:n, 0:c, :], top_f[0:n, 0:c, :], \
                    pair[0:n, :, 0:c]
                w, o = we[0:n, :, 0:c], onehot[0:n, :, 0:c]
                line(dve.tensor_tensor(lg, raw, mid(bias, c), ALU.add))
                for t in range(c):
                    ins = dve.max(tv[:, t, :], lg[:, t, :])
                line(ins)
                dve.tensor_tensor(pr[:, 0, :], tv[:, :, 1], tv[:, :, 0], ALU.subtract).then_inc(s.diff, 1)
                for t in range(c):
                    ins = dve.max_index(ti[:, t, :], tv[:, t, :], lg[:, t, :])
                line(ins)
                line(dve.tensor_copy(tf, ti[:, :, 0:2]))
                dve.wait_ge(s.exp, 1)
                line(dve.tensor_scalar(pr[:, 3, :], pr[:, 1, :], 1.0, None, ALU.add))
                line(dve.reciprocal(pr[:, 2, :], pr[:, 3, :]))
                line(dve.tensor_tensor(pr[:, 3, :], pr[:, 1, :], pr[:, 2, :], ALU.mult))
                experts = last(row("iota", n), c)
                line(dve.tensor_tensor(w, experts, mid(tf[:, :, 0], E), ALU.is_equal))
                line(dve.tensor_tensor(w, w, mid(pr[:, 2, :], E), ALU.mult))
                line(dve.tensor_tensor(o, experts, mid(tf[:, :, 1], E), ALU.is_equal))
                line(dve.tensor_tensor(o, o, mid(pr[:, 3, :], E), ALU.mult))
                dve.tensor_tensor(w, w, o, ALU.add).then_inc(s.we, 1)

            def prepare(m):
                s = prep[m]
                for j in range(NBLK):
                    v = slice(j * BLK, (j + 1) * BLK)
                    dve.wait_ge(s.hT, j + 1)
                    dve.tensor_copy(hT_hi[:, v], hT[:, v]).then_inc(s.hi, 1)
                    dve.wait_ge(s.hi, j + 1)
                    dve.tensor_tensor(hT_lo[:, v], hT[:, v], hT_hi[:, v].bitcast(F32), ALU.subtract
                                      ).then_inc(s.lo, 1)
                dve.wait_ge(s.logits, 1)
                route(s, P, NT, bank[2][:, 0:NT * E].rearrange("p (t e) -> p t e", t=NT),
                      row(("bg", "gate_b0")[m]))

            def token_moe(m):
                s = moe[m]
                n_w = 3 if m == 0 else 2
                which = (0, 1, 2) if m == 0 else (0, 2)
                dve.sem_inc(s.split, 12)
                dve.sem_inc(s.lo, U32_FREE)
                if m == 1:
                    dve.sem_inc(s.scaled, 2 * NBLK)
                else:
                    dve.sem_inc(s.gate, ACT_FREE)

                def split(i, e, n):
                    w, low = which[min(n // 2, n_w - 1)], n % 2
                    exp = 2 * i + e
                    if n == 0:
                        dve.wait_ge(w_ld[e], 16 * (m * 3 * E // 2 + n_w * (i + 1)))
                        dve.wait_ge(s.y, EC * (exp - 1) + U_FREE + m * NBLK) if not isinstance(exp, int) or exp > 0 else None
                        for j, name in enumerate(("b1a", "b1b") if m == 0 else ("e_b1",)):
                            dve.tensor_copy(bias1[:, e, j, :], cols[:, bass.ds(COL[name][0] + FC * exp, FC)])
                    if n // 2 >= n_w:
                        dve.sem_inc(s.split, 1)
                    elif not low:
                        dve.tensor_copy(whi[:, e, w, :], wraw[:, e, w, :]).then_inc(s.split, 1)
                    else:
                        dve.wait_ge(s.split, 12 + 6 * exp + n)
                        dve.tensor_tensor(wlo[:, e, w, :], wraw[:, e, w, :], whi[:, e, w, :].bitcast(F32),
                                          ALU.subtract).then_inc(s.split, 1)

                def gate(i, kk):
                    k = 2 * EC * i + kk
                    e, c = kk // EC, kk % FC
                    dve.wait_ge(s.b, k + 1)
                    dve.wait_ge(s.act, k + 1)
                    dve.wait_ge(s.scaled, 2 * EC + k - 1)
                    dve.scalar_tensor_tensor(out=gated[:, kk % 2, :], in0=bank[2 + kk % 2][:],
                                             scalar=bias1[:, e, 1, c:c + 1], in1=act_s[:, kk % 4, :],
                                             op0=ALU.add, op1=ALU.mult).then_inc(s.gate, 1)

                def combine(i, kk):
                    e, blk = kk // EC, kk % EC // FC
                    k = 2 * NBLK * i + kk // FC
                    if blk == 0:
                        dve.wait_ge(r_ld[e], 16 * (E // 2 + i + 1))
                    dve.wait_ge(s.y, U_FREE + NBLK + FC * (k + 1))
                    dve.wait_ge(s.sum, k + 1)
                    dve.tensor_tensor(product[:, kk // FC % 2, :], bank[4 + blk][:],
                                      wbc[:, e, blk * BLK:(blk + 1) * BLK], ALU.mult).then_inc(s.scaled, 1)

                def low(i, kk):
                    k = 2 * EC * i + kk
                    dve.wait_ge(s.hi, k + 1) if m == 0 else dve.wait_ge(s.act, A_FREE + k + 1)
                    full = u32 if m == 0 else act_s
                    dve.tensor_tensor(u_lo[:, kk % U_FREE, :], full[:, kk % U32_FREE, :],
                                      u_hi[:, kk % U_FREE, :].bitcast(F32), ALU.subtract).then_inc(s.lo, 1)

                def mix(i, n):
                    b, gg = 2 * i + n // E, n % E
                    a0 = ROW["cond"][0]
                    acc = weff[:, bass.ds(b, 1), :].rearrange("p a o -> p (a o)")
                    c = rows[:, bass.ds(a0 + E * b + gg, 1)]
                    if gg == 0:
                        dve.tensor_scalar(acc, wt[:, gg, :], c, None, ALU.mult).then_inc(g.mix, 1)
                    else:
                        dve.wait_ge(g.mix, 2 * E * i + n)
                        dve.scalar_tensor_tensor(out=acc, in0=wt[:, gg, :], scalar=c, in1=acc, op0=ALU.mult,
                                                 op1=ALU.add).then_inc(g.mix, 1)

                lead = 2 if m == 0 else 3
                ahead = gate if m == 0 else low

                def body(i, last_pair):
                    for kk in range(2 * EC):
                        nk = kk + lead
                        if nk < 2 * EC:
                            ahead(i, nk)
                        elif not last_pair:
                            ahead(i + 1, nk - 2 * EC)
                        if m == 0:
                            low(i, kk)
                        elif kk % FC == FC - 1:
                            combine(i, kk)
                        if 4 <= kk % EC < 10:
                            if kk < EC:
                                split(i, 1, kk % EC - 4)
                            elif not last_pair:
                                split(i + 1, 0, kk % EC - 4)
                        if m == 0 and kk % 2:
                            mix(i, kk // 2)

                for n in range(6):
                    split(0, 0, n)
                if m == 0:
                    dve.wait_ge(g.mixmask, 1)
                for kk in range(lead):
                    ahead(0, kk)
                with dve.Fori(0, E // 2 - 1) as i:
                    body(i, False)
                body(E // 2 - 1, True)

            prepare(0)
            token_moe(0)
            dve.wait_ge(moe[0].y, U_FREE + CH)
            for j in range(NBLK):
                v = xTs[:, j * BLK:(j + 1) * BLK]
                dve.tensor_tensor(v, v, bank[4 + j][:], ALU.add).then_inc(g.x1, 1)
            for j in range(NBLK):
                dve.wait_ge(g.z_mm, j + 1)
                dve.tensor_tensor(z[:, TPB + TB * j:TPB + TB * (j + 1), :],
                                  bank[j][:].rearrange("p (t o) -> p t o", t=TB), mid(row("bias"), TB), ALU.add
                                  ).then_inc(g.z_ok, 1)
            dve.wait_ge(g.z_ok, NBLK)

            def attention(l):
                s = att
                if l == 0:
                    dve.sem_inc(s.red, S_FREE)
                    dve.sem_inc(s.z, BANK_FREE)

                layer_norm(norm1[l])
                for j in range(NBLK):
                    dve.wait_ge(s.v_mm, l * PER["v_mm"] + j + 1)
                    dve.tensor_tensor(hn[:, TB * j:TB * (j + 1), :], bank[2 + j][:].rearrange("p (t d) -> p t d", t=TB),
                                      mid(row(f"bv{l}"), TB), ALU.add).then_inc(s.v, 1)

                def project(a):
                    dve.wait_ge(s.qk_mm, l * PER["qk_mm"] + a + 1)
                    dve.tensor_scalar(qk32[:, 0, :], bank[0][:, 0:S], col("bq", l), None, ALU.add)
                    dve.tensor_scalar(qk32[:, 1, :], bank[0][:, S:2 * S], col("bk", l), None, ALU.add
                                      ).then_inc(s.qk, 1)

                def rest(a):
                    dve.wait_ge(s.p1, l * PER["p1"] + a + 1)
                    dve.tensor_tensor(qkr, qk32, qks[:, 0], ALU.subtract).then_inc(s.r, 1)

                def rest2(a):
                    dve.wait_ge(s.p2, l * PER["p2"] + a + 1)
                    dve.tensor_tensor(qks[:, 2], qkr, qks[:, 1], ALU.subtract).then_inc(s.p3, 1)

                def reduce(b, u):
                    dve.wait_ge(s.s_mm, l * PER["s_mm"] + SUNITS * b + u + 1)
                    n = 4 if u < 4 else 2
                    h = 4 * u if u < 4 else 2 * (u - 4)
                    dve.tensor_reduce(mmax[:, int(u >= 4), h:h + n], bank[2 + u % 2][:].rearrange(
                        "p (h k) -> p h k", h=n), AX.X, ALU.max).then_inc(s.red, 1)

                def minus_max(b):
                    dve.wait_ge(s.red, l * PER["red"] + S_FREE + SUNITS * (b + 1))
                    dve.wait_ge(s.mT_mm, l * PER["mT_mm"] + b)
                    dve.tensor_scalar(msp[:, :, 0, :], mmax, -1.0, None, ALU.mult).then_inc(s.mhi, 1)
                    dve.wait_ge(s.mhi, l * PER["mhi"] + b + 1)
                    dve.scalar_tensor_tensor(out=msp[:, :, 1, :], in0=mmax, scalar=-1.0, in1=msp[:, :, 0, :],
                                             op0=ALU.mult, op1=ALU.subtract).then_inc(s.msp, 1)

                def normalize(d1):
                    for t in range(TPB):
                        dve.wait_ge(s.oTT, l * PER["oTT"] + TPB * (d1 - 1) + t + 1)
                        v = bank[t][:].rearrange("p (h s) -> p h s", h=H)
                        dve.reciprocal(orec[:, t, :], v[:, :, HD]).then_inc(s.rec, 1)
                    for t in range(TPB):
                        v = bank[t][:].rearrange("p (h s) -> p h s", h=H)
                        dve.wait_ge(s.rec, l * PER["rec"] + TPB * (d1 - 1) + t + 1)
                        dve.tensor_tensor(onorm[:, t, :].rearrange("p (h d) -> p h d", h=H), v[:, :, 0:HD],
                                          last(orec[:, t, :], HD), ALU.mult).then_inc(s.on, 1)

                def residual(d1):
                    dve.wait_ge(s.wo_mm, l * PER["wo_mm"] + d1)
                    zb = z[:, bass.ds(TPB * (d1 - 1 + 1) - TPB, TPB), :]
                    dve.tensor_tensor(zb, zb, bank[1][:, 0:S].rearrange("p (t d) -> p t d", t=TPB), ALU.add
                                      ).then_inc(s.z, 1)

                def step(b, k, more_a, more_b):
                    if more_b:
                        reduce(b + 1, 0)
                        reduce(b + 1, 1)
                    if more_a:
                        project(b + 2)
                    if more_b:
                        reduce(b + 1, 2)
                    if more_a:
                        rest(b + 2)
                    if more_b:
                        reduce(b + 1, 3)
                    if more_a:
                        rest2(b + 2)
                    if more_b:
                        reduce(b + 1, 4)
                        reduce(b + 1, 5)
                    normalize(b + 1)
                    if more_b:
                        for u in range(6, 10):
                            reduce(b + 1, u)
                    residual(b + 1)
                    if more_b:
                        reduce(b + 1, 10)
                        reduce(b + 1, 11)
                        minus_max(b + 1)

                for a in range(2):
                    project(a)
                    rest(a)
                    rest2(a)
                for u in range(SUNITS):
                    reduce(0, u)
                minus_max(0)
                dve.wait_ge(s.zb, (l + 1) * NBLK)
                with dve.Fori(0, (B - 2) // RING) as i:
                    for k in range(RING):
                        step(RING * i + k, k, True, True)
                step(B - 2, (B - 2) % RING, False, True)
                step(B - 1, (B - 1) % RING, False, False)
                normalize(B + 1)
                residual(B + 1)
                dve.wait_ge(s.z, l * PER["z"] + BANK_FREE + B + 1)

            attention(0)
            layer_norm(prep[1])
            prepare(1)
            token_moe(1)
            for j in range(NBLK):
                dve.wait_ge(g.back_mm, j + 1)
                v = z[:, TPB + TB * j:TPB + TB * (j + 1), :]
                dve.tensor_tensor(v, v, bank[j][:].rearrange("p (t o) -> p t o", t=TB), ALU.add).then_inc(g.back, 1)
            dve.wait_ge(g.back, NBLK)
            attention(1)
            layer_norm(prep[2])

            s = prep[2]
            dve.wait_ge(s.hT, NBLK)
            line(dve.tensor_reduce(hmean, hT[:].rearrange("p (b t) -> p b t", b=B), AX.X, ALU.add))
            dve.tensor_scalar(hmean, hmean, 1.0 / S, None, ALU.mult).then_inc(q.mean, 1)
            dve.wait_ge(s.logits, 1)
            route(s, B, 1, bank[2][0:B, 0:E].rearrange("p (t e) -> p t e", t=1), row("gate_b1", B))
            dve.tensor_tensor(diag[0:B], last(ident[0:B, 0:B], 2),
                              pair[0:B, 2:4, 0].rearrange("p (a k) -> p a k", a=1).to_broadcast([B, B, 2]), ALU.mult
                              ).then_inc(q.cw_in, 1)
            dve.sem_inc(q.ug, 2)
            dve.wait_ge(q.cw, 1)

            def scale6(i, k):
                n = 4 * i + k
                b = 2 * i + k // 2
                dve.wait_ge(q.gel, GEL_FREE + 2 * n + 2)
                dve.wait_ge(q.y, n + 3)
                dve.tensor_scalar(ug[:, k % 2], gel[:, k % 2], cw[:, bass.ds(b, 1), k % 2], None, ALU.mult
                                  ).then_inc(q.ug, 1)

            dve.wait_ge(q.b2, 1)
            with dve.Fori(0, B // 2) as i:
                for k in range(4):
                    scale6(i, k)
                    if k % 2:
                        b = 2 * i + k // 2
                        dve.wait_ge(q.y, 4 + 2 * b + 2)
                        dve.scalar_tensor_tensor(out=yx[:, k // 2, :], in0=bank[4 + k // 2][:, 0:S],
                                                 scalar=b2s[:, bass.ds(b, 1)], in1=xTs[:, bass.ds(S * b, S)],
                                                 op0=ALU.add, op1=ALU.add).then_inc(q.yx, 1)
                        dve.wait_ge(q.t, b + 1)
                        dve.tensor_tensor(oseq_at(b), z[:, bass.ds(TPB * (b + 1), TPB), :],
                                          bank[6 + k // 2][:, 0:S].rearrange("p (t d) -> p t d", t=TPB), ALU.add
                                          ).then_inc(q.o, 1)

        @block.tensor
        def _(pe):
            pe.wait_ge(g.bsw, 1)
            pe.wait_ge(g.ld_lora, 16 * 5)
            for j in range(2):
                pe.matmul(bank[j][:], As_sb, bsw[:, 4 * j:4 * j + 4, :].rearrange("p b o -> p (b o)"), start=True,
                          stop=True).then_inc(g.weff_mm, 1)
            for t in range(NT):
                b = t // TPB
                if b % 4 == 0:
                    pe.wait_ge(g.weff_ok, b // 4 + 1)
                mm = pe.matmul(bank[2 + t // TB][:, (t % TB) * P:(t % TB + 1) * P], xTs[:, t * P:(t + 1) * P],
                               weff[:, b, :], start=True, stop=True)
                if t % TB == TB - 1:
                    mm.then_inc(g.h0_mm, 1)
            pe.wait_ge(g.ident, 3)
            pe.wait_ge(g.ld_rest, 16 * 5)

            def transposes(s):
                for j in range(NBLK):
                    pe.wait_ge(s.hn, j + 1)
                    if j >= 2:
                        pe.wait_ge(s.hT, j - 1)
                    for t in range(TB):
                        mm = pe.transpose(bank[j % 2][:, t * P:(t + 1) * P], hn[:, TB * j + t, :], ident[:])
                    mm.then_inc(s.tr, 1)

            def prepare(m):
                s = prep[m]
                transposes(s)
                for t in range(NT):
                    if t % TB == 0:
                        pe.wait_ge(s.hT, t // TB + 1)
                    mm = pe.matmul(bank[2][:, t * E:(t + 1) * E], hT[:, t * P:(t + 1) * P], gate_sb[:, m, :],
                                   start=True, stop=True)
                mm.then_inc(s.logits, 1)
                pe.wait_ge(s.we, 1)
                pe.transpose(bank[3][:, 0:P], we[:].rearrange("p e t -> p (e t)"), ident[:]).then_inc(s.weT_mm, 1)

            def token_moe(m):
                s = moe[m]
                n_a = 2 if m == 0 else 4
                pe.sem_inc(s.y, U_FREE)
                pe.wait_ge(prep[m].load, 16)
                pe.wait_ge(prep[m].lo, NBLK)
                for j in range(NBLK):
                    mm = pe.matmul(bank[4 + j][:], b2_sb[:, m, :], weT8[:, j * BLK:(j + 1) * BLK], start=True,
                                   stop=(m == 1), skip_group_check=True)
                    if m == 1:
                        mm.then_inc(s.y, 1)

                def three(dst, w, x, sl, start, done=None):
                    pe.matmul(dst, w[0], x[0], start=start, stop=False, skip_group_check=True)
                    pe.matmul(dst, w[0], x[1], start=False, stop=False, skip_group_check=True)
                    pe.matmul(dst, w[1], x[0], start=False, stop=True, skip_group_check=True).then_inc(done, 1)

                def first(i, kk):
                    k = 2 * EC * i + kk
                    e, blk, c = kk // EC, kk % EC // FC, kk % FC
                    if kk % EC == 0:
                        pe.wait_ge(s.split, 12 + 6 * (2 * i + e + 1))
                    tok, f = slice(blk * BLK, (blk + 1) * BLK), slice(c * P, (c + 1) * P)
                    x = hT_hi[:, tok], hT_lo[:, tok]
                    if m == 1:
                        pe.wait_ge(s.act, k + 1)
                    elif not isinstance(k, int) or k >= n_a:
                        pe.wait_ge(s.act, k - n_a + 1)
                    three(bank[kk % n_a][:], (whi[:, e, 0, f], wlo[:, e, 0, f]), x, None, True, s.a)
                    if m == 0:
                        pe.wait_ge(s.gate, ACT_FREE + k - 1)
                        three(bank[2 + kk % 2][:], (whi[:, e, 1, f], wlo[:, e, 1, f]), x, None, True, s.b)

                def second(i, kk):
                    k = 2 * EC * i + kk
                    e, blk, c = kk // EC, kk % EC // FC, kk % FC
                    d = slice(c * D, (c + 1) * D)
                    if m == 1 and c == 0:
                        pe.wait_ge(s.scaled, NBLK + 2 * NBLK * i + kk // FC + 1)
                    pe.wait_ge(s.lo, U32_FREE + k + 1)
                    three(bank[4 + blk][:], (whi[:, e, 2, d], wlo[:, e, 2, d]),
                          (u_hi[:, kk % U_FREE, :], u_lo[:, kk % U_FREE, :]), None, m == 1 and c == 0, s.y)

                lead = 3

                def body(i, last_pair):
                    for kk in range(2 * EC):
                        nk = kk + lead
                        if nk < 2 * EC:
                            first(i, nk)
                        elif not last_pair:
                            first(i + 1, nk - 2 * EC)
                        second(i, kk)

                for kk in range(lead):
                    first(0, kk)
                if m == 1:
                    pe.wait_ge(s.init, NBLK)
                with pe.Fori(0, E // 2 - 1) as i:
                    body(i, False)
                body(E // 2 - 1, True)

            prepare(0)
            token_moe(0)
            for t in range(NT):
                if t % TB == 0:
                    pe.wait_ge(g.x1, t // TB + 1)
                if t == 0:
                    pe.wait_ge(g.mix, B * E)
                mm = pe.matmul(bank[t // TB][:, (t % TB) * P:(t % TB + 1) * P], xTs[:, t * P:(t + 1) * P],
                               weff[:, t // TPB, :], start=True, stop=True)
                if t % TB == TB - 1:
                    mm.then_inc(g.z_mm, 1)

            def attention(l):
                s = att
                pe.wait_ge(g.masks, 5)
                pe.wait_ge(g.pad, 4)
                pe.wait_ge(s.vinit, l * PER["vinit"] + 3)
                if l == 0:
                    pe.sem_inc(s.av, PROB_FREE)

                transposes(norm1[l])
                for t in range(NT):
                    if t % TB == 0:
                        pe.wait_ge(norm1[l].hT, t // TB + 1)
                    mm = pe.matmul(bank[2 + t // TB][:, (t % TB) * P:(t % TB + 1) * P], hT[:, t * P:(t + 1) * P],
                                   att_w[:, l, 2, :], start=True, stop=True)
                    if t % TB == TB - 1:
                        mm.then_inc(s.v_mm, 1)

                def project(a):
                    tok = hT[:, bass.ds(S * a, S)]
                    pe.matmul(bank[0][:, 0:S], att_w[:, l, 0, :], tok, start=True, stop=True)
                    pe.matmul(bank[0][:, S:2 * S], att_w[:, l, 1, :], tok, start=True, stop=True).then_inc(s.qk_mm, 1)

                def scores(b, r, u):
                    pe.wait_ge(s.red, l * PER["red"] + SUNITS * b + u + 1)
                    if u == 0:
                        pe.wait_ge(s.qk_ld, l * PER["qk_ld"] + 16 * QK_LOADS * (b + 1))
                        pe.wait_ge(s.mT, l * PER["mT"] + b)
                    t = int(u >= 4)
                    n = 4 if u < 4 else 2
                    h0 = 4 * u if u < 4 else 2 * (u - 4)
                    keys = BLK // n
                    dst = bank[2 + u % 2]
                    for j in range(n):
                        h = (h0 + j) * S
                        pe.matmul(dst[:, j * keys:(j + 1) * keys], qp[:, r, h + t * P:h + (t + 1) * P],
                                  kp[:, r, h:h + keys], start=(j == 0), stop=False, skip_group_check=True)
                    pe.matmul(dst[:].rearrange("p (h k) -> p h k", h=n)[:, :, keys - P:keys], ident_bf[:],
                              mid(mask_q[:], n), start=False, stop=True, skip_group_check=True).then_inc(s.s_mm, 1)

                def scores_T(b, r, gr):
                    if gr == 0:
                        pe.wait_ge(s.m_ld, l * PER["m_ld"] + 16 * MROWS * (b + 1))
                    for t in range(3):
                        pe.wait_ge(s.exp, l * PER["exp"] + SUNITS * b + 3 * gr + t + 1)
                        n = 2 if t < 2 else 4
                        kt = int(t == 2)
                        keys, width = slice(kt * P, (kt + 1) * P), BLK // n
                        dst = bank[4 + t]
                        for j in range(n):
                            h = (HG * gr + (2 * t + j if t < 2 else j)) * S
                            pe.matmul(dst[:, j * width:(j + 1) * width], kp[:, r, h + kt * P:h + (kt + 1) * P],
                                      qp[:, r, h + kt * P:h + S], start=(j == 0), stop=False, skip_group_check=True)
                        pe.matmul(dst[:].rearrange("p (h k) -> p h k", h=n)[:, :, 0:P], ident_bf[:], mid(mask_k[:], n),
                                  start=False, stop=True, skip_group_check=True).then_inc(s.t_mm, 1)

                def attend(b, r, gr):
                    pe.wait_ge(s.exp, l * PER["exp"] + T_FREE + SUNITS * b + 3 * gr + 3)
                    pe.wait_ge(s.vr, l * PER["vr"] + b + 1)
                    if gr % 2 == 0:
                        pe.wait_ge(s.oT, l * PER["oT"] + OT_FREE + 2 * b + gr // 2)
                    for j in range(HG):
                        pe.matmul(bank[7][SLOT * j:SLOT * (j + 1), (gr % 2) * S:(gr % 2 + 1) * S],
                                  vaug[:, r, 0, HG * gr + j, :], prob[:, gr % 2, j * S:(j + 1) * S], start=True,
                                  stop=False, skip_group_check=True)
                    for j in range(HG):
                        mm = pe.matmul(bank[7][SLOT * j:SLOT * (j + 1), (gr % 2) * S + P:(gr % 2 + 1) * S],
                                       vaug[:, r, 1, HG * gr + j, :],
                                       prob[:, gr % 2, 2 * BLK + j * P:2 * BLK + (j + 1) * P], start=False, stop=True,
                                       skip_group_check=True)
                    mm.then_inc(s.av, 1)

                def attended_T(d1, n_a):
                    pe.wait_ge(s.oT, l * PER["oT"] + OT_FREE + 2 * (d1 - 1))
                    pe.wait_ge(s.onT, l * PER["onT"] + BANK_FREE + d1 - 1)
                    pe.wait_ge(s.z, l * PER["z"] + BANK_FREE + d1 - 1)
                    pe.wait_ge(s.qk, l * PER["qk"] + n_a)
                    for t in range(TPB):
                        for gr in range(NG):
                            mm = pe.transpose(bank[t][:, gr * P:(gr + 1) * P], oT[:, gr, t * P:(t + 1) * P], ident[:])
                        mm.then_inc(s.oTT, 1)

                def normal_T(d1):
                    pe.wait_ge(s.on, l * PER["on"] + TPB * d1)
                    for t in range(TPB):
                        mm = pe.transpose(bank[0][:, t * P:(t + 1) * P], onorm[:, t, :], ident[:])
                    mm.then_inc(s.on_mm, 1)

                def output(d1):
                    pe.wait_ge(s.onT, l * PER["onT"] + BANK_FREE + d1)
                    for t in range(TPB):
                        mm = pe.matmul(bank[1][:, t * P:(t + 1) * P], onT[:, t * P:(t + 1) * P], att_w[:, l, 3, :],
                                       start=True, stop=True)
                    mm.then_inc(s.wo_mm, 1)

                def maxima_T(b):
                    pe.wait_ge(s.msp, l * PER["msp"] + b + 1)
                    for t in range(TPB):
                        mm = pe.transpose(bank[2][0:MROWS * H, 0:P].bitcast(BF16)[:, t * P:(t + 1) * P],
                                          msp[:, t].rearrange("p r h -> p (r h)"), ident_bf[:])
                    mm.then_inc(s.mT_mm, 1)

                def step(b, k, more_a, more_b):
                    r, r1 = k % RING, (k + 1) % RING

                    def maxima_scores(u):
                        if more_b:
                            scores(b + 1, r1, u)
                            scores(b + 1, r1, u + 1)

                    maxima_scores(0)
                    if more_a:
                        pe.wait_ge(s.onT, l * PER["onT"] + BANK_FREE + b)
                        project(b + 2)
                    scores_T(b, r, 0)
                    maxima_scores(2)
                    scores_T(b, r, 1)
                    maxima_scores(4)
                    attended_T(b + 1, b + 3 if more_a else B)
                    attend(b, r, 0)
                    maxima_scores(6)
                    scores_T(b, r, 2)
                    normal_T(b + 1)
                    maxima_scores(8)
                    attend(b, r, 1)
                    output(b + 1)
                    maxima_scores(10)
                    scores_T(b, r, 3)
                    attend(b, r, 2)
                    if more_b:
                        maxima_T(b + 1)
                    attend(b, r, 3)

                project(0)
                pe.wait_ge(s.qk, l * PER["qk"] + 1)
                project(1)
                pe.wait_ge(s.v, (l + 1) * NBLK)
                for u in range(SUNITS):
                    scores(0, 0, u)
                maxima_T(0)
                with pe.Fori(0, (B - 2) // RING) as i:
                    for k in range(RING):
                        step(RING * i + k, k, True, True)
                step(B - 2, (B - 2) % RING, False, True)
                step(B - 1, (B - 1) % RING, False, False)
                attended_T(B + 1, B)
                normal_T(B + 1)
                output(B + 1)

            attention(0)
            prepare(1)
            token_moe(1)
            for t in range(NT):
                if t % TB == 0:
                    pe.wait_ge(moe[1].sum, PRODUCT_FREE + (E - 1) * NBLK + t // TB + 1)
                mm = pe.transpose(bank[t // TB][:, (t % TB) * P:(t % TB + 1) * P],
                                  y_sum[:, t // TB, (t % TB) * P:(t % TB + 1) * P], ident[:])
                if t % TB == TB - 1:
                    mm.then_inc(g.back_mm, 1)
            pe.wait_ge(g.back, NBLK)
            attention(1)

            s = prep[2]
            transposes(s)
            pe.wait_ge(q.mean, 1)
            pe.matmul(bank[2][0:B, 0:E], hmean, gate_sb[:, 2, :], start=True, stop=True).then_inc(s.logits, 1)
            pe.wait_ge(q.ones, 1)
            pe.wait_ge(q.cw_in, 1)
            pe.matmul(bank[2][:, 0:2 * B], ones8[0:B, :], diag[0:B].rearrange("p b k -> p (b k)"), start=True,
                      stop=True).then_inc(q.cw_mm, 1)
            pe.transpose(bank[3][0:E, 0:B], we[0:B, :, 0], ident[0:B, 0:B]).then_inc(q.weT_mm, 1)
            pe.wait_ge(q.weT, 1)
            pe.matmul(bank[3][:, 0:B], b2_sb[:, 2, :], weT[0:E, 0:B], start=True, stop=True).then_inc(q.b2_mm, 1)
            pe.wait_ge(q.b2, 1)
            pe.sem_inc(q.y, 4)

            def first6(i, k):
                n = 4 * i + k
                pe.wait_ge(q_w[k], 48 * (i + 1))
                pe.wait_ge(q.gel, GEL_FREE + 2 * n - 2)
                tok = hT[:, bass.ds(S * (2 * i + k // 2), S)]
                for c in range(FC):
                    mm = pe.matmul(bank[2 * (k % 2) + c // 2][:, (c % 2) * S:(c % 2 + 1) * S],
                                   w1s[:, k, c * P:(c + 1) * P], tok, start=True, stop=True)
                    if c % 2:
                        mm.then_inc(q.a, 1)

            def second6(i, k):
                n = 4 * i + k
                pe.wait_ge(q.ug, n + 3)
                for c in range(FC):
                    mm = pe.matmul(bank[4 + k // 2][:, 0:S], w2s[:, k, c, :], ug[:, k % 2, c, :],
                                   start=(k % 2 == 0 and c == 0), stop=(k % 2 == 1 and c == FC - 1))
                mm.then_inc(q.y, 1)

            def body6(i, last_two):
                for k in range(4):
                    if k < 3:
                        first6(i, k + 1)
                    elif not last_two:
                        first6(i + 1, 0)
                    second6(i, k)
                    if k % 2:
                        pe.wait_ge(q.yx, 2 * i + k // 2 + 1)
                        for t in range(TPB):
                            mm = pe.transpose(bank[6 + k // 2][:, t * P:(t + 1) * P], yx[:, k // 2, t * P:(t + 1) * P],
                                              ident[:])
                        mm.then_inc(q.t, 1)

            first6(0, 0)
            with pe.Fori(0, B // 2 - 1) as i:
                body6(i, False)
            body6(B // 2 - 1, True)


def kernel(x, cond_8, L0_cond_W_base, L0_cond_b_base, L0_cond_As, L0_cond_Bs, L0_ffn_ln_w, L0_ffn_Wg, L0_ffn_bg,
           L0_ffn_W1a, L0_ffn_b1a, L0_ffn_W1b, L0_ffn_b1b, L0_ffn_W2, L0_ffn_b2, L1_cond_weight, L1_cond_mask,
           L1_cond_bias, L1_ffn_ln1_w, L1_ffn_ln1_b, L1_ffn_ln2_w, L1_ffn_ln2_b, L1_ffn_wq, L1_ffn_wk, L1_ffn_wv,
           L1_ffn_wo, L1_ffn_bq, L1_ffn_bk, L1_ffn_bv, L1_ffn_bo, L1_ffn_gate_w, L1_ffn_gate_b, L1_ffn_e_w1,
           L1_ffn_e_b1, L1_ffn_e_w2, L1_ffn_e_b2):
    import numpy as _np
    import concourse.bacc as _bacc
    from concourse import mybir as _mybir
    from concourse.bass_utils import run_bass_kernel_spmd as _run

    def npa(a):
        return _np.asarray(a)

    def dim_major(w):
        w = npa(w)
        return w.reshape(w.shape[:-1] + (H, HD)).swapaxes(-1, -2).reshape(w.shape)

    def chunks(b):
        return npa(b).reshape(-1, P).T

    cols = _np.concatenate([npa(L0_ffn_ln_w).reshape(D, 1), npa(L1_ffn_ln1_w).T, npa(L1_ffn_ln1_b).T,
                            npa(L1_ffn_ln2_w).T, npa(L1_ffn_ln2_b).T, dim_major(L1_ffn_bq).T, dim_major(L1_ffn_bk).T,
                            chunks(L0_ffn_b1a), chunks(L0_ffn_b1b), chunks(npa(L1_ffn_e_b1)[0])], axis=1)
    rows = _np.concatenate([npa(v).reshape(-1) for v in (
        L0_cond_b_base, L1_cond_bias, L0_ffn_bg, L1_ffn_gate_b, L1_ffn_bv, L1_ffn_bo, cond_8,
        _np.arange(E, dtype=_np.float32))]).reshape(1, -1)
    arrays = {
        "xT": npa(x).reshape(N, D).T,
        "As": npa(L0_cond_As).reshape(P, D),
        "BsT": npa(L0_cond_Bs).transpose(0, 2, 1).reshape(P, D),
        "WbT": npa(L0_cond_W_base).T,
        "w_er": _np.repeat(npa(cond_8).T, P // E, axis=0),
        "cols": cols,
        "rows": rows,
        "Wg": _np.stack([npa(L0_ffn_Wg), npa(L1_ffn_gate_w)[0], npa(L1_ffn_gate_w)[1]], axis=1),
        "W1a": npa(L0_ffn_W1a), "W1b": npa(L0_ffn_W1b), "W2": npa(L0_ffn_W2),
        "b2": _np.stack([npa(L0_ffn_b2), npa(L1_ffn_e_b2)[0], npa(L1_ffn_e_b2)[1]], axis=1),
        "WT": npa(L1_cond_weight).transpose(2, 0, 1),
        "maskT": npa(L1_cond_mask).T,
        "att_w": _np.stack([dim_major(L1_ffn_wq), dim_major(L1_ffn_wk), npa(L1_ffn_wv), npa(L1_ffn_wo)],
                           axis=1).transpose(2, 0, 1, 3),
        "e_w1": npa(L1_ffn_e_w1), "e_w2": npa(L1_ffn_e_w2),
        "e_b1s": npa(L1_ffn_e_b1)[1].reshape(E, FC, P).transpose(0, 2, 1),
    }
    nc = _bacc.Bacc("TRN2", target_bir_lowering=False, num_devices=1)
    feeds, args = {}, []
    for name, a in arrays.items():
        a = _np.ascontiguousarray(a)
        feeds[f"in_{name}"] = a
        args.append(nc.dram_tensor(f"in_{name}", a.shape, _mybir.dt.from_np(a.dtype), kind="ExternalInput").ap())
    args.append(nc.dram_tensor("out_0", (B, S, D), F32, kind="ExternalOutput").ap())
    build(nc, *args)
    r = _run(nc, [feeds], core_ids=[0])
    return r.results[0]["out_0"]
```

```python
from contextlib import ExitStack

import numpy as np

import concourse.bass as bass
from concourse import mybir

F32 = mybir.dt.float32
F32R = mybir.dt.float32r
BF16 = mybir.dt.bfloat16
U32 = mybir.dt.uint32
ALU = mybir.AluOpType
ACT = mybir.ActivationFunctionType
AX = mybir.AxisListType

B, S, D = 8, 256, 128
P = 128
N = B * S
NT = N // P
TPB = S // P
BLK = 512
NBLK = N // BLK
TB = BLK // P
E = 8
F = 512
FC = F // P
EC = NBLK * FC
CH = E * EC
H, HD = 16, 8
L = 2
HG = 4
NG = H // HG
SLOT = 32
LORA_SCALE = 2.0
RMS_EPS = float(np.finfo(np.float32).eps)
LN_EPS = 1e-5
ATT_SCALE = HD ** -0.5
NEG = -1e30
PARTS = 3
ROW_OF = [0, 3 * HD, 5 * HD]
MROW = 6 * HD
MROWS = 2
TWO_ONES = 1.0 + 0x3F80 / 2 ** 23
RING = 3
QK_LOADS = 2 * PARTS + 1
SUNITS = 12
T_FREE = 3
S_FREE = 2
PROB_FREE = 2
OT_FREE = 2
BANK_FREE = 1
GEL_FREE = 4
U_FREE = 4
ACT_FREE = 4
A_FREE = 4
PRODUCT_FREE = 2
U32_FREE = 4


def lay(items):
    table, at = {}, 0
    for name, n in items:
        table[name] = (at, at + n)
        at += n
    return table, at


COL, NCOL = lay([("ln_w", 1), ("ln1_w", L), ("ln1_b", L), ("ln2_w", L), ("ln2_b", L), ("bq", L), ("bk", L),
                 ("b1a", E * FC), ("b1b", E * FC), ("e_b1", E * FC)])
ROW, NROW = lay([("b_base", D), ("bias", D), ("bg", E), ("gate_b0", E), ("gate_b1", E), ("bv0", D), ("bv1", D),
                 ("bo0", D), ("bo1", D), ("cond", B * E), ("iota", E)])


class Signals:

    def __init__(self, sem, tag, names):
        self.all = {n: sem(f"{tag}_{n}") for n in names.split()}

    def __getattr__(self, name):
        return self.all[name]


def build(nc, xT, As, BsT, WbT, w_er, cols_in, rows_in, Wg, W1a, W1b, W2, b2, WT, maskT,
          att_in, e_w1, e_w2, e_b1s, out):
    we_dram = [nc.dram_tensor(f"we_dram{m}", [E, N], F32, kind="Internal").ap() for m in range(2)]
    qk_dram = nc.dram_tensor("qk_dram", [RING, PARTS, 2, HD, H * S], BF16, kind="Internal").ap()

    with ExitStack() as ctx:
        def sb(name, shape, dt=F32):
            return ctx.enter_context(nc.sbuf_tensor(name, shape, dt))

        def sem(name):
            return ctx.enter_context(nc.semaphore(name))

        bank = [ctx.enter_context(nc.psum_tensor(f"bank{i}", [P, BLK], F32)) for i in range(8)]

        xTs = sb("xTs", [P, N])
        z = sb("z", [P, TPB + NT, D])
        hn = sb("hn", [P, NT, D])
        hT = sb("hT", [P, N])
        hT_hi = sb("hT_hi", [P, N], F32R)
        hT_lo = sb("hT_lo", [P, N], F32R)
        cols = sb("cols", [P, NCOL])
        rows = sb("rows", [P, NROW])
        ident = sb("ident", [P, P])
        ident_bf = sb("ident_bf", [P, P], BF16)
        mask_q = sb("mask_q", [P, P], BF16)
        mask_k = sb("mask_k", [P, P], BF16)
        weff = sb("weff", [P, B, D])
        stat = sb("stat", [P, NT, 6])
        mv = sb("mv", [P, NT, 2])
        var = sb("var", [P, NT])
        rstd = sb("rstd", [P, NT])
        half = sb("half", [P, NT])
        logit = sb("logit", [P, NT, E])
        top_v = sb("top_v", [P, NT, 8])
        top_i = sb("top_i", [P, NT, 8], U32)
        top_f = sb("top_f", [P, NT, 2])
        pair = sb("pair", [P, 4, NT])
        we = sb("we", [P, E, NT])
        onehot = sb("onehot", [P, E, NT])
        weT = sb("weT", [P, P])
        gate_sb = sb("gate_sb", [P, 3, E])
        b2_sb = sb("b2_sb", [P, 3, D])
        att_w = sb("att_w", [P, L, 4, D])
        whi = sb("whi", [P, 2, 3, F], F32R)
        wlo = sb("wlo", [P, 2, 3, F], F32R)
        bias1 = sb("bias1", [P, 2, 2, FC])
        u_hi = sb("u_hi", [P, U_FREE, BLK], F32R)
        u_lo = sb("u_lo", [P, U_FREE, BLK], F32R)
        qp = sb("qp", [P, RING, H * S], BF16)
        kp = sb("kp", [P, RING, H * S], BF16)
        mT = sb("mT", [MROWS * H, S], BF16)
        ids = sb("ids", [1, B * 2], U32)
        weT8 = hn[:].rearrange("p t d -> p (t d)")

        arena = sb("arena", [P, 12288])

        def views(items):
            got, at = [], 0
            for shape, dt in items:
                n = int(np.prod(shape)) * (2 if dt == BF16 else 4) // 4
                v = arena[:, at:at + n]
                at += n
                v = v.bitcast(BF16) if dt == BF16 else v
                if len(shape) == 4 and shape[1] == PARTS:
                    v = v.rearrange("p (r n w t) -> p r n w t", r=shape[0], n=PARTS, w=2)
                    got.append(v)
                    continue
                if len(shape) == 2:
                    v = v.rearrange("p (a b) -> p a b", a=shape[0])
                elif len(shape) == 3:
                    v = v.rearrange("p (a b c) -> p a b c", a=shape[0], b=shape[1])
                elif len(shape) == 4:
                    v = v.rearrange("p (a b c d) -> p a b c d", a=shape[0], b=shape[1], c=shape[2])
                got.append(v)
            assert at <= arena.shape[1], at
            return got

        wraw, wbc, act_s, gated, u32 = views([([2, 3, F], F32), ([2, N], F32), ([4, BLK], F32), ([2, BLK], F32),
                                              ([U32_FREE, BLK], F32)])
        product = gated
        y_sum = u32
        (prob, vaug, oT, qk32, qkr, qks, onorm, onT, orec, mmax, msp) = views([
            ([2, 3 * BLK], F32), ([RING, TPB, H, SLOT], F32), ([NG, S], F32), ([2, S], F32), ([2, S], F32),
            ([RING, PARTS, 2, S], BF16), ([TPB, D], F32), ([S], F32), ([TPB, H], F32),
            ([TPB, H], F32), ([TPB, MROWS, H], BF16)])
        w1s, w2s, b1s, gel, ug, yx, oseq, cw, diag, ones8, b2s, hmean = views([
            ([4, F], F32), ([4, FC, D], F32), ([4, FC], F32), ([2, FC, S], F32), ([2, FC, S], F32), ([2, S], F32),
            ([B, TPB, D], F32), ([B, 2], F32), ([B, 2], F32), ([P], F32), ([B], F32), ([B], F32)])
        start = z[:, TPB:, :].rearrange("p t d -> p (t d)")
        wt = start[:, 0:B * D].rearrange("p (g o) -> p g o", g=E)
        As_sb, BsT_sb, WbT_sb, maskT_sb = (start[:, (8 + n) * D:(9 + n) * D] for n in range(4))
        behind = arena[:, 2 * 3 * F:]
        bsw = behind[:, 0:B * D].rearrange("p (b o) -> p b o", b=B)
        wer = behind[:, B * D:B * D + B]
        square = behind[:, 2 * B * D:2 * B * D + D]

        def oseq_at(b):
            return oseq[:, bass.ds(b, 1)].rearrange("p a t d -> p (a t) d")

        def col(name, i=0):
            a = COL[name][0] + i
            return cols[:, a:a + 1]

        def row(name, n=P):
            a, b = ROW[name]
            return rows[0:n, a:b]

        def mid(v, n):
            return v.rearrange("p (a d) -> p a d", a=1).to_broadcast([v.shape[0], n, v.shape[1]])

        def last(v, n):
            return v.unsqueeze(2).to_broadcast([v.shape[0], v.shape[1], n])

        g = Signals(sem, "g", "ld_lora ld_x ld_vec ld_rest ident masks bsw weff_mm weff_ok h0_mm h0_ok sq ms rms "
                    "zero ld_b2 line mixmask mix x1 z_mm z_ok back_mm back pad carry_sp")
        prep = [Signals(sem, f"p{m}", "hn tr hT logits diff exp we var rstd" +
                        (" hi lo weT_mm weT zero store load" if m < 2 else "")) for m in range(3)]
        norm1 = [Signals(sem, f"n{l}", "hn tr hT var rstd") for l in range(L)]
        moe = [Signals(sem, f"x{m}", "split a act scaled lo y " + ("b gate hi", "init sum")[m]) for m in range(2)]
        PER = {}
        PER.update({n: B for n in "qk_mm qk vr p1 r p2 p3 mhi msp mT_mm mT".split()})
        PER.update({n: NBLK for n in "zb v_mm v".split()})
        PER.update({n: SUNITS * B for n in "s_mm red t_mm exp".split()})
        PER.update({n: TPB * (B + 1) for n in "oTT rec on".split()})
        PER.update({n: B + 1 for n in "on_mm onT wo_mm z".split()})
        PER.update(vinit=3, av=NG * B, oT=2 * B, qk_st=16 * B, qk_ld=16 * QK_LOADS * B, m_ld=16 * MROWS * B)
        att = Signals(sem, "a", " ".join(PER))
        q = Signals(sem, "q", "mean cw_in cw_mm cw b2_mm b2 a gel ug y yx t o store top ids_ld weT weT_mm ones")
        w_ld = [sem(f"w_ld{n}") for n in range(2)]
        r_ld = [sem(f"r_ld{n}") for n in range(2)]
        q_w = [sem(f"q_w{n}") for n in range(4)]

        block = ctx.enter_context(nc.Block())

        def expert_dram(m):
            return ([W1a, W1b], W2) if m == 0 else ([e_w1[0]], e_w2[0])

        @block.sync
        def _(sp):
            for dst, src in ((BsT_sb, BsT), (wer, w_er), (As_sb, As), (WbT_sb, WbT)):
                sp.dma_start(dst, src).then_inc(g.ld_lora, 16)
            sp.dma_start(xTs[:], xT).then_inc(g.ld_x, 16)
            sp.dma_start(cols[:], cols_in).then_inc(g.ld_vec, 16)
            sp.dma_start(rows[:], rows_in.to_broadcast([P, NROW])).then_inc(g.ld_vec, 16)
            for dst, src in ((gate_sb[:], Wg), (wt, WT), (maskT_sb, maskT), (att_w[:], att_in)):
                sp.dma_start(dst, src).then_inc(g.ld_rest, 16)

            def prepare(m):
                s = prep[m]
                if m == 0:
                    sp.wait_ge(g.zero, 1)
                    sp.dma_start(b2_sb[0:E], b2).then_inc(g.ld_b2, 16)
                sp.wait_ge(s.weT, 1)
                sp.dma_start(we_dram[m].rearrange("e (t p) -> (e t) p", t=NT), weT[:]).then_inc(s.store, 16)
                sp.wait_ge(s.store, 16)
                sp.wait_ge(s.zero, 1)
                sp.dma_start(weT8[0:E], we_dram[m]).then_inc(s.load, 16)

            def raw_weights(m, k, e):
                firsts, second = expert_dram(m)
                for n, w in enumerate(firsts):
                    sp.dma_start(wraw[:, k, n, :], w[e]).then_inc(w_ld[k], 16)
                sp.dma_start(wraw[:, k, 2, :].rearrange("p (c d) -> p c d", c=FC),
                             second.rearrange("e (c p) d -> e p c d", p=P)[e]).then_inc(w_ld[k], 16)

            def routing_weights(m, k, e):
                sp.dma_start(wbc[:, k, :], we_dram[m][bass.ds(e, 1), :].to_broadcast([P, N])).then_inc(r_ld[k], 16)

            def moe_loads(m):
                s = moe[m]
                routing_weights(m, 0, 0)
                routing_weights(m, 1, 1)
                with sp.Fori(1, E // 2) as i:
                    for k in range(2):
                        e = 2 * i + k
                        sp.wait_ge(s.split, 6 * e + 6)
                        sp.sem_inc(g.carry_sp, 1)
                        raw_weights(m, k, e)
                        used = EC if m == 0 else NBLK
                        sp.wait_ge(s.scaled, used * e + used)
                        sp.sem_inc(g.carry_sp, 1)
                        routing_weights(m, k, e)

            def attention(l):
                s = att

                def queries_keys(a, r):
                    sp.wait_ge(s.p3, l * PER["p3"] + a + 1)
                    sp.sem_inc(g.carry_sp, 1)
                    sp.dma_start(qk_dram[r].rearrange("n w d (h t) -> (d h) n w t", h=H), qks[:, r]
                                 ).then_inc(s.qk_st, 16)
                    sp.wait_ge(s.qk_st, l * PER["qk_st"] + 16 * (a + 1))
                    sp.sem_inc(g.carry_sp, 1)
                    if l or not isinstance(a, int) or a:
                        sp.wait_ge(s.qk_ld, l * PER["qk_ld"] + 16 * QK_LOADS * a)
                        sp.sem_inc(g.carry_sp, 1)
                    for i in range(PARTS):
                        n = PARTS - i
                        to = slice(ROW_OF[i], ROW_OF[i] + HD * n)
                        part = qk_dram[r, i, 0].rearrange("(a d) x -> a d x", a=1).to_broadcast([n, HD, H * S])
                        sp.dma_start(qp[to, r, :], part).then_inc(s.qk_ld, 16)
                        sp.dma_start(kp[to, r, :], qk_dram[r, 0:n, 1]).then_inc(s.qk_ld, 16)
                    sp.dma_start(qp[MROW:MROW + MROWS, r, :], qp[2 * 32:2 * 32 + MROWS, r, :]).then_inc(s.qk_ld, 16)

                def maxima(b, r):
                    sp.wait_ge(s.mT, l * PER["mT"] + b + 1)
                    sp.sem_inc(g.carry_sp, 1)
                    dst = qp[MROW:MROW + MROWS, r, :].rearrange("r (h t) -> r h t", h=H)
                    for n in range(MROWS):
                        sp.dma_start(dst[n:n + 1], mT[n * H:(n + 1) * H, :]).then_inc(s.m_ld, 16)

                queries_keys(0, 0)
                queries_keys(1, 1)
                maxima(0, 0)

                def step(b, k, more_a, more_b):
                    if more_a:
                        sp.wait_ge(s.exp, l * PER["exp"] + T_FREE + SUNITS * b)
                        sp.sem_inc(g.carry_sp, 1)
                        queries_keys(b + 2, (k + 2) % RING)
                    if more_b:
                        maxima(b + 1, (k + 1) % RING)

                with sp.Fori(0, (B - 2) // RING) as i:
                    for k in range(RING):
                        step(RING * i + k, k, True, True)
                step(B - 2, (B - 2) % RING, False, True)

            for k in range(2):
                raw_weights(0, k, k)
            prepare(0)
            moe_loads(0)
            attention(0)
            sp.wait_ge(att.av, PROB_FREE + NG * B)
            for k in range(2):
                raw_weights(1, k, k)
            prepare(1)
            moe_loads(1)
            attention(1)

            sp.wait_ge(q.top, 1)
            sp.dma_start(ids[:].rearrange("p (b k) -> p b k", k=2), top_i[0:B, 0, 0:2]).then_inc(q.ids_ld, 16)
            sp.wait_ge(q.ids_ld, 16)
            second = e_w2[1].rearrange("e (c p) d -> e p c d", p=P)
            def expert_loads(i, k):
                e = sp.value_load(ids[0:1, bass.ds(4 * i + k, 1)], min_val=0, max_val=E - 1)
                sp.wait_ge(q.y, 4 * i + k + 1)
                sp.sem_inc(g.carry_sp, 1)
                sp.dma_start(w1s[:, k, :], e_w1[1][bass.ds(e, 1), :, :].rearrange("a p f -> (a p) f")
                             ).then_inc(q_w[k], 16)
                sp.dma_start(w2s[:, k], second[bass.ds(e, 1)].rearrange("a p c d -> (a p) c d")
                             ).then_inc(q_w[k], 16)
                sp.dma_start(b1s[:, k, :], e_b1s[bass.ds(e, 1)].rearrange("a p c -> (a p) c")
                             ).then_inc(q_w[k], 16)

            def store(b):
                sp.wait_ge(q.o, b + 1)
                sp.sem_inc(g.carry_sp, 1)
                sp.dma_start(out[bass.ds(b, 1)].rearrange("a (t p) d -> p (a t) d", p=P), oseq_at(b)
                             ).then_inc(q.store, 16)

            for k in range(4):
                expert_loads(0, k)
            with sp.Fori(1, B // 2) as i:
                for k in range(4):
                    expert_loads(i, k)
                    if k % 2:
                        store(2 * i - 2 + k // 2)
            store(B - 2)
            store(B - 1)
            sp.wait_ge(q.store, 16 * B)

        @block.gpsimd
        def _(pool):
            pool.memset(ident[:], 0.0).then_inc(g.ident, 1)
            pool.wait_ge(g.ident, 1)
            pool.affine_select(out=ident[:], in_=ident[:], compare_op=ALU.not_equal, fill=1.0, base=0,
                               pattern=[[-1, P]], channel_multiplier=1).then_inc(g.ident, 1)
            pool.memset(half[:], -0.5).then_inc(g.masks, 1)
            pool.memset(mask_q[:], 0.0).then_inc(g.masks, 1)
            pool.memset(mask_k[:], 0.0).then_inc(g.masks, 1)
            pool.wait_ge(g.ident, 2)
            pool.tensor_copy(ident_bf[:], ident[:]).then_inc(g.ident, 1)
            pool.wait_ge(g.masks, 3)
            pool.affine_select(out=mask_q[:], in_=mask_q[:], compare_op=ALU.is_ge, fill=NEG,
                               base=0, pattern=[[-1, P]], channel_multiplier=1).then_inc(g.masks, 1)
            pool.affine_select(out=mask_k[:], in_=mask_k[:], compare_op=ALU.is_ge, fill=NEG,
                               base=0, pattern=[[1, P]], channel_multiplier=-1).then_inc(g.masks, 1)

            pool.memset(qp[:].bitcast(F32), 0.0).then_inc(g.pad, 1)
            pool.memset(kp[:].bitcast(F32), TWO_ONES).then_inc(g.pad, 1)
            pool.memset(z[:, 0:TPB, :], 0.0).then_inc(g.pad, 1)
            pool.memset(b2_sb[:], 0.0).then_inc(g.zero, 1)

            def power(before, after):
                for j in range(NBLK):
                    pool.wait_ge(before, j + 1)
                    v = slice(TB * j, TB * (j + 1))
                    pool.tensor_tensor(rstd[:, v], var[:, v], half[:, v], ALU.pow).then_inc(after, 1)

            power(g.ms, g.rms)
            pool.wait_ge(prep[0].hT, NBLK)
            pool.memset(weT8, 0.0).then_inc(prep[0].zero, 1)
            pool.wait_ge(g.ld_rest, 16 * 4)
            pool.tensor_tensor(wt, wt, mid(maskT_sb, E), ALU.mult).then_inc(g.mixmask, 1)
            s = moe[0]
            pool.sem_inc(s.scaled, 2 * EC)
            with pool.Fori(0, E // 2) as i:
                for kk in range(2 * EC):
                    k = 2 * EC * i + kk
                    e, blk = kk // EC, kk % EC // FC
                    if kk % EC == 0:
                        pool.wait_ge(r_ld[e], 16 * (i + 1))
                    pool.wait_ge(s.gate, ACT_FREE + k + 1)
                    pool.wait_ge(s.lo, k + 1)
                    pool.tensor_tensor(u32[:, kk % U32_FREE, :], gated[:, kk % 2, :],
                                       wbc[:, e, blk * BLK:(blk + 1) * BLK], ALU.mult).then_inc(s.scaled, 1)

            def attention(l):
                s = att
                power(norm1[l].var, norm1[l].rstd)
                pool.wait_ge(moe[l].lo, U32_FREE + CH)
                if l:
                    pool.wait_ge(g.back_mm, NBLK)
                v = vaug.rearrange("p r k h s -> p (r k h) s")
                pool.memset(v, 0.0).then_inc(s.vinit, 1)
                pool.memset(oT.rearrange("p a b -> p (a b)"), 1.0).then_inc(s.vinit, 1)
                pool.wait_ge(s.vinit, l * PER["vinit"] + 2)
                pool.memset(v[:, :, HD:HD + 1], 1.0).then_inc(s.vinit, 1)

                for j in range(NBLK):
                    pool.wait_ge(norm1[l].hn, j + 1)
                    zb = z[:, TPB + TB * j:TPB + TB * (j + 1), :]
                    pool.tensor_tensor(zb, zb, mid(row(f"bo{l}"), TB), ALU.add).then_inc(s.zb, 1)

                def values(a, r):
                    for t in range(TPB):
                        cp = pool.tensor_copy(vaug[:, r, t, :, 0:HD], hn[:, bass.ds(TPB * a + t, 1), :].rearrange(
                            "p a (h d) -> p (a h) d", h=H))
                    cp.then_inc(s.vr, 1)

                pool.wait_ge(s.vinit, l * PER["vinit"] + 3)
                pool.wait_ge(s.v, (l + 1) * NBLK)
                values(0, 0)
                values(1, 1)
                with pool.Fori(0, (B - 2) // RING) as i:
                    for k in range(RING):
                        a = RING * i + 2 + k
                        pool.wait_ge(s.av, l * PER["av"] + PROB_FREE + NG * (RING * i + k))
                        values(a, (2 + k) % RING)

            attention(0)
            power(prep[1].var, prep[1].rstd)
            pool.wait_ge(prep[1].hT, NBLK)
            pool.memset(weT8, 0.0).then_inc(prep[1].zero, 1)
            s = moe[1]
            pool.sem_inc(s.sum, PRODUCT_FREE)
            pool.wait_ge(s.init, NBLK)
            with pool.Fori(0, E // 2) as i:
                for kk in range(2 * NBLK):
                    k = 2 * NBLK * i + kk
                    pool.wait_ge(s.scaled, 2 * NBLK + k + 1)
                    pool.wait_ge(s.sum, PRODUCT_FREE + k)
                    acc = y_sum[:, kk % NBLK, :]
                    pool.tensor_tensor(acc, acc, product[:, kk % 2, :], ALU.add).then_inc(s.sum, 1)
            attention(1)
            power(prep[2].var, prep[2].rstd)
            pool.memset(ones8, 1.0).then_inc(q.ones, 1)

        @block.scalar
        def _(act):
            for t in range(NT):
                if t % TB == 0:
                    act.wait_ge(g.h0_ok, t // TB + 1)
                if t:
                    act.wait_ge(g.sq, t)
                act.activation(square, hn[:, t, :], ACT.Square, accum_out=stat[:, t, 0:1]).then_inc(g.sq, 1)

            def to_hT(m, j):
                s = prep[m]
                act.wait_ge(s.tr, j + 1)
                if m == 0:
                    act.activation(hT[:, j * BLK:(j + 1) * BLK], bank[2 + j % 2][:], ACT.Copy,
                                   scale=col("ln_w")).then_inc(s.hT, 1)
                else:
                    act.activation(hT[:, j * BLK:(j + 1) * BLK], bank[2 + j % 2][:], ACT.Identity,
                                   bias=col("ln2_b", m - 1), scale=col("ln2_w", m - 1)).then_inc(s.hT, 1)

            def prepare(m):
                s = prep[m]
                if m == 0:
                    for j in range(NBLK):
                        to_hT(0, j)
                n, c = (P, NT) if m < 2 else (B, 1)
                act.wait_ge(s.diff, 1)
                act.activation(pair[0:n, 1, 0:c], pair[0:n, 0, 0:c], ACT.Exp).then_inc(s.exp, 1)
                if m < 2:
                    act.wait_ge(s.weT_mm, 1)
                    act.activation(weT[:], bank[7][:, 0:P], ACT.Copy).then_inc(s.weT, 1)

            def token_moe_1():
                s = moe[1]
                act.sem_inc(s.act, A_FREE)
                with act.Fori(0, E // 2) as i:
                    for kk in range(2 * EC):
                        k = 2 * EC * i + kk
                        e, c = kk // EC, kk % FC
                        act.wait_ge(s.a, k + 1)
                        act.wait_ge(s.lo, k + 1)
                        act.activation(act_s[:, kk % 4, :], bank[kk % 4][:], ACT.Gelu, bias=bias1[:, e, 0, c:c + 1])
                        act.wait_ge(s.y, NBLK + k + 1)
                        act.activation(u_hi[:, kk % U_FREE, :], bank[kk % 4][:], ACT.Gelu,
                                       bias=bias1[:, e, 0, c:c + 1]).then_inc(s.act, 1)

            def token_moe_0():
                s = moe[0]

                def nonlinear(i, kk):
                    k = 2 * EC * i + kk
                    e, c = kk // EC, kk % FC
                    act.wait_ge(s.a, k + 1)
                    act.wait_ge(s.gate, k + 1)
                    act.activation(act_s[:, kk % 4, :], bank[kk % 2][:], ACT.Silu,
                                   bias=bias1[:, e, 0, c:c + 1]).then_inc(s.act, 1)

                def high(i, kk):
                    k = 2 * EC * i + kk
                    act.wait_ge(s.scaled, 2 * EC + k + 1)
                    act.wait_ge(s.y, k + 1)
                    act.activation(u_hi[:, kk % U_FREE, :], u32[:, kk % U32_FREE, :], ACT.Copy).then_inc(s.hi, 1)

                def body(i, end):
                    for kk in range(2 * EC):
                        if kk + 2 < end:
                            if kk + 2 < 2 * EC:
                                nonlinear(i, kk + 2)
                            else:
                                nonlinear(i + 1, kk + 2 - 2 * EC)
                        high(i, kk)

                nonlinear(0, 0)
                nonlinear(0, 1)
                with act.Fori(0, E // 2 - 1) as i:
                    body(i, 2 * EC + 2)
                body(E // 2 - 1, 2 * EC)

            prepare(0)
            token_moe_0()

            def attention(l):
                s = att

                def normal(j):
                    act.wait_ge(norm1[l].tr, j + 1)
                    act.activation(hT[:, j * BLK:(j + 1) * BLK], bank[6 + j % 2][:], ACT.Identity, bias=col("ln1_b", l),
                                   scale=col("ln1_w", l)).then_inc(norm1[l].hT, 1)

                def part(a, r, n):
                    if n == 0:
                        act.wait_ge(s.qk, l * PER["qk"] + a + 1)
                        if l or not isinstance(a, int):
                            act.wait_ge(s.qk_st, l * PER["qk_st"] + 16 * (a - 1))
                        act.activation(qks[:, r, 0], qk32, ACT.Copy).then_inc(s.p1, 1)
                    else:
                        act.wait_ge(s.r, l * PER["r"] + a + 1)
                        act.activation(qks[:, r, 1], qkr, ACT.Copy).then_inc(s.p2, 1)

                def exps(b, gr):
                    for t in range(3):
                        act.wait_ge(s.t_mm, l * PER["t_mm"] + SUNITS * b + 3 * gr + t + 1)
                        if t == 0:
                            act.wait_ge(s.av, l * PER["av"] + NG * b + gr + 1)
                        act.activation(prob[:, gr % 2, t * BLK:(t + 1) * BLK], bank[4 + t][:], ACT.Exp,
                                       scale=ATT_SCALE).then_inc(s.exp, 1)

                def attended(b, r):
                    act.wait_ge(s.av, l * PER["av"] + PROB_FREE + NG * b + 2 * r + 2)
                    act.wait_ge(s.oTT, l * PER["oTT"] + TPB * (b + 1))
                    act.activation(oT[:, 2 * r:2 * r + 2, :], bank[7][:].rearrange("p (g t) -> p g t", g=2),
                                   ACT.Copy).then_inc(s.oT, 1)

                def normal_T(d1):
                    act.wait_ge(s.on_mm, l * PER["on_mm"] + d1)
                    act.activation(onT, bank[0][:, 0:S], ACT.Copy).then_inc(s.onT, 1)

                def maxima_T(b):
                    act.wait_ge(s.mT_mm, l * PER["mT_mm"] + b + 1)
                    act.wait_ge(s.m_ld, l * PER["m_ld"] + 16 * MROWS * b)
                    act.activation(mT[:], bank[2][0:MROWS * H, 0:P].bitcast(BF16), ACT.Copy).then_inc(s.mT, 1)

                def step(b, k, more_a, more_b):
                    exps(b, 0)
                    if more_a:
                        part(b + 2, (k + 2) % RING, 0)
                        part(b + 2, (k + 2) % RING, 1)
                    exps(b, 1)
                    exps(b, 2)
                    normal_T(b + 1)
                    attended(b, 0)
                    exps(b, 3)
                    if more_b:
                        maxima_T(b + 1)
                    attended(b, 1)

                if l == 0:
                    act.sem_inc(s.exp, T_FREE)
                    act.sem_inc(s.oT, OT_FREE)
                    act.sem_inc(s.onT, BANK_FREE)
                normal(0)
                normal(1)
                for a in range(2):
                    part(a, a, 0)
                    part(a, a, 1)
                    if a == 0:
                        normal(2)
                        normal(3)
                maxima_T(0)
                with act.Fori(0, (B - 2) // RING) as i:
                    for k in range(RING):
                        step(RING * i + k, k, True, True)
                step(B - 2, None, False, True)
                step(B - 1, None, False, False)
                to_hT(l + 1, 0)
                to_hT(l + 1, 1)
                normal_T(B + 1)
                to_hT(l + 1, 2)
                to_hT(l + 1, 3)

            attention(0)
            prepare(1)
            token_moe_1()
            attention(1)
            prepare(2)

            act.sem_inc(q.gel, GEL_FREE)
            act.wait_ge(q.cw_mm, 1)
            act.activation(cw.rearrange("p b k -> p (b k)"), bank[2][:, 0:2 * B], ACT.Copy).then_inc(q.cw, 1)
            act.wait_ge(q.weT_mm, 1)
            act.activation(weT[0:E, 0:B], bank[3][0:E, 0:B], ACT.Copy).then_inc(q.weT, 1)
            act.wait_ge(q.b2_mm, 1)
            act.activation(b2s, bank[3][:, 0:B], ACT.Copy).then_inc(q.b2, 1)
            with act.Fori(0, B // 2) as i:
                for k in range(4):
                    n = 4 * i + k
                    act.wait_ge(q.ug, n + 1)
                    for c in range(FC):
                        if c % 2 == 0:
                            act.wait_ge(q.a, 2 * n + c // 2 + 1)
                        last_ = act.activation(gel[:, k % 2, c, :],
                                               bank[2 * (k % 2) + c // 2][:, (c % 2) * S:(c % 2 + 1) * S], ACT.Gelu,
                                               bias=b1s[:, k, c:c + 1])
                        if c % 2:
                            last_.then_inc(q.gel, 1)

        @block.vector
        def _(dve):
            lines = [0]

            def line(ins):
                lines[0] += 1
                ins.then_inc(g.line, 1)
                dve.wait_ge(g.line, lines[0])

            dve.wait_ge(g.ld_lora, 16 * 4)
            for b in range(B):
                up = dve.tensor_scalar(bsw[:, b, :], BsT_sb, wer[:, b:b + 1], LORA_SCALE, ALU.mult, ALU.mult)
            up.then_inc(g.bsw, 1)
            for j in range(2):
                dve.wait_ge(g.weff_mm, j + 1)
                dve.tensor_tensor(weff[:, 4 * j:4 * j + 4, :], bank[j][:].rearrange("p (b o) -> p b o", b=4),
                                  mid(WbT_sb, 4), ALU.add).then_inc(g.weff_ok, 1)
            dve.wait_ge(g.ld_vec, 32)
            for j in range(NBLK):
                dve.wait_ge(g.h0_mm, j + 1)
                dve.tensor_tensor(hn[:, TB * j:TB * (j + 1), :], bank[2 + j][:].rearrange("p (t o) -> p t o", t=TB),
                                  mid(row("b_base"), TB), ALU.add).then_inc(g.h0_ok, 1)
            def statistics(s, j):
                for t in range(TB * j, TB * (j + 1)):
                    ins = dve.bn_stats(stat[:, t, :], z[:, TPB + t, :])
                line(ins)
                for t in range(TB * j, TB * (j + 1)):
                    ins = dve.bn_aggr(mv[:, t, :], stat[:, t, :])
                line(ins)
                v = slice(TB * j, TB * (j + 1))
                dve.tensor_scalar(var[:, v], mv[:, v, 1], LN_EPS, None, ALU.add).then_inc(s.var, 1)

            def normal(s, j):
                dve.wait_ge(s.rstd, j + 1)
                for t in range(TB * j, TB * (j + 1)):
                    ins = dve.tensor_scalar(hn[:, t, :], z[:, TPB + t, :], mv[:, t, 0:1], rstd[:, t:t + 1],
                                            ALU.subtract, ALU.mult)
                ins.then_inc(s.hn, 1)

            def route(s, n, c, raw, bias):
                lg, tv, ti, tf, pr = logit[0:n, 0:c, :], top_v[0:n, 0:c, :], top_i[0:n, 0:c, :], top_f[0:n, 0:c, :], \
                    pair[0:n, :, 0:c]
                w, o = we[0:n, :, 0:c], onehot[0:n, :, 0:c]
                line(dve.tensor_tensor(lg, raw, mid(bias, c), ALU.add))
                for t in range(c):
                    ins = dve.max(tv[:, t, :], lg[:, t, :])
                line(ins)
                dve.tensor_tensor(pr[:, 0, :], tv[:, :, 1], tv[:, :, 0], ALU.subtract).then_inc(s.diff, 1)
                for t in range(c):
                    ins = dve.max_index(ti[:, t, :], tv[:, t, :], lg[:, t, :])
                line(ins)
                if n == B:
                    dve.sem_inc(q.top, 1)
                line(dve.tensor_copy(tf, ti[:, :, 0:2]))
                dve.wait_ge(s.exp, 1)
                line(dve.tensor_scalar(pr[:, 3, :], pr[:, 1, :], 1.0, None, ALU.add))
                line(dve.reciprocal(pr[:, 2, :], pr[:, 3, :]))
                line(dve.tensor_tensor(pr[:, 3, :], pr[:, 1, :], pr[:, 2, :], ALU.mult))
                experts = last(row("iota", n), c)
                line(dve.tensor_tensor(w, experts, mid(tf[:, :, 0], E), ALU.is_equal))
                line(dve.tensor_tensor(w, w, mid(pr[:, 2, :], E), ALU.mult))
                line(dve.tensor_tensor(o, experts, mid(tf[:, :, 1], E), ALU.is_equal))
                line(dve.tensor_tensor(o, o, mid(pr[:, 3, :], E), ALU.mult))
                dve.tensor_tensor(w, w, o, ALU.add).then_inc(s.we, 1)

            def prepare(m):
                s = prep[m]
                for j in range(NBLK):
                    v = slice(j * BLK, (j + 1) * BLK)
                    dve.wait_ge(s.hT, j + 1)
                    dve.tensor_copy(hT_hi[:, v], hT[:, v]).then_inc(s.hi, 1)
                    dve.wait_ge(s.hi, j + 1)
                    dve.tensor_tensor(hT_lo[:, v], hT[:, v], hT_hi[:, v].bitcast(F32), ALU.subtract
                                      ).then_inc(s.lo, 1)
                dve.wait_ge(s.logits, NBLK)
                route(s, P, NT, bank[6][:, 0:NT * E].rearrange("p (t e) -> p t e", t=NT),
                      row(("bg", "gate_b0")[m]))

            def first_norm(split):
                for j in range(NBLK + 1):
                    if j < NBLK:
                        t = slice(TB * j, TB * (j + 1))
                        dve.wait_ge(g.sq, TB * (j + 1))
                        dve.tensor_scalar(var[:, t], stat[:, t, 0], 1.0 / D, RMS_EPS, ALU.mult, ALU.add
                                          ).then_inc(g.ms, 1)
                    if j < 3:
                        split(0, 0, 2 * j)
                        split(0, 0, 2 * j + 1)
                    if j:
                        v = hn[:, TB * (j - 1):TB * j, :]
                        dve.wait_ge(g.rms, j)
                        dve.tensor_tensor(v, v, last(rstd[:, TB * (j - 1):TB * j], D), ALU.mult).then_inc(prep[0].hn, 1)

            def token_moe(m):
                s = moe[m]
                n_w = 3 if m == 0 else 2
                which = (0, 1, 2) if m == 0 else (0, 2)
                dve.sem_inc(s.split, 12)
                dve.sem_inc(s.lo, U32_FREE)
                if m == 1:
                    dve.sem_inc(s.scaled, 2 * NBLK)
                else:
                    dve.sem_inc(s.gate, ACT_FREE)

                def split(i, e, n):
                    w, low = which[min(n // 2, n_w - 1)], n % 2
                    exp = 2 * i + e
                    if n == 0:
                        dve.wait_ge(w_ld[e], 16 * (m * 3 * E // 2 + n_w * (i + 1)))
                        if not isinstance(exp, int) or exp > 0:
                            dve.wait_ge(s.y, EC * (exp - 1) + U_FREE + m * NBLK)
                        for j, name in enumerate(("b1a", "b1b") if m == 0 else ("e_b1",)):
                            dve.tensor_copy(bias1[:, e, j, :], cols[:, bass.ds(COL[name][0] + FC * exp, FC)])
                    if n // 2 >= n_w:
                        dve.sem_inc(s.split, 1)
                    elif not low:
                        dve.tensor_copy(whi[:, e, w, :], wraw[:, e, w, :]).then_inc(s.split, 1)
                    else:
                        dve.wait_ge(s.split, 12 + 6 * exp + n)
                        dve.tensor_tensor(wlo[:, e, w, :], wraw[:, e, w, :], whi[:, e, w, :].bitcast(F32),
                                          ALU.subtract).then_inc(s.split, 1)

                def gate(i, kk):
                    k = 2 * EC * i + kk
                    e, c = kk // EC, kk % FC
                    dve.wait_ge(s.b, k + 1)
                    dve.wait_ge(s.act, k + 1)
                    dve.wait_ge(s.scaled, 2 * EC + k - 1)
                    dve.scalar_tensor_tensor(out=gated[:, kk % 2, :], in0=bank[2 + kk % 2][:],
                                             scalar=bias1[:, e, 1, c:c + 1], in1=act_s[:, kk % 4, :],
                                             op0=ALU.add, op1=ALU.mult).then_inc(s.gate, 1)

                def combine(i, kk):
                    e, blk = kk // EC, kk % EC // FC
                    k = 2 * NBLK * i + kk // FC
                    if blk == 0:
                        dve.wait_ge(r_ld[e], 16 * (E // 2 + i + 1))
                    dve.wait_ge(s.y, U_FREE + NBLK + FC * (k + 1))
                    dve.wait_ge(s.sum, k + 1)
                    dve.tensor_tensor(product[:, kk // FC % 2, :], bank[4 + blk][:],
                                      wbc[:, e, blk * BLK:(blk + 1) * BLK], ALU.mult).then_inc(s.scaled, 1)

                def low(i, kk):
                    k = 2 * EC * i + kk
                    dve.wait_ge(s.hi, k + 1) if m == 0 else dve.wait_ge(s.act, A_FREE + k + 1)
                    full = u32 if m == 0 else act_s
                    dve.tensor_tensor(u_lo[:, kk % U_FREE, :], full[:, kk % U32_FREE, :],
                                      u_hi[:, kk % U_FREE, :].bitcast(F32), ALU.subtract).then_inc(s.lo, 1)

                def mix(i, n):
                    b, gg = 2 * i + n // E, n % E
                    a0 = ROW["cond"][0]
                    acc = weff[:, bass.ds(b, 1), :].rearrange("p a o -> p (a o)")
                    c = rows[:, bass.ds(a0 + E * b + gg, 1)]
                    if gg == 0:
                        dve.tensor_scalar(acc, wt[:, gg, :], c, None, ALU.mult).then_inc(g.mix, 1)
                    else:
                        dve.wait_ge(g.mix, 2 * E * i + n)
                        dve.scalar_tensor_tensor(out=acc, in0=wt[:, gg, :], scalar=c, in1=acc, op0=ALU.mult,
                                                 op1=ALU.add).then_inc(g.mix, 1)

                lead = 2 if m == 0 else 3
                ahead = gate if m == 0 else low

                def body(i, last_pair):
                    for kk in range(2 * EC):
                        nk = kk + lead
                        if nk < 2 * EC:
                            ahead(i, nk)
                        elif not last_pair:
                            ahead(i + 1, nk - 2 * EC)
                        if m == 0:
                            low(i, kk)
                        elif kk % FC == FC - 1:
                            combine(i, kk)
                        if 4 <= kk % EC < 10:
                            if kk < EC:
                                split(i, 1, kk % EC - 4)
                            elif not last_pair:
                                split(i + 1, 0, kk % EC - 4)
                        if m == 0 and kk % 2:
                            mix(i, kk // 2)

                if m == 0:
                    first_norm(split)
                    prepare(0)
                    dve.wait_ge(g.mixmask, 1)
                else:
                    for n in range(6):
                        split(0, 0, n)
                    for j in range(NBLK):
                        dve.wait_ge(s.y, U_FREE + j + 1)
                        dve.tensor_copy(y_sum[:, j, :], bank[4 + j][:]).then_inc(s.init, 1)
                for kk in range(lead):
                    ahead(0, kk)
                with dve.Fori(0, E // 2 - 1) as i:
                    body(i, False)
                body(E // 2 - 1, True)

            token_moe(0)
            dve.wait_ge(moe[0].y, U_FREE + CH)
            for j in range(NBLK):
                v = xTs[:, j * BLK:(j + 1) * BLK]
                dve.tensor_tensor(v, v, bank[4 + j][:], ALU.add).then_inc(g.x1, 1)
            for j in range(NBLK):
                dve.wait_ge(g.z_mm, j + 1)
                dve.tensor_tensor(z[:, TPB + TB * j:TPB + TB * (j + 1), :],
                                  bank[j][:].rearrange("p (t o) -> p t o", t=TB), mid(row("bias"), TB), ALU.add
                                  ).then_inc(g.z_ok, 1)
            dve.wait_ge(g.z_ok, NBLK)

            def attention(l):
                s = att
                if l == 0:
                    dve.sem_inc(s.red, S_FREE)
                    dve.sem_inc(s.z, BANK_FREE)

                def value(j):
                    dve.wait_ge(s.v_mm, l * PER["v_mm"] + j + 1)
                    dve.tensor_tensor(hn[:, TB * j:TB * (j + 1), :], bank[2 + j][:].rearrange("p (t d) -> p t d", t=TB),
                                      mid(row(f"bv{l}"), TB), ALU.add).then_inc(s.v, 1)

                def project(a):
                    dve.wait_ge(s.qk_mm, l * PER["qk_mm"] + a + 1)
                    dve.tensor_scalar(qk32[:, 0, :], bank[0][:, 0:S], col("bq", l), None, ALU.add)
                    dve.tensor_scalar(qk32[:, 1, :], bank[0][:, S:2 * S], col("bk", l), None, ALU.add
                                      ).then_inc(s.qk, 1)

                def rest(a, r):
                    dve.wait_ge(s.p1, l * PER["p1"] + a + 1)
                    dve.tensor_tensor(qkr, qk32, qks[:, r, 0], ALU.subtract).then_inc(s.r, 1)

                def rest2(a, r):
                    dve.wait_ge(s.p2, l * PER["p2"] + a + 1)
                    dve.tensor_tensor(qks[:, r, 2], qkr, qks[:, r, 1], ALU.subtract).then_inc(s.p3, 1)

                def reduce(b, u):
                    dve.wait_ge(s.s_mm, l * PER["s_mm"] + SUNITS * b + u + 1)
                    n = 4 if u < 4 else 2
                    h = 4 * u if u < 4 else 2 * (u - 4)
                    dve.tensor_reduce(mmax[:, int(u >= 4), h:h + n], bank[2 + u % 2][:].rearrange(
                        "p (h k) -> p h k", h=n), AX.X, ALU.max).then_inc(s.red, 1)

                def minus_max(b):
                    dve.wait_ge(s.red, l * PER["red"] + S_FREE + SUNITS * (b + 1))
                    dve.wait_ge(s.mT_mm, l * PER["mT_mm"] + b)
                    dve.tensor_scalar(msp[:, :, 0, :], mmax, -1.0, None, ALU.mult).then_inc(s.mhi, 1)
                    dve.wait_ge(s.mhi, l * PER["mhi"] + b + 1)
                    dve.scalar_tensor_tensor(out=msp[:, :, 1, :], in0=mmax, scalar=-1.0, in1=msp[:, :, 0, :],
                                             op0=ALU.mult, op1=ALU.subtract).then_inc(s.msp, 1)

                def normalize(d1):
                    for t in range(TPB):
                        dve.wait_ge(s.oTT, l * PER["oTT"] + TPB * (d1 - 1) + t + 1)
                        v = bank[t][:].rearrange("p (h s) -> p h s", h=H)
                        dve.reciprocal(orec[:, t, :], v[:, :, HD]).then_inc(s.rec, 1)
                    for t in range(TPB):
                        v = bank[t][:].rearrange("p (h s) -> p h s", h=H)
                        dve.wait_ge(s.rec, l * PER["rec"] + TPB * (d1 - 1) + t + 1)
                        dve.tensor_tensor(onorm[:, t, :].rearrange("p (h d) -> p h d", h=H), v[:, :, 0:HD],
                                          last(orec[:, t, :], HD), ALU.mult).then_inc(s.on, 1)

                def residual(d1):
                    dve.wait_ge(s.wo_mm, l * PER["wo_mm"] + d1)
                    zb = z[:, bass.ds(TPB * (d1 - 1), TPB), :]
                    dve.tensor_tensor(zb, zb, bank[1][:, 0:S].rearrange("p (t d) -> p t d", t=TPB), ALU.add
                                      ).then_inc(s.z, 1)

                def step(b, k, more_a, more_b):
                    if more_b:
                        reduce(b + 1, 0)
                        reduce(b + 1, 1)
                    if more_a:
                        project(b + 2)
                    if more_b:
                        reduce(b + 1, 2)
                    if more_a:
                        rest(b + 2, (k + 2) % RING)
                    if more_b:
                        reduce(b + 1, 3)
                    if more_a:
                        rest2(b + 2, (k + 2) % RING)
                    if more_b:
                        reduce(b + 1, 4)
                        reduce(b + 1, 5)
                    normalize(b + 1)
                    if more_b:
                        for u in range(6, 10):
                            reduce(b + 1, u)
                    residual(b + 1)
                    if more_b:
                        reduce(b + 1, 10)
                        reduce(b + 1, 11)
                        minus_max(b + 1)

                n1 = norm1[l]
                statistics(n1, 0)
                statistics(n1, 1)
                normal(n1, 0)
                statistics(n1, 2)
                normal(n1, 1)
                project(0)
                statistics(n1, 3)
                rest(0, 0)
                normal(n1, 2)
                rest2(0, 0)
                normal(n1, 3)
                value(0)
                project(1)
                value(1)
                rest(1, 1)
                value(2)
                rest2(1, 1)
                value(3)
                for u in range(SUNITS):
                    reduce(0, u)
                minus_max(0)
                dve.wait_ge(s.zb, (l + 1) * NBLK)
                with dve.Fori(0, (B - 2) // RING) as i:
                    for k in range(RING):
                        step(RING * i + k, k, True, True)
                n2 = prep[l + 1]
                step(B - 2, (B - 2) % RING, False, True)
                dve.wait_ge(s.z, l * PER["z"] + BANK_FREE + B - 1)
                statistics(n2, 0)
                statistics(n2, 1)
                step(B - 1, (B - 1) % RING, False, False)
                dve.wait_ge(s.vr, (l + 1) * PER["vr"])
                normal(n2, 0)
                statistics(n2, 2)
                normal(n2, 1)
                normalize(B + 1)
                normal(n2, 2)
                residual(B + 1)
                dve.wait_ge(s.z, l * PER["z"] + BANK_FREE + B + 1)
                statistics(n2, 3)
                normal(n2, 3)

            attention(0)
            prepare(1)
            token_moe(1)
            for j in range(NBLK):
                dve.wait_ge(g.back_mm, j + 1)
                v = z[:, TPB + TB * j:TPB + TB * (j + 1), :]
                dve.tensor_tensor(v, v, bank[j][:].rearrange("p (t o) -> p t o", t=TB), ALU.add).then_inc(g.back, 1)
            dve.wait_ge(g.back, NBLK)
            attention(1)

            s = prep[2]
            for j in range(NBLK):
                dve.wait_ge(s.hT, j + 1)
                b = slice(j * BLK // S, (j + 1) * BLK // S)
                ins = dve.tensor_reduce(hmean[:, b], hT[:, j * BLK:(j + 1) * BLK].rearrange("p (b t) -> p b t", t=S),
                                        AX.X, ALU.add)
            line(ins)
            dve.tensor_scalar(hmean, hmean, 1.0 / S, None, ALU.mult).then_inc(q.mean, 1)
            dve.wait_ge(s.logits, 1)
            route(s, B, 1, bank[2][0:B, 0:E].rearrange("p (t e) -> p t e", t=1), row("gate_b1", B))
            dve.tensor_tensor(diag[0:B], last(ident[0:B, 0:B], 2),
                              pair[0:B, 2:4, 0].rearrange("p (a k) -> p a k", a=1).to_broadcast([B, B, 2]), ALU.mult
                              ).then_inc(q.cw_in, 1)
            dve.sem_inc(q.ug, 2)
            dve.wait_ge(q.cw, 1)

            def scale6(i, k):
                n = 4 * i + k
                b = 2 * i + k // 2
                dve.wait_ge(q.gel, GEL_FREE + 2 * n + 2)
                dve.wait_ge(q.y, n + 3)
                dve.tensor_scalar(ug[:, k % 2], gel[:, k % 2], cw[:, bass.ds(b, 1), k % 2], None, ALU.mult
                                  ).then_inc(q.ug, 1)

            dve.wait_ge(q.b2, 1)
            with dve.Fori(0, B // 2) as i:
                for k in range(4):
                    scale6(i, k)
                    if k % 2:
                        b = 2 * i + k // 2
                        dve.wait_ge(q.y, 4 + 2 * b + 2)
                        dve.scalar_tensor_tensor(out=yx[:, k // 2, :], in0=bank[4 + k // 2][:, 0:S],
                                                 scalar=b2s[:, bass.ds(b, 1)], in1=xTs[:, bass.ds(S * b, S)],
                                                 op0=ALU.add, op1=ALU.add).then_inc(q.yx, 1)
                        dve.wait_ge(q.t, b + 1)
                        dve.tensor_tensor(oseq_at(b), z[:, bass.ds(TPB * (b + 1), TPB), :],
                                          bank[6 + k // 2][:, 0:S].rearrange("p (t d) -> p t d", t=TPB), ALU.add
                                          ).then_inc(q.o, 1)

        @block.tensor
        def _(pe):
            pe.wait_ge(g.bsw, 1)
            pe.wait_ge(g.ld_lora, 16 * 4)
            for j in range(2):
                pe.matmul(bank[j][:], As_sb, bsw[:, 4 * j:4 * j + 4, :].rearrange("p b o -> p (b o)"), start=True,
                          stop=True).then_inc(g.weff_mm, 1)
            pe.wait_ge(g.ld_x, 16)
            for t in range(NT):
                b = t // TPB
                if b % 4 == 0:
                    pe.wait_ge(g.weff_ok, b // 4 + 1)
                mm = pe.matmul(bank[2 + t // TB][:, (t % TB) * P:(t % TB + 1) * P], xTs[:, t * P:(t + 1) * P],
                               weff[:, b, :], start=True, stop=True)
                if t % TB == TB - 1:
                    mm.then_inc(g.h0_mm, 1)
            pe.wait_ge(g.ident, 3)
            pe.wait_ge(g.ld_rest, 16 * 4)

            def transpose(s, j, first_bank=2):
                pe.wait_ge(s.hn, j + 1)
                if j >= 2:
                    pe.wait_ge(s.hT, j - 1)
                for t in range(TB):
                    mm = pe.transpose(bank[first_bank + j % 2][:, t * P:(t + 1) * P], hn[:, TB * j + t, :], ident[:])
                mm.then_inc(s.tr, 1)

            def logits(m, j):
                s = prep[m]
                pe.wait_ge(s.hT, j + 1)
                for t in range(TB * j, TB * (j + 1)):
                    mm = pe.matmul(bank[6][:, t * E:(t + 1) * E], hT[:, t * P:(t + 1) * P], gate_sb[:, m, :],
                                   start=True, stop=True)
                mm.then_inc(s.logits, 1)

            def prepare(m, meanwhile=None):
                s = prep[m]
                if m == 0:
                    transpose(s, 0)
                    transpose(s, 1)
                    logits(m, 0)
                    transpose(s, 2)
                    logits(m, 1)
                    transpose(s, 3)
                else:
                    logits(m, 0)
                    logits(m, 1)
                logits(m, 2)
                logits(m, 3)
                if meanwhile:
                    meanwhile()
                pe.wait_ge(s.we, 1)
                pe.transpose(bank[7][:, 0:P], we[:].rearrange("p e t -> p (e t)"), ident[:]).then_inc(s.weT_mm, 1)

            def token_moe(m):
                s = moe[m]
                n_a = 2 if m == 0 else 4
                pe.sem_inc(s.y, U_FREE)
                def three(dst, w, x, sl, start, done=None):
                    pe.matmul(dst, w[0], x[0], start=start, stop=False, skip_group_check=True)
                    pe.matmul(dst, w[0], x[1], start=False, stop=False, skip_group_check=True)
                    pe.matmul(dst, w[1], x[0], start=False, stop=True, skip_group_check=True).then_inc(done, 1)

                def first(i, kk):
                    k = 2 * EC * i + kk
                    e, blk, c = kk // EC, kk % EC // FC, kk % FC
                    if kk % EC == 0:
                        pe.wait_ge(s.split, 12 + 6 * (2 * i + e + 1))
                    tok, f = slice(blk * BLK, (blk + 1) * BLK), slice(c * P, (c + 1) * P)
                    x = hT_hi[:, tok], hT_lo[:, tok]
                    if m == 1:
                        pe.wait_ge(s.act, k + 1)
                    elif not isinstance(k, int) or k >= n_a:
                        pe.wait_ge(s.act, k - n_a + 1)
                    three(bank[kk % n_a][:], (whi[:, e, 0, f], wlo[:, e, 0, f]), x, None, True, s.a)
                    if m == 0:
                        pe.wait_ge(s.gate, ACT_FREE + k - 1)
                        three(bank[2 + kk % 2][:], (whi[:, e, 1, f], wlo[:, e, 1, f]), x, None, True, s.b)

                def second(i, kk):
                    k = 2 * EC * i + kk
                    e, blk, c = kk // EC, kk % EC // FC, kk % FC
                    d = slice(c * D, (c + 1) * D)
                    if m == 1 and c == 0:
                        pe.wait_ge(s.scaled, NBLK + 2 * NBLK * i + kk // FC + 1)
                    pe.wait_ge(s.lo, U32_FREE + k + 1)
                    three(bank[4 + blk][:], (whi[:, e, 2, d], wlo[:, e, 2, d]),
                          (u_hi[:, kk % U_FREE, :], u_lo[:, kk % U_FREE, :]), None, m == 1 and c == 0, s.y)

                lead = 3

                def begin():
                    pe.wait_ge(prep[m].lo, NBLK)
                    first(0, 0)
                    first(0, 1)

                def body(i, last_pair):
                    for kk in range(2 * EC):
                        nk = kk + lead
                        if nk < 2 * EC:
                            first(i, nk)
                        elif not last_pair:
                            first(i + 1, nk - 2 * EC)
                        second(i, kk)

                if m == 0:
                    prepare(0, begin)
                else:
                    prepare(1)
                    begin()
                first(0, 2)
                pe.wait_ge(prep[m].load, 16)
                pe.wait_ge(g.ld_b2, 16)
                for j in range(NBLK):
                    mm = pe.matmul(bank[4 + j][:], b2_sb[:, m, :], weT8[:, j * BLK:(j + 1) * BLK], start=True,
                                   stop=(m == 1), skip_group_check=True)
                    if m == 1:
                        mm.then_inc(s.y, 1)
                if m == 1:
                    pe.wait_ge(s.init, NBLK)
                with pe.Fori(0, E // 2 - 1) as i:
                    body(i, False)
                body(E // 2 - 1, True)

            token_moe(0)
            for t in range(NT):
                if t % TB == 0:
                    pe.wait_ge(g.x1, t // TB + 1)
                if t == 0:
                    pe.wait_ge(g.mix, B * E)
                mm = pe.matmul(bank[t // TB][:, (t % TB) * P:(t % TB + 1) * P], xTs[:, t * P:(t + 1) * P],
                               weff[:, t // TPB, :], start=True, stop=True)
                if t % TB == TB - 1:
                    mm.then_inc(g.z_mm, 1)

            def attention(l):
                s = att
                pe.wait_ge(g.masks, 5)
                pe.wait_ge(g.pad, 3)
                if l == 0:
                    pe.sem_inc(s.av, PROB_FREE)

                def project(a):
                    tok = hT[:, bass.ds(S * a, S)]
                    pe.matmul(bank[0][:, 0:S], att_w[:, l, 0, :], tok, start=True, stop=True)
                    pe.matmul(bank[0][:, S:2 * S], att_w[:, l, 1, :], tok, start=True, stop=True).then_inc(s.qk_mm, 1)

                def scores(b, r, u):
                    pe.wait_ge(s.red, l * PER["red"] + SUNITS * b + u + 1)
                    if u == 0:
                        pe.wait_ge(s.qk_ld, l * PER["qk_ld"] + 16 * QK_LOADS * (b + 1))
                        pe.wait_ge(s.mT, l * PER["mT"] + b)
                    t = int(u >= 4)
                    n = 4 if u < 4 else 2
                    h0 = 4 * u if u < 4 else 2 * (u - 4)
                    keys = BLK // n
                    dst = bank[2 + u % 2]
                    for j in range(n):
                        h = (h0 + j) * S
                        pe.matmul(dst[:, j * keys:(j + 1) * keys], qp[:, r, h + t * P:h + (t + 1) * P],
                                  kp[:, r, h:h + keys], start=(j == 0), stop=False, skip_group_check=True)
                    pe.matmul(dst[:].rearrange("p (h k) -> p h k", h=n)[:, :, keys - P:keys], ident_bf[:],
                              mid(mask_q[:], n), start=False, stop=True, skip_group_check=True).then_inc(s.s_mm, 1)

                def scores_T(b, r, gr):
                    if gr == 0:
                        pe.wait_ge(s.m_ld, l * PER["m_ld"] + 16 * MROWS * (b + 1))
                    for t in range(3):
                        pe.wait_ge(s.exp, l * PER["exp"] + SUNITS * b + 3 * gr + t + 1)
                        n = 2 if t < 2 else 4
                        kt = int(t == 2)
                        keys, width = slice(kt * P, (kt + 1) * P), BLK // n
                        dst = bank[4 + t]
                        for j in range(n):
                            h = (HG * gr + (2 * t + j if t < 2 else j)) * S
                            pe.matmul(dst[:, j * width:(j + 1) * width], kp[:, r, h + kt * P:h + (kt + 1) * P],
                                      qp[:, r, h + kt * P:h + S], start=(j == 0), stop=False, skip_group_check=True)
                        pe.matmul(dst[:].rearrange("p (h k) -> p h k", h=n)[:, :, 0:P], ident_bf[:], mid(mask_k[:], n),
                                  start=False, stop=True, skip_group_check=True).then_inc(s.t_mm, 1)

                def attend(b, r, gr):
                    pe.wait_ge(s.exp, l * PER["exp"] + T_FREE + SUNITS * b + 3 * gr + 3)
                    pe.wait_ge(s.vr, l * PER["vr"] + b + 1)
                    if gr % 2 == 0:
                        pe.wait_ge(s.oT, l * PER["oT"] + OT_FREE + 2 * b + gr // 2)
                    for j in range(HG):
                        pe.matmul(bank[7][SLOT * j:SLOT * (j + 1), (gr % 2) * S:(gr % 2 + 1) * S],
                                  vaug[:, r, 0, HG * gr + j, :], prob[:, gr % 2, j * S:(j + 1) * S], start=True,
                                  stop=False, skip_group_check=True)
                    for j in range(HG):
                        mm = pe.matmul(bank[7][SLOT * j:SLOT * (j + 1), (gr % 2) * S + P:(gr % 2 + 1) * S],
                                       vaug[:, r, 1, HG * gr + j, :],
                                       prob[:, gr % 2, 2 * BLK + j * P:2 * BLK + (j + 1) * P], start=False, stop=True,
                                       skip_group_check=True)
                    mm.then_inc(s.av, 1)

                def attended_T(d1, n_a):
                    pe.wait_ge(s.oT, l * PER["oT"] + OT_FREE + 2 * (d1 - 1))
                    pe.wait_ge(s.onT, l * PER["onT"] + BANK_FREE + d1 - 1)
                    pe.wait_ge(s.z, l * PER["z"] + BANK_FREE + d1 - 1)
                    pe.wait_ge(s.qk, l * PER["qk"] + n_a)
                    for t in range(TPB):
                        for gr in range(NG):
                            mm = pe.transpose(bank[t][:, gr * P:(gr + 1) * P], oT[:, gr, t * P:(t + 1) * P], ident[:])
                        mm.then_inc(s.oTT, 1)

                def normal_T(d1):
                    pe.wait_ge(s.on, l * PER["on"] + TPB * d1)
                    for t in range(TPB):
                        mm = pe.transpose(bank[0][:, t * P:(t + 1) * P], onorm[:, t, :], ident[:])
                    mm.then_inc(s.on_mm, 1)

                def output(d1):
                    pe.wait_ge(s.onT, l * PER["onT"] + BANK_FREE + d1)
                    for t in range(TPB):
                        mm = pe.matmul(bank[1][:, t * P:(t + 1) * P], onT[:, t * P:(t + 1) * P], att_w[:, l, 3, :],
                                       start=True, stop=True)
                    mm.then_inc(s.wo_mm, 1)

                def maxima_T(b):
                    pe.wait_ge(s.msp, l * PER["msp"] + b + 1)
                    for t in range(TPB):
                        mm = pe.transpose(bank[2][0:MROWS * H, 0:P].bitcast(BF16)[:, t * P:(t + 1) * P],
                                          msp[:, t].rearrange("p r h -> p (r h)"), ident_bf[:])
                    mm.then_inc(s.mT_mm, 1)

                def step(b, k, more_a, more_b):
                    r, r1 = k % RING, (k + 1) % RING

                    def maxima_scores(*units):
                        if more_b:
                            for u in units:
                                scores(b + 1, r1, u)

                    maxima_scores(0, 1)
                    if more_a:
                        pe.wait_ge(s.onT, l * PER["onT"] + BANK_FREE + b)
                        project(b + 2)
                    scores_T(b, r, 0)
                    maxima_scores(2, 3)
                    scores_T(b, r, 1)
                    maxima_scores(4)
                    attended_T(b + 1, b + 3 if more_a else B)
                    maxima_scores(5)
                    attend(b, r, 0)
                    maxima_scores(6)
                    scores_T(b, r, 2)
                    maxima_scores(7)
                    normal_T(b + 1)
                    maxima_scores(8)
                    attend(b, r, 1)
                    maxima_scores(9)
                    output(b + 1)
                    maxima_scores(10, 11)
                    scores_T(b, r, 3)
                    attend(b, r, 2)
                    if more_b:
                        maxima_T(b + 1)
                    attend(b, r, 3)

                def value(j):
                    pe.wait_ge(norm1[l].hT, j + 1)
                    for t in range(TB):
                        mm = pe.matmul(bank[2 + j][:, t * P:(t + 1) * P], hT[:, (TB * j + t) * P:(TB * j + t + 1) * P],
                                       att_w[:, l, 2, :], start=True, stop=True)
                    mm.then_inc(s.v_mm, 1)

                transpose(norm1[l], 0, 6)
                transpose(norm1[l], 1, 6)
                pe.wait_ge(norm1[l].hT, 1)
                project(0)
                transpose(norm1[l], 2, 6)
                transpose(norm1[l], 3, 6)
                value(0)
                pe.wait_ge(s.qk, l * PER["qk"] + 1)
                project(1)
                value(1)
                value(2)
                value(3)
                pe.wait_ge(s.v, (l + 1) * NBLK)
                pe.wait_ge(s.vinit, l * PER["vinit"] + 3)
                for u in range(SUNITS):
                    scores(0, 0, u)
                maxima_T(0)
                with pe.Fori(0, (B - 2) // RING) as i:
                    for k in range(RING):
                        step(RING * i + k, k, True, True)
                step(B - 2, (B - 2) % RING, False, True)
                step(B - 1, (B - 1) % RING, False, False)
                after = prep[l + 1]
                transpose(after, 0)
                transpose(after, 1)
                attended_T(B + 1, B)
                transpose(after, 2)
                normal_T(B + 1)
                output(B + 1)
                transpose(after, 3)

            attention(0)
            token_moe(1)
            for t in range(NT):
                if t % TB == 0:
                    pe.wait_ge(moe[1].sum, PRODUCT_FREE + (E - 1) * NBLK + t // TB + 1)
                mm = pe.transpose(bank[t // TB][:, (t % TB) * P:(t % TB + 1) * P],
                                  y_sum[:, t // TB, (t % TB) * P:(t % TB + 1) * P], ident[:])
                if t % TB == TB - 1:
                    mm.then_inc(g.back_mm, 1)
            pe.wait_ge(g.back, NBLK)
            attention(1)

            s = prep[2]
            pe.wait_ge(q.mean, 1)
            pe.matmul(bank[2][0:B, 0:E], hmean, gate_sb[:, 2, :], start=True, stop=True).then_inc(s.logits, 1)
            pe.wait_ge(q.ones, 1)
            pe.wait_ge(q.cw_in, 1)
            pe.matmul(bank[2][:, 0:2 * B], ones8[0:B, :], diag[0:B].rearrange("p b k -> p (b k)"), start=True,
                      stop=True).then_inc(q.cw_mm, 1)
            pe.transpose(bank[3][0:E, 0:B], we[0:B, :, 0], ident[0:B, 0:B]).then_inc(q.weT_mm, 1)
            pe.wait_ge(q.weT, 1)
            pe.matmul(bank[3][:, 0:B], b2_sb[0:E, 2, :], weT[0:E, 0:B], start=True, stop=True).then_inc(q.b2_mm, 1)
            pe.wait_ge(q.b2, 1)
            pe.sem_inc(q.y, 4)

            def first6(i, k):
                n = 4 * i + k
                pe.wait_ge(q_w[k], 48 * (i + 1))
                pe.wait_ge(q.gel, GEL_FREE + 2 * n - 2)
                tok = hT[:, bass.ds(S * (2 * i + k // 2), S)]
                for c in range(FC):
                    mm = pe.matmul(bank[2 * (k % 2) + c // 2][:, (c % 2) * S:(c % 2 + 1) * S],
                                   w1s[:, k, c * P:(c + 1) * P], tok, start=True, stop=True)
                    if c % 2:
                        mm.then_inc(q.a, 1)

            def second6(i, k):
                n = 4 * i + k
                pe.wait_ge(q.ug, n + 3)
                for c in range(FC):
                    mm = pe.matmul(bank[4 + k // 2][:, 0:S], w2s[:, k, c, :], ug[:, k % 2, c, :],
                                   start=(k % 2 == 0 and c == 0), stop=(k % 2 == 1 and c == FC - 1))
                mm.then_inc(q.y, 1)

            def body6(i, last_two):
                for k in range(4):
                    if k < 3:
                        first6(i, k + 1)
                    elif not last_two:
                        first6(i + 1, 0)
                    second6(i, k)
                    if k % 2:
                        pe.wait_ge(q.yx, 2 * i + k // 2 + 1)
                        for t in range(TPB):
                            mm = pe.transpose(bank[6 + k // 2][:, t * P:(t + 1) * P], yx[:, k // 2, t * P:(t + 1) * P],
                                              ident[:])
                        mm.then_inc(q.t, 1)

            first6(0, 0)
            with pe.Fori(0, B // 2 - 1) as i:
                body6(i, False)
            body6(B // 2 - 1, True)


def kernel(x, cond_8, L0_cond_W_base, L0_cond_b_base, L0_cond_As, L0_cond_Bs, L0_ffn_ln_w, L0_ffn_Wg, L0_ffn_bg,
           L0_ffn_W1a, L0_ffn_b1a, L0_ffn_W1b, L0_ffn_b1b, L0_ffn_W2, L0_ffn_b2, L1_cond_weight, L1_cond_mask,
           L1_cond_bias, L1_ffn_ln1_w, L1_ffn_ln1_b, L1_ffn_ln2_w, L1_ffn_ln2_b, L1_ffn_wq, L1_ffn_wk, L1_ffn_wv,
           L1_ffn_wo, L1_ffn_bq, L1_ffn_bk, L1_ffn_bv, L1_ffn_bo, L1_ffn_gate_w, L1_ffn_gate_b, L1_ffn_e_w1,
           L1_ffn_e_b1, L1_ffn_e_w2, L1_ffn_e_b2):
    import numpy as _np
    import concourse.bacc as _bacc
    from concourse import mybir as _mybir
    from concourse.bass_utils import run_bass_kernel_spmd as _run

    def npa(a):
        return _np.asarray(a)

    def dim_major(w):
        w = npa(w)
        return w.reshape(w.shape[:-1] + (H, HD)).swapaxes(-1, -2).reshape(w.shape)

    def chunks(b):
        return npa(b).reshape(-1, P).T

    cols = _np.concatenate([npa(L0_ffn_ln_w).reshape(D, 1), npa(L1_ffn_ln1_w).T, npa(L1_ffn_ln1_b).T,
                            npa(L1_ffn_ln2_w).T, npa(L1_ffn_ln2_b).T, dim_major(L1_ffn_bq).T, dim_major(L1_ffn_bk).T,
                            chunks(L0_ffn_b1a), chunks(L0_ffn_b1b), chunks(npa(L1_ffn_e_b1)[0])], axis=1)
    rows = _np.concatenate([npa(v).reshape(-1) for v in (
        L0_cond_b_base, L1_cond_bias, L0_ffn_bg, L1_ffn_gate_b, L1_ffn_bv, L1_ffn_bo, cond_8,
        _np.arange(E, dtype=_np.float32))]).reshape(1, -1)
    arrays = {
        "xT": npa(x).reshape(N, D).T,
        "As": npa(L0_cond_As).reshape(P, D),
        "BsT": npa(L0_cond_Bs).transpose(0, 2, 1).reshape(P, D),
        "WbT": npa(L0_cond_W_base).T,
        "w_er": _np.repeat(npa(cond_8).T, P // E, axis=0),
        "cols": cols,
        "rows": rows,
        "Wg": _np.stack([npa(L0_ffn_Wg), npa(L1_ffn_gate_w)[0], npa(L1_ffn_gate_w)[1]], axis=1),
        "W1a": npa(L0_ffn_W1a), "W1b": npa(L0_ffn_W1b), "W2": npa(L0_ffn_W2),
        "b2": _np.stack([npa(L0_ffn_b2), npa(L1_ffn_e_b2)[0], npa(L1_ffn_e_b2)[1]], axis=1),
        "WT": npa(L1_cond_weight).transpose(2, 0, 1),
        "maskT": npa(L1_cond_mask).T,
        "att_w": _np.stack([dim_major(L1_ffn_wq), dim_major(L1_ffn_wk), npa(L1_ffn_wv), npa(L1_ffn_wo)],
                           axis=1).transpose(2, 0, 1, 3),
        "e_w1": npa(L1_ffn_e_w1), "e_w2": npa(L1_ffn_e_w2),
        "e_b1s": npa(L1_ffn_e_b1)[1].reshape(E, FC, P).transpose(0, 2, 1),
    }
    nc = _bacc.Bacc("TRN2", target_bir_lowering=False, num_devices=1)
    feeds, args = {}, []
    for name, a in arrays.items():
        a = _np.ascontiguousarray(a)
        feeds[f"in_{name}"] = a
        args.append(nc.dram_tensor(f"in_{name}", a.shape, _mybir.dt.from_np(a.dtype), kind="ExternalInput").ap())
    args.append(nc.dram_tensor("out_0", (B, S, D), F32, kind="ExternalOutput").ap())
    build(nc, *args)
    r = _run(nc, [feeds], core_ids=[0])
    return r.results[0]["out_0"]
```
